# Optimizing a Trainium2 kernel written in Bass

```python
import numpy as np
import jax
import jax.numpy as jnp

def _softmax(x, axis=-1):
    return jax.nn.softmax(x, axis=axis)

def _gelu(x):
    return jax.nn.gelu(x, approximate=True)

def _silu(x):
    return jax.nn.silu(x)

def _sigmoid(x):
    return jax.nn.sigmoid(x)

def _layernorm(x, axis=-1, eps=1e-05):
    m = jnp.mean(x, axis=axis, keepdims=True)
    v = jnp.var(x, axis=axis, keepdims=True)
    return (x - m) / jnp.sqrt(v + eps)

def _scatter_add(tgt, idx, src, axis=0):
    return tgt.at[idx].add(src)

def _segment_sum(src, seg, n):
    return jax.ops.segment_sum(src, seg, n)
kernel_name = 'mk_gnn_resnorm_d2_gnn_r32_94d09d'

def setup_inputs(seed: int=0):
    np.random.seed(seed)
    _w = jnp.asarray

    def _rec_inputs():
        import jax
        import jax.numpy as jnp
        _gk = jax.random.key(seed)
        x = -0.0005121 + 1.001 * jax.random.normal(jax.random.fold_in(_gk, 1), (50000, 64), jnp.float32)
        src = jax.random.randint(jax.random.fold_in(_gk, 2), (50000,), 0, 50000, jnp.int32)
        dst = jax.random.randint(jax.random.fold_in(_gk, 3), (50000,), 0, 50000, jnp.int32)
        _o = jnp.argsort(dst, stable=True)
        src = src[_o]
        dst = dst[_o]
        edge_attr_16 = 0.000254156 + 0.999948 * jax.random.normal(jax.random.fold_in(_gk, 12), (50000, 16), jnp.float32)
        edge_type_8 = jax.random.randint(jax.random.fold_in(_gk, 14), (50000,), 0, 8, jnp.int32)
        return (x, src, dst, edge_attr_16, edge_type_8)
    x, src, dst, edge_attr_16, edge_type_8 = _rec_inputs()

    def _L0_gnn_setup():
        import jax, jax.numpy as jnp
        import numpy as np
        N = 50000
        E = 25000
        DIM = 64
        EDGE_DIM = 16
        HEADS = 4
        TIME_STEP = 3
        NEG_SLOPE = 0.2
        HC = HEADS * DIM

        def _mhta(x, src, dst, edge_attr, Wn, We, Wa, Ws, b):
            xp = x @ Wn
            ep = (edge_attr @ We).reshape(-1, HEADS, DIM)
            x_j = xp[src].reshape(-1, HEADS, DIM)
            x_i = xp[dst].reshape(-1, HEADS, DIM)
            wa = Wa.reshape(HEADS, 3, DIM)
            alpha = jnp.einsum('ehc,hc->eh', x_i, wa[:, 0]) + jnp.einsum('ehc,hc->eh', ep, wa[:, 1]) + jnp.einsum('ehc,hc->eh', x_j, wa[:, 2])
            alpha = jax.nn.leaky_relu(alpha, NEG_SLOPE)
            amax = jax.ops.segment_max(alpha, dst, num_segments=N)
            alpha = jnp.exp(alpha - amax[dst])
            denom = jax.ops.segment_sum(alpha, dst, num_segments=N)
            alpha = alpha / (denom[dst] + 1e-16)
            msg = (alpha[:, :, None] * ep * x_j).reshape(-1, HC)
            aggr = jax.ops.segment_sum(msg, dst, num_segments=N)
            return aggr @ Ws + b

        def _gru_step(m, h, Wih, Whh, bih, bhh):
            gi = m @ Wih.T + bih
            gh = h @ Whh.T + bhh
            i_r, i_z, i_n = jnp.split(gi, 3, axis=-1)
            h_r, h_z, h_n = jnp.split(gh, 3, axis=-1)
            r = jax.nn.sigmoid(i_r + h_r)
            z = jax.nn.sigmoid(i_z + h_z)
            n = jnp.tanh(i_n + r * h_n)
            return (1.0 - z) * n + z * h

        def _layernorm(x, gamma, beta, eps=1e-05):
            mu = jnp.mean(x, axis=-1, keepdims=True)
            var = jnp.mean((x - mu) ** 2, axis=-1, keepdims=True)
            return (x - mu) * jax.lax.rsqrt(var + eps) * gamma + beta
        key = jax.random.key(seed)
        ks = jax.random.split(key, 16)
        rn = lambda k, shape, s=0.1: jax.random.normal(k, shape, jnp.float32) * s
        return {'x': jax.random.normal(ks[0], (N, DIM), jnp.float32), 'edge_index': jax.random.randint(ks[1], (2, E), 0, N, jnp.int32), 'edge_attr': jax.random.normal(ks[2], (E, EDGE_DIM), jnp.float32), 'Wn': rn(ks[3], (DIM, HC)), 'We': rn(ks[4], (EDGE_DIM, HC)), 'Wa': rn(ks[5], (1, HEADS, 3 * DIM)), 'Ws': rn(ks[6], (HC, DIM)), 'b': jnp.zeros((DIM,), jnp.float32), 'Wih': rn(ks[7], (3 * DIM, DIM)), 'Whh': rn(ks[8], (3 * DIM, DIM)), 'bih': rn(ks[9], (3 * DIM,)), 'bhh': rn(ks[10], (3 * DIM,)), 'gamma': jnp.ones((DIM,), jnp.float32), 'beta': jnp.zeros((DIM,), jnp.float32)}
    _L0_gnn_all = _L0_gnn_setup()
    _L0_gnn_in = {k: v for k, v in _L0_gnn_all.items() if k in ('Wn', 'We', 'Wa', 'Ws', 'b', 'Wih', 'Whh', 'bih', 'bhh', 'gamma', 'beta')}
    del _L0_gnn_all

    def _L1_gnn_setup():
        import jax, jax.numpy as jnp
        import numpy as np
        N_NODES = 50000
        N_EDGES = 25000
        FEAT_DIM = 64
        NUM_RELS = 8
        key = jax.random.key(seed)
        k1, k2, k3, k4, k5 = jax.random.split(key, 5)
        features = jax.random.normal(k1, (N_NODES, FEAT_DIM), dtype=jnp.float32)
        limit = np.sqrt(2.0) * np.sqrt(6.0 / (FEAT_DIM + FEAT_DIM))
        weight_r = jax.random.uniform(k2, (NUM_RELS, FEAT_DIM, FEAT_DIM), dtype=jnp.float32, minval=-limit, maxval=limit)
        src = jax.random.randint(k3, (N_EDGES,), 0, N_NODES, dtype=jnp.int64 if jax.config.jax_enable_x64 else jnp.int32)
        dst = jax.random.randint(k4, (N_EDGES,), 0, N_NODES, dtype=src.dtype)
        etype = jax.random.randint(k5, (N_EDGES,), 0, NUM_RELS, dtype=src.dtype)
        return {'features': features, 'weight_r': weight_r, 'src': src, 'dst': dst, 'etype': etype}
    _L1_gnn_all = _L1_gnn_setup()
    _L1_gnn_in = {k: v for k, v in _L1_gnn_all.items() if k in ('weight_r',)}
    del _L1_gnn_all
    return {'x': x, 'src': src, 'dst': dst, 'edge_attr_16': edge_attr_16, 'edge_type_8': edge_type_8, 'L0_gnn_Wn': _L0_gnn_in['Wn'], 'L0_gnn_We': _L0_gnn_in['We'], 'L0_gnn_Wa': _L0_gnn_in['Wa'], 'L0_gnn_Ws': _L0_gnn_in['Ws'], 'L0_gnn_b': _L0_gnn_in['b'], 'L0_gnn_Wih': _L0_gnn_in['Wih'], 'L0_gnn_Whh': _L0_gnn_in['Whh'], 'L0_gnn_bih': _L0_gnn_in['bih'], 'L0_gnn_bhh': _L0_gnn_in['bhh'], 'L0_gnn_gamma': _L0_gnn_in['gamma'], 'L0_gnn_beta': _L0_gnn_in['beta'], 'L1_gnn_weight_r': _L1_gnn_in['weight_r']}

def reference(x, src, dst, edge_attr_16, edge_type_8, L0_gnn_Wn, L0_gnn_We, L0_gnn_Wa, L0_gnn_Ws, L0_gnn_b, L0_gnn_Wih, L0_gnn_Whh, L0_gnn_bih, L0_gnn_bhh, L0_gnn_gamma, L0_gnn_beta, L1_gnn_weight_r):
    import jax
    import jax.numpy as jnp

    def _L0_gnn_ref(x, edge_index, edge_attr, Wn, We, Wa, Ws, b, Wih, Whh, bih, bhh, gamma, beta):
        import jax, jax.numpy as jnp
        import numpy as np
        N = 50000
        E = 25000
        DIM = 64
        EDGE_DIM = 16
        HEADS = 4
        TIME_STEP = 3
        NEG_SLOPE = 0.2
        HC = HEADS * DIM

        def _mhta(x, src, dst, edge_attr, Wn, We, Wa, Ws, b):
            xp = x @ Wn
            ep = (edge_attr @ We).reshape(-1, HEADS, DIM)
            x_j = xp[src].reshape(-1, HEADS, DIM)
            x_i = xp[dst].reshape(-1, HEADS, DIM)
            wa = Wa.reshape(HEADS, 3, DIM)
            alpha = jnp.einsum('ehc,hc->eh', x_i, wa[:, 0]) + jnp.einsum('ehc,hc->eh', ep, wa[:, 1]) + jnp.einsum('ehc,hc->eh', x_j, wa[:, 2])
            alpha = jax.nn.leaky_relu(alpha, NEG_SLOPE)
            amax = jax.ops.segment_max(alpha, dst, num_segments=N)
            alpha = jnp.exp(alpha - amax[dst])
            denom = jax.ops.segment_sum(alpha, dst, num_segments=N)
            alpha = alpha / (denom[dst] + 1e-16)
            msg = (alpha[:, :, None] * ep * x_j).reshape(-1, HC)
            aggr = jax.ops.segment_sum(msg, dst, num_segments=N)
            return aggr @ Ws + b

        def _gru_step(m, h, Wih, Whh, bih, bhh):
            gi = m @ Wih.T + bih
            gh = h @ Whh.T + bhh
            i_r, i_z, i_n = jnp.split(gi, 3, axis=-1)
            h_r, h_z, h_n = jnp.split(gh, 3, axis=-1)
            r = jax.nn.sigmoid(i_r + h_r)
            z = jax.nn.sigmoid(i_z + h_z)
            n = jnp.tanh(i_n + r * h_n)
            return (1.0 - z) * n + z * h

        def _layernorm(x, gamma, beta, eps=1e-05):
            mu = jnp.mean(x, axis=-1, keepdims=True)
            var = jnp.mean((x - mu) ** 2, axis=-1, keepdims=True)
            return (x - mu) * jax.lax.rsqrt(var + eps) * gamma + beta
        src, dst = (edge_index[0], edge_index[1])
        h = x
        xc = x
        for _ in range(TIME_STEP):
            m = jax.nn.celu(_mhta(xc, src, dst, edge_attr, Wn, We, Wa, Ws, b))
            h = _gru_step(m, h, Wih, Whh, bih, bhh)
            xc = _layernorm(h, gamma, beta)
        return xc

    def _L1_gnn_ref(features, weight_r, src, dst, etype):
        import jax, jax.numpy as jnp
        import numpy as np
        N_NODES = 50000
        N_EDGES = 25000
        FEAT_DIM = 64
        NUM_RELS = 8
        N, D = features.shape
        c = 0.2
        deg = jax.ops.segment_sum(jnp.ones(dst.shape, dtype=features.dtype), dst, num_segments=N)
        hw = jnp.einsum('nd,rdf->rnf', features, weight_r)
        msg = hw[etype, src] / deg[dst][:, None]
        M = jax.ops.segment_sum(msg, dst, num_segments=N)
        updated = jax.nn.relu(c * features + (1.0 - c) * M)
        return jnp.where((deg > 0)[:, None], updated, features)
    edge_index = jnp.stack([src, dst])
    x = _layernorm(x + _L0_gnn_ref(x, edge_index, edge_attr_16, L0_gnn_Wn, L0_gnn_We, L0_gnn_Wa, L0_gnn_Ws, L0_gnn_b, L0_gnn_Wih, L0_gnn_Whh, L0_gnn_bih, L0_gnn_bhh, L0_gnn_gamma, L0_gnn_beta), axis=-1)
    x = _layernorm(x + _L1_gnn_ref(x, L1_gnn_weight_r, src, dst, edge_type_8), axis=-1)
    return x

_drawn_inputs = setup_inputs


def setup_inputs(seed=0):
    import zlib

    import numpy as np

    out = dict(_drawn_inputs(seed))
    spreads = {'L0_gnn_b': (0.0, 0.1), 'L0_gnn_gamma': (1.0, 0.2), 'L0_gnn_beta': (0.0, 0.1)}
    factors = {}
    for name, (base, spread) in spreads.items():
        noise = np.random.default_rng([zlib.crc32(name.encode()), seed]).standard_normal(out[name].shape)
        drawn = base * np.exp(spread * noise) if base else spread * noise
        out[name] = jnp.asarray(drawn.astype(out[name].dtype))
    for name, factor in factors.items():
        out[name] = (out[name] * factor).astype(out[name].dtype)
    return out
```

```python
from contextlib import ExitStack, contextmanager

import concourse.bass as bass
from concourse import mybir

F32 = mybir.dt.float32
F16 = mybir.dt.float16
I32 = mybir.dt.int32
ALU = mybir.AluOpType
ACT = mybir.ActivationFunctionType
AX = mybir.AxisListType.X

P = 128
N = 50000
D = 64
K = 16
HEADS = 4
HC = HEADS * D
RELS = 8
TILES = -(-N // P) + 1
J = 8
NB = TILES // J
SLOTS = P * TILES
Q = J // 2
BIG = 1.0e30
STEPS = 3
assert TILES % J == 0 and SLOTS >= N

TO_GATE = {}


class Shared:
    pass


class Phase:
    def __init__(self, sem, sb, pb):
        self.sem, self.sb, self.pb = sem, sb, pb


def need(eng, sem, value):
    if isinstance(value, int):
        if value > 0:
            eng.wait_ge(sem, value)
    else:
        eng.wait_ge(sem, value)
        eng.sem_inc(TO_GATE[eng.engine], 1)


def pipelined(eng, *stages):
    depth = len(stages)

    def at(time, parity, half):
        for k in reversed(range(depth)):
            if stages[k] is None:
                continue
            if isinstance(time, int):
                if 0 <= time - k < NB:
                    stages[k](time - k, (time - k) % 2, (time - k) // 2)
            else:
                base = parity - k
                stages[k](time - k, base % 2, half + base // 2)

    first = depth + 2 + (depth % 2)
    pairs = (NB - first) // 2
    for time in range(first):
        at(time, 0, 0)
    with eng.Fori(0, pairs) as it:
        at(it * 2 + first, 0, it + first // 2)
        at(it * 2 + (first + 1), 1, it + first // 2)
    for time in range(first + 2 * pairs, NB + depth - 1):
        at(time, 0, 0)


@contextmanager
def phase(nc, name):
    with ExitStack() as ctx:
        used = []

        def sem(what):
            s = ctx.enter_context(nc.semaphore(f"{name}_{what}"))
            used.append(s)
            return s

        def sb(what, shape, dtype=F32):
            return ctx.enter_context(nc.sbuf_tensor(f"{name}_{what}", shape, dtype))

        def pb(what, shape):
            return ctx.enter_context(nc.psum_tensor(f"{name}_{what}", shape, F32))

        yield Phase(sem, sb, pb)

        with nc.Block() as block:
            @block.gpsimd
            def _(pool):
                for s in used:
                    pool.sem_clear(s)


def rows(table, blk, first=0):
    return table[first:first + SLOTS, :].rearrange("(p j) d -> p j d", p=P)[:, bass.ds(blk * J, J), :]


def cols(t, blk):
    return t[:, bass.ds(blk * J, J)]


def hcols(t, blk):
    return t[:, :, bass.ds(blk * J, J)].rearrange("p h t -> p t h")


def setup_phase(nc, g, dram):
    with phase(nc, "setup") as ph:
        loaded, made, chain, widened = (ph.sem(n) for n in ("loaded", "made", "chain", "widened"))
        prev, cur, nxt = (ph.sb(n, [P, TILES]) for n in ("prev", "cur", "nxt"))
        iprev, icur, inxt = (ph.sb("i" + n, [P, TILES], I32) for n in ("prev", "cur", "nxt"))
        wn, we = ph.sb("wn", [P, HC]), ph.sb("we", [P, HC])
        wa = ph.sb("wa", [P, 3, HC])
        prod = ph.sb("prod", [P, 3, HC])
        w4 = ph.sb("w4", [P, 3, HEADS])
        half, eighth = ph.sb("half", [P, 2]), ph.sb("eighth", [P, J])
        ones = ph.sb("ones", [P, TILES])
        whole = ph.sb("whole", [P, 3, HEADS])
        loads = [(icur, dram["dst_cur"]), (iprev, dram["dst_prev"]), (inxt, dram["dst_next"]), (g.src, dram["src"]),
                 (g.rel, dram["rel"]), (wn, dram["wn_twice"]), (we, dram["we_eight"]), (wa, dram["wa"]), (half, dram["half"]),
                 (eighth, dram["eighth"]), (g.wn, dram["wn"]), (g.we, dram["we"]), (g.ws, dram["ws"]), (g.wg, dram["wg"]),
                 (g.bg, dram["bg"]), (g.ident, dram["ident"]), (g.b, dram["b"]), (g.gamma, dram["gamma"]),
                 (g.beta, dram["beta"])]
        ps = ph.pb("ps", [P, 3, P])

        with nc.Block() as block:
            @block.sync
            def _(sp):
                for dst, src in loads:
                    sp.dma_start(dst[:], src).then_inc(loaded, 16)
                sp.wait_ge(loaded, 16 * len(loads))

            @block.vector
            def _(dve):
                n = [0]

                def link(ins):
                    n[0] += 1
                    ins.then_inc(chain, 1)
                    dve.wait_ge(chain, n[0])

                dve.wait_ge(loaded, 16 * len(loads))
                link(dve.memset(ones[:], 1.0))
                link(dve.memset(g.half_power[:], -0.5))
                link(dve.memset(g.ones2[:], 1.0))
                link(dve.tensor_copy(g.dst_idx[:], icur[:]))
                for f, i in ((cur, icur), (prev, iprev), (nxt, inxt)):
                    link(dve.tensor_copy(f[:], i[:]))
                link(dve.tensor_tensor(g.goes_on[:], cur[:], prev[:], ALU.is_equal))
                link(dve.tensor_tensor(g.not_end[:], cur[:], nxt[:], ALU.is_equal))
                link(dve.tensor_scalar(g.shut[:], g.goes_on[:], -1.0, BIG, ALU.add, ALU.mult))
                link(dve.tensor_scalar(g.is_end[:], g.not_end[:], -1.0, 1.0, ALU.mult, ALU.add))
                link(dve.tensor_tensor_scan(g.head[:], g.goes_on[:], ones[:], 1.0, ALU.mult, ALU.mult))
                link(dve.tensor_scalar(prev[:], g.not_end[:], float(1 << 20), None, ALU.mult))
                link(dve.tensor_tensor(cur[:], cur[:], prev[:], ALU.add))
                link(dve.tensor_copy(g.out_idx[:], cur[:]))
                for k in range(3):
                    link(dve.tensor_tensor(prod[:, k, :], (we if k == 1 else wn)[:], wa[:, k, :], ALU.mult))
                link(dve.tensor_reduce(w4[:], prod[:].rearrange("p k (h c) -> p k h c", h=HEADS), AX, ALU.add))
                for out, k, mask, m in ((g.w_dst, 0, half, 2), (g.w_src, 2, half, 2), (g.w_edge, 1, eighth, J)):
                    link(dve.tensor_tensor(out[:], mask[:].unsqueeze(2).to_broadcast([P, m, HEADS]),
                                           w4[:, k, :].unsqueeze(1).to_broadcast([P, m, HEADS]), ALU.mult))
                link(dve.tensor_reduce(whole[:, 0, 0:1], g.goes_on[:], AX, ALU.min))
                link(dve.tensor_reduce(whole[:, 1, 0:1], g.shut[:], AX, ALU.min))
                link(dve.tensor_reduce(whole[:, 2, 0:1], g.not_end[:], AX, ALU.min))
                for k in range(3):
                    dve.tensor_copy(g.whole64[:, k, :], whole[:, k, 0:1].to_broadcast([P, D])).then_inc(widened, 1)
                dve.wait_ge(made, 1)
                link(dve.tensor_copy(g.whole_t[:], ps[0:D, :, :]))

            @block.tensor
            def _(pe):
                pe.wait_ge(loaded, 16 * len(loads))
                pe.wait_ge(widened, 3)
                for k in range(3):
                    ins = pe.transpose(ps[0:D, k, :], g.whole64[:, k, :], g.ident[:])
                ins.then_inc(made, 1)


def gather_phase(nc, g, name, table, width, idx, weights, logits, keep=None, save=None, pos=None):
    with phase(nc, name) as ph:
        copied, gathered, compact = ph.sem("idx_copied"), g.gathered, ph.sem("compact")
        turned, evacuated, kept = ph.sem("turned"), ph.sem("evacuated"), ph.sem("kept")
        projected, logits_out = ph.sem("projected"), ph.sem("logits_out")
        saved = [ph.sem("saved0"), ph.sem("saved1")]
        pos_out = ph.sem("pos_out")
        stage_idx = ph.sb("stage_idx", [P, 2, J], I32)
        stage = ph.sb("stage", [P, 2, J, width])
        tight = ph.sb("tight", [P, 2, J, D]) if pos is not None else stage
        xt = ph.sb("xt", [P, 2, Q, P])
        ps_x, ps_l = ph.pb("ps_x", [P, 2, Q * P]), ph.pb("ps_l", [P, 2, 512])
        done = list(g.gathered_count)
        g.gathered_count[0] += P * (NB - NB // 2)
        g.gathered_count[1] += P * (NB // 2)

        with nc.Block() as block:
            @block.gpsimd
            def _(pool):
                def gather(i, p, n):
                    need(pool, gathered[p], n * P + done[p])
                    pool.tensor_copy(stage_idx[:, p, :], cols(idx, i)).then_inc(copied, 1)
                    need(pool, copied, i + 1)
                    need(pool, turned if pos is None else pos_out, i - 1)
                    if save is not None:
                        need(pool, saved[p], n * 16)
                    for u in range(J):
                        pool.indirect_dma_start(stage[:, p, u, :], None, table,
                                                bass.IndirectOffsetOnAxis(ap=stage_idx[:, p, u:u + 1], axis=0)
                                                ).then_inc(gathered[p], 16)

                pipelined(pool, gather)

            @block.sync
            def _(sp):
                def store(i, p, n):
                    need(sp, gathered[p], n * P + (P + done[p]))
                    sp.dma_start(rows(save, i), stage[:, p, :, :]).then_inc(saved[p], 16)

                if save is not None:
                    pipelined(sp, store)
                    sp.wait_ge(saved[0], 16 * (NB - NB // 2))
                    sp.wait_ge(saved[1], 16 * (NB // 2))

            @block.tensor
            def _(pe):
                def turn(i, p, n):
                    need(pe, gathered[p], n * P + (P + done[p]))
                    if pos is not None:
                        need(pe, compact, i + 1)
                    need(pe, evacuated, i - 1)
                    for q in range(Q):
                        ins = pe.transpose(ps_x[:, p, q * P:(q + 1) * P], tight[:, p, 2 * q:2 * q + 2, :], g.ident[:])
                    ins.then_inc(turned, 1)

                def project(i, p, n):
                    need(pe, evacuated, i + 1)
                    need(pe, logits_out, i - 1)
                    for q in range(Q):
                        ins = pe.matmul(ps_l[:, p, q * 2 * HEADS:(q + 1) * 2 * HEADS], xt[:, p, q, :],
                                        weights[:].rearrange("p s h -> p (s h)"), start=True, stop=True)
                    ins.then_inc(projected, 1)

                pipelined(pe, turn, project)

            @block.scalar
            def _(act):
                def evacuate(i, p, n):
                    need(act, turned, i + 1)
                    need(act, projected, i - 1)
                    if keep is not None:
                        need(act, kept, i - 1)
                    act.activation(xt[:, p, :, :].rearrange("p q e -> p (q e)"), ps_x[:, p, :], ACT.Copy
                                   ).then_inc(evacuated, 1)

                pipelined(act, evacuate)

            @block.vector
            def _(dve):
                def tighten(i, p, n):
                    need(dve, gathered[p], n * P + (P + done[p]))
                    need(dve, turned, i - 1)
                    dve.tensor_copy(tight[:, p, :, :], stage[:, p, :, 0:D]).then_inc(compact, 1)
                    need(dve, compact, i + 1)
                    dve.tensor_copy(cols(pos, i), stage[:, p, :, D]).then_inc(pos_out, 1)

                def hold(i, p, n):
                    need(dve, evacuated, i + 1)
                    dve.tensor_copy(keep[:, bass.ds(i * (J * D), J * D)], xt[:, p, :, :].rearrange("p q e -> p (q e)")
                                    ).then_inc(kept, 1)

                def out(i, p, n):
                    need(dve, projected, i + 1)
                    dve.tensor_copy(hcols(logits, i), ps_l[:, p, 0:J * HEADS].rearrange("p (t h) -> p t h", h=HEADS)
                                    ).then_inc(logits_out, 1)

                pipelined(dve, tighten if pos is not None else None, hold if keep is not None else None, out)


def edge_logit_phase(nc, g, dram):
    with phase(nc, "edge_logit") as ph:
        loaded = [ph.sem("loaded0"), ph.sem("loaded1")]
        turned, evacuated, projected, out_done = (ph.sem(n) for n in ("turned", "evacuated", "projected", "out"))
        ea, et = ph.sb("ea", [P, 2, J, K]), ph.sb("et", [P, 2, P])
        ps_t, ps_l = ph.pb("ps_t", [P, 2, 512]), ph.pb("ps_l", [P, 2, 512])
        with nc.Block() as block:
            @block.sync
            def _(sp):
                def load(i, p, n):
                    need(sp, turned, i - 1)
                    sp.dma_start(ea[:, p, :, :], rows(dram["edge"], i)).then_inc(loaded[p], 16)

                pipelined(sp, load)

            @block.tensor
            def _(pe):
                def turn(i, p, n):
                    need(pe, loaded[p], n * 16 + 16)
                    need(pe, evacuated, i - 1)
                    pe.transpose(ps_t[:, p, 0:P], ea[:, p, :, :].rearrange("p t k -> p (t k)"), g.ident[:]
                                 ).then_inc(turned, 1)

                def project(i, p, n):
                    need(pe, evacuated, i + 1)
                    need(pe, out_done, i - 1)
                    pe.matmul(ps_l[:, p, 0:J * HEADS], et[:, p, :], g.w_edge[:].rearrange("p t h -> p (t h)"),
                              start=True, stop=True).then_inc(projected, 1)

                pipelined(pe, turn, project)

            @block.scalar
            def _(act):
                def evacuate(i, p, n):
                    need(act, turned, i + 1)
                    need(act, projected, i - 1)
                    act.activation(et[:, p, :], ps_t[:, p, 0:P], ACT.Copy).then_inc(evacuated, 1)

                pipelined(act, evacuate)

            @block.vector
            def _(dve):
                def out(i, p, n):
                    need(dve, projected, i + 1)
                    dve.tensor_copy(hcols(g.l_edge, i), ps_l[:, p, 0:J * HEADS].rearrange("p (t h) -> p t h", h=HEADS)
                                    ).then_inc(out_done, 1)

                pipelined(dve, out)


def scans_phase(nc, g, name, plan, width, program, exp_wanted):
    with phase(nc, name) as ph:
        chain, ends, ends_out, back = (ph.sem(n) for n in ("chain", "ends_turned", "ends_out", "carry_turned"))
        exp_asked, exp_done = ph.sem("exp_asked"), ph.sem("exp_done")
        last = ph.sb("last", [P, width])
        carried = ph.sb("carried", [width, P + 1])
        carry = ph.sb("carry", [P, width])
        ps_e, ps_c = ph.pb("ps_e", [P, 512]), ph.pb("ps_c", [P, 512])

        with nc.Block() as block:
            @block.tensor
            def _(pe):
                for k, (kind, backward) in enumerate(plan):
                    pe.wait_ge(ends, k + 1)
                    pe.transpose(ps_e[0:width, 0:P], last[:], g.ident[:]).then_inc(ends_out, 1)
                    pe.wait_ge(back, k + 1)
                    into = carried[:, 1:P + 1] if backward else carried[:, 0:P]
                    pe.transpose(ps_c[:, 0:width], into, g.ident[0:width, 0:width]).then_inc(ends_out, 1)

            @block.scalar
            def _(act):
                if exp_wanted:
                    act.wait_ge(exp_asked, 1)
                    act.activation(g.alpha[:], g.alpha[:], ACT.Exp).then_inc(exp_done, 1)

            @block.vector
            def _(dve):
                n, k = [0], [0]

                def link(*instructions):
                    for ins in instructions:
                        n[0] += 1
                        ins.then_inc(chain, 1)
                    dve.wait_ge(chain, n[0])

                def scan(out, data):
                    kind, backward = plan[k[0]]
                    flag = g.not_end if backward else g.shut if kind == "max" else g.goes_on
                    ops = (ALU.add, ALU.max) if kind == "max" else (ALU.mult, ALU.add)
                    low = -BIG if kind == "max" else 0.0
                    turn = slice(None, None, -1) if backward else slice(None)

                    def level(start):
                        link(*[dve.tensor_tensor_scan(out[:, h, turn], flag[:, turn], data[:, h, turn], start(h), *ops)
                               for h in range(width)])

                    level(lambda h: low)
                    end = 0 if backward else TILES - 1
                    dve.tensor_copy(last[:], out[:, :, end]).then_inc(ends, 1)
                    whole = g.whole_t[0:width, 2 if backward else 1 if kind == "max" else 0, :]
                    link(dve.memset(carried[:], low))
                    dve.wait_ge(ends_out, 2 * k[0] + 1)
                    into = carried[:, 0:P] if backward else carried[:, 1:P + 1]
                    dve.tensor_tensor_scan(into[:, turn], whole[:, turn], ps_e[0:width, 0:P][:, turn], low, *ops
                                           ).then_inc(back, 1)
                    dve.wait_ge(ends_out, 2 * k[0] + 2)
                    link(dve.tensor_copy(carry[:], ps_c[:, 0:width]))
                    level(lambda h: carry[:, h:h + 1])
                    k[0] += 1

                def exp():
                    dve.sem_inc(exp_asked, 1)
                    dve.wait_ge(exp_done, 1)

                program(dve, scan, link, exp)


def softmax_phase(nc, g, name):
    ends4 = g.is_end[:].unsqueeze(1).to_broadcast([P, HEADS, TILES])

    def program(dve, scan, link, exp):
        link(dve.tensor_tensor(g.tmp[:], g.l_dst[:], ends4, ALU.mult))
        scan(g.alpha, g.tmp)
        link(dve.tensor_tensor(g.alpha[:], g.alpha[:], g.l_edge[:], ALU.add))
        link(dve.tensor_tensor(g.alpha[:], g.alpha[:], g.l_src[:], ALU.add))
        link(dve.scalar_tensor_tensor(g.alpha[:], g.alpha[:], 0.2, g.alpha[:], ALU.mult, ALU.max))
        scan(g.tmp, g.alpha)
        link(dve.tensor_tensor(g.tmp[:], g.tmp[:], ends4, ALU.mult))
        scan(g.l_dst, g.tmp)
        link(dve.tensor_tensor(g.alpha[:], g.alpha[:], g.l_dst[:], ALU.subtract))
        exp()
        scan(g.tmp, g.alpha)
        link(dve.tensor_tensor(g.tmp[:], g.tmp[:], ends4, ALU.mult))
        scan(g.l_dst, g.tmp)
        link(dve.tensor_scalar(g.l_dst[:], g.l_dst[:], 1.0e-16, None, ALU.add))
        link(dve.reciprocal(g.l_dst[:], g.l_dst[:]))
        link(dve.tensor_tensor(g.alpha[:], g.alpha[:], g.l_dst[:], ALU.mult))

    plan = [("sum", True), ("max", False), ("sum", True), ("sum", False), ("sum", True)]
    scans_phase(nc, g, name, plan, HEADS, program, True)


def degree_phase(nc, g):
    def program(dve, scan, link, exp):
        link(dve.memset(g.tmp[:, 0:1, :], 1.0))
        scan(g.l_dst[:, 0:1, :], g.tmp[:, 0:1, :])
        link(dve.reciprocal(g.tmp[:, 0, :], g.l_dst[:, 0, :]))
        link(dve.tensor_scalar(g.share[:], g.tmp[:, 0, :], 0.8, None, ALU.mult))

    scans_phase(nc, g, "degree", [("sum", False)], 1, program, False)


def message_phase(nc, g, name, dram):
    with phase(nc, name) as ph:
        loaded = [ph.sem("loaded0"), ph.sem("loaded1")]
        weighted, turned, evacuated = ph.sem("weighted"), ph.sem("turned"), ph.sem("evacuated")
        node_done, edge_done, node_out, joined = (ph.sem(n) for n in ("node_done", "edge_done", "node_out", "joined"))
        folded, out_done = ph.sem("folded"), ph.sem("out")
        ea = ph.sb("ea", [P, 2, J, K])
        u = ph.sb("u", [P, 2, J, HEADS, K])
        ut = ph.sb("ut", [P, 2, Q * P])
        node = ph.sb("node", [P, 2, Q * P])
        msg = ph.sb("msg", [P, 2, 4, Q * P])
        ps_u, ps_n = ph.pb("ps_u", [P, 2, 512]), ph.pb("ps_n", [P, 2, 512])
        ps_e, ps_m = ph.pb("ps_e", [P, 2, 512]), ph.pb("ps_m", [P, 2, 512])
        units = [(par, c) for par in range(2) for c in range(2)]

        with nc.Block() as block:
            @block.sync
            def _(sp):
                def load(i, p, n):
                    need(sp, weighted, i - 1)
                    sp.dma_start(ea[:, p, :, :], rows(dram["edge"], i)).then_inc(loaded[p], 16)

                pipelined(sp, load)

            @block.tensor
            def _(pe):
                def turn(i, p, n):
                    need(pe, weighted, i + 1)
                    need(pe, evacuated, i - 1)
                    for q in range(Q):
                        ins = pe.transpose(ps_u[:, p, q * P:(q + 1) * P],
                                           u[:, p, 2 * q:2 * q + 2, :, :].rearrange("p t h k -> p (t h k)"), g.ident[:])
                    ins.then_inc(turned, 1)

                def products(i, p, n):
                    need(pe, evacuated, i + 1)
                    for k, (par, c) in enumerate(units):
                        need(pe, node_out, i * 4 + (k - 1))
                        pe.matmul(ps_n[:, k % 2, :], g.wn[:, par, c * P:(c + 1) * P],
                                  g.big[:, bass.ds(i * (J * D), J * D)], start=True, stop=True).then_inc(node_done, 1)
                        need(pe, joined, i * 4 + (k - 1))
                        pe.matmul(ps_e[:, k % 2, :], g.we[:, par, c * P:(c + 1) * P], ut[:, p, :],
                                  start=True, stop=True).then_inc(edge_done, 1)

                def fold(i, p, n):
                    need(pe, joined, i * 4 + 4)
                    need(pe, out_done, i - 1)
                    for t in range(J):
                        for c in range(2):
                            ins = pe.matmul(ps_m[:, p, t * D:(t + 1) * D],
                                            msg[:, p, 2 * (t % 2) + c, (t // 2) * P:(t // 2 + 1) * P], g.ws[:, c, :],
                                            start=(c == 0), stop=(c == 1))
                    ins.then_inc(folded, 1)

                pipelined(pe, turn, products, fold)

            @block.scalar
            def _(act):
                def evacuate(i, p, n):
                    need(act, turned, i + 1)
                    need(act, edge_done, i * 4 - 4)
                    act.activation(ut[:, p, :], ps_u[:, p, :], ACT.Copy).then_inc(evacuated, 1)

                def node_part(i, p, n):
                    for k in range(4):
                        need(act, node_done, i * 4 + (k + 1))
                        need(act, joined, i * 4 + (k - 1))
                        act.activation(node[:, k % 2, :], ps_n[:, k % 2, :], ACT.Copy).then_inc(node_out, 1)

                pipelined(act, evacuate, node_part)

            @block.vector
            def _(dve):
                def weigh(i, p, n):
                    need(dve, loaded[p], n * 16 + 16)
                    need(dve, turned, i - 1)
                    dve.tensor_tensor(u[:, p, :, :, :], hcols(g.alpha, i).unsqueeze(3).to_broadcast([P, J, HEADS, K]),
                                      ea[:, p, :, :].unsqueeze(2).to_broadcast([P, J, HEADS, K]), ALU.mult
                                      ).then_inc(weighted, 1)

                def join(i, p, n):
                    need(dve, folded, i - 1)
                    for k in range(4):
                        need(dve, node_out, i * 4 + (k + 1))
                        need(dve, edge_done, i * 4 + (k + 1))
                        dve.tensor_tensor(msg[:, p, k, :], ps_e[:, k % 2, :], node[:, k % 2, :], ALU.mult
                                          ).then_inc(joined, 1)

                def out(i, p, n):
                    need(dve, folded, i + 1)
                    dve.tensor_copy(g.big[:, bass.ds(i * (J * D), J * D)], ps_m[:, p, :]).then_inc(out_done, 1)

                pipelined(dve, weigh, join, out)


def segment_sum_phase(nc, g, name):
    big3 = g.big[:].rearrange("p (j f) -> p j f", f=D)
    each = 4
    with phase(nc, name) as ph:
        summed, turned, carried_done, back = (ph.sem(n) for n in ("summed", "turned", "carried", "back"))
        cleared = ph.sem("cleared")
        last, carried = ph.sb("last", [P, D]), ph.sb("carried", [D, P + 1])
        copied, out_done = ph.sem("copied"), ph.sem("out")
        ps = ph.pb("ps", [P, 2, 512])
        with nc.Block() as block:
            @block.vector
            def _(dve):
                with dve.Fori(0, D // each) as f:
                    for k in range(each):
                        column = big3[:, :, bass.ds(f * each + k, 1)].rearrange("p j f -> p (j f)")
                        dve.tensor_tensor_scan(column, g.goes_on[:], column, 0.0, ALU.mult, ALU.add).then_inc(summed, 1)
                dve.memset(carried[:], 0.0).then_inc(cleared, 1)
                dve.wait_ge(summed, D)
                dve.tensor_copy(last[:], big3[:, TILES - 1, :]).then_inc(copied, 1)
                dve.wait_ge(cleared, 1)
                dve.wait_ge(turned, 1)
                dve.tensor_tensor_scan(carried[:, 1:P + 1], g.whole_t[:, 0, :], ps[0:D, 0, 0:P], 0.0, ALU.mult, ALU.add
                                       ).then_inc(carried_done, 1)
                dve.wait_ge(back, 1)
                dve.tensor_copy(g.carry[:], ps[:, 1, 0:D]).then_inc(out_done, 1)

            @block.tensor
            def _(pe):
                pe.wait_ge(copied, 1)
                pe.transpose(ps[0:D, 0, 0:P], last[:], g.ident[:]).then_inc(turned, 1)
                pe.wait_ge(carried_done, 1)
                pe.transpose(ps[:, 1, 0:D], carried[:, 0:P], g.ident[0:D, 0:D]).then_inc(back, 1)


def gru_phase(nc, g, name, summed, state_in, state_out, normed, first, logits):
    big = g.big
    with phase(nc, name) as ph:
        (s_carry1, s_carry2, s_total, s_expd, s_capped, s_celu, s_turned, s_evacuated, s_gates,
         s_tanh_rz, s_reset1, s_reset2, s_cand, s_diff, s_mixed, s_h_new, s_sum1, s_mean, s_centred,
         s_squared, s_sum2, s_spread, s_power, s_scaled, s_gained, s_shifted, s_turned2, s_evacuated2,
         s_projected, s_logits_out) = (
            ph.sem(n) for n in ("carry1", "carry2", "total", "expd", "capped", "celu", "turned", "evacuated", "gates",
            "tanh_rz", "reset1", "reset2", "cand", "diff", "mixed", "h_new", "sum1", "mean",
            "centred", "squared", "sum2", "spread", "power", "scaled", "gained", "shifted",
            "turned2", "evacuated2", "projected", "logits_out"))
        loaded, h_saved, x_saved = ([ph.sem(f"{n}{p}") for p in range(2)] for n in ("loaded", "h_saved", "x_saved"))
        mh, mht = (g.work[:, k * 4 * J * D:(k + 1) * 4 * J * D].rearrange("p (s j f) -> p s j f", s=2, j=J) for k in range(2))
        shape = [P, 2, J, D]
        first_part, total, expd = ph.sb("first_part", shape), ph.sb("total", shape), ph.sb("expd", shape)
        rz = ph.sb("rz", [P, 2, J, 2 * D])
        cand, diff, h_new = ph.sb("cand", shape), ph.sb("diff", shape), ph.sb("h_new", shape)
        centred, normal = ph.sb("centred", shape), ph.sb("normal", shape)
        small = ph.sb("small", [P, 2, 5, J])
        nt = ph.sb("nt", [P, 2, Q, P])
        ps_t = ph.pb("ps_t", [P, J, P])
        ps_g = ph.pb("ps_g", [P, J, 2 * P])
        ps_x, ps_l = ph.pb("ps_x", [P, 512]), ph.pb("ps_l", [P, 512])
        bias = g.b[:].unsqueeze(1).to_broadcast([P, J, D])
        H = J // 2

        def sub(p, h):
            return (slice(None), p, slice(h * H, (h + 1) * H))

        with nc.Block() as block:
            @block.sync
            def _(sp):
                def load(i, p, n):
                    need(sp, s_mixed, i - 1)
                    need(sp, s_turned, i - 1)
                    need(sp, s_diff, i - 1)
                    sp.dma_start(mh[:, p, :, D:2 * D], rows(state_in, i)).then_inc(loaded[p], 16)

                def store_h(i, p, n):
                    need(sp, s_h_new, i + 1)
                    sp.dma_start(rows(state_out, i), h_new[:, p, :, :]).then_inc(h_saved[p], 16)

                def store_x(i, p, n):
                    need(sp, s_shifted, i + 1)
                    sp.dma_start(rows(normed, i, first), normal[:, p, :, :]).then_inc(x_saved[p], 16)

                pipelined(sp, load, None, None, store_h, store_x)
                for q in (h_saved, x_saved):
                    sp.wait_ge(q[0], 16 * (NB - NB // 2))
                    sp.wait_ge(q[1], 16 * (NB // 2))

            @block.gpsimd
            def _(pool):
                def carries(i, p, n):
                    need(pool, s_total, i - 1)
                    pool.tensor_tensor(first_part[:, p], cols(g.head, i).unsqueeze(2).to_broadcast([P, J, D]),
                                       g.carry[:].unsqueeze(1).to_broadcast([P, J, D]), ALU.mult).then_inc(s_carry1, 1)
                    need(pool, s_carry1, i + 1)
                    pool.tensor_tensor(first_part[:, p], first_part[:, p], bias, ALU.add).then_inc(s_carry2, 1)

                def gain(i, p, n):
                    need(pool, s_spread, i + 1)
                    pool.tensor_tensor(small[:, p, 4], small[:, p, 3], g.half_power[:], ALU.pow).then_inc(s_power, 1)
                    need(pool, s_scaled, i + 1)
                    need(pool, s_power, i + 1)
                    pool.tensor_tensor(normal[:, p], normal[:, p], g.gamma[:].unsqueeze(1).to_broadcast([P, J, D]),
                                       ALU.mult).then_inc(s_gained, 1)
                    need(pool, s_gained, i + 1)
                    pool.tensor_tensor(normal[:, p], normal[:, p], g.beta[:].unsqueeze(1).to_broadcast([P, J, D]),
                                       ALU.add).then_inc(s_shifted, 1)

                pipelined(pool, carries if summed else None, None, None, None, gain)

            @block.vector
            def _(dve):
                def total_of(i, p, n):
                    need(dve, s_expd, i - 1)
                    if summed:
                        need(dve, s_carry2, i + 1)
                        dve.tensor_tensor(total[:, p], big[:, bass.ds(i * (J * D), J * D)].rearrange("p (j f) -> p j f", f=D),
                                          first_part[:, p], ALU.add).then_inc(s_total, 1)
                    else:
                        dve.tensor_copy(total[:, p], bias).then_inc(s_total, 1)

                def celu(i, p, n):
                    need(dve, s_expd, i + 1)
                    dve.tensor_scalar(expd[:, p], expd[:, p], -1.0, 0.0, ALU.add, ALU.min).then_inc(s_capped, 1)
                    need(dve, s_capped, i + 1)
                    need(dve, s_turned, i - 1)
                    dve.scalar_tensor_tensor(mh[:, p, :, 0:D], total[:, p], 0.0, expd[:, p], ALU.max, ALU.add
                                             ).then_inc(s_celu, 1)

                def reset(i, p, n):
                    for h in range(2):
                        need(dve, s_gates, 2 * i + (h + 1))
                        need(dve, s_tanh_rz, 2 * i + (h + 1))
                        at = sub(p, h)
                        dve.scalar_tensor_tensor(cand[at], rz[at][:, :, 0:D], 1.0, ps_g[:, h * H:(h + 1) * H, 3 * D:4 * D],
                                                 ALU.add, ALU.mult).then_inc(s_reset1, 1)
                        need(dve, s_reset1, 2 * i + (h + 1))
                        dve.scalar_tensor_tensor(cand[at], cand[at], 0.5, ps_g[:, h * H:(h + 1) * H, 2 * D:3 * D],
                                                 ALU.mult, ALU.add).then_inc(s_reset2, 1)

                def mix(i, p, n):
                    need(dve, s_cand, i + 1)
                    need(dve, loaded[p], n * 16 + 16)
                    dve.tensor_tensor(diff[:, p], mh[:, p, :, D:2 * D], cand[:, p], ALU.subtract).then_inc(s_diff, 1)
                    need(dve, s_diff, i + 1)
                    dve.scalar_tensor_tensor(diff[:, p], rz[:, p, :, D:2 * D], 1.0, diff[:, p], ALU.add, ALU.mult
                                             ).then_inc(s_mixed, 1)
                    need(dve, s_mixed, i + 1)
                    need(dve, h_saved[p], n * 16)
                    dve.scalar_tensor_tensor(h_new[:, p], diff[:, p], 0.5, cand[:, p], ALU.mult, ALU.add
                                             ).then_inc(s_h_new, 1)
                    need(dve, s_h_new, i + 1)
                    dve.tensor_reduce(small[:, p, 0], h_new[:, p], AX, ALU.add).then_inc(s_sum1, 1)
                    need(dve, s_sum1, i + 1)
                    dve.tensor_scalar(small[:, p, 1], small[:, p, 0], 1.0 / D, None, ALU.mult).then_inc(s_mean, 1)
                    need(dve, s_mean, i + 1)
                    dve.tensor_tensor(centred[:, p], h_new[:, p], small[:, p, 1].unsqueeze(2).to_broadcast([P, J, D]),
                                      ALU.subtract).then_inc(s_centred, 1)

                def norm(i, p, n):
                    need(dve, s_squared, i + 1)
                    dve.tensor_reduce(small[:, p, 2], diff[:, p], AX, ALU.add).then_inc(s_sum2, 1)
                    need(dve, s_sum2, i + 1)
                    dve.tensor_scalar(small[:, p, 3], small[:, p, 2], 1.0 / D, 1.0e-5, ALU.mult, ALU.add
                                      ).then_inc(s_spread, 1)
                    need(dve, s_power, i + 1)
                    need(dve, x_saved[p], n * 16)
                    if logits is not None:
                        need(dve, s_turned2, i - 1)
                    dve.tensor_tensor(normal[:, p], centred[:, p], small[:, p, 4].unsqueeze(2).to_broadcast([P, J, D]),
                                      ALU.mult).then_inc(s_scaled, 1)

                def logit_out(i, p, n):
                    need(dve, s_projected, i + 1)
                    dve.tensor_copy(hcols(logits, i), ps_l[:, 0:J * HEADS].rearrange("p (t h) -> p t h", h=HEADS)
                                    ).then_inc(s_logits_out, 1)

                pipelined(dve, total_of, celu, reset, mix, norm, logit_out if logits is not None else None)

            @block.scalar
            def _(act):
                def exp(i, p, n):
                    need(act, s_total, i + 1)
                    need(act, s_celu, i - 1)
                    act.activation(expd[:, p], total[:, p], ACT.Exp).then_inc(s_expd, 1)

                def evacuate(i, p, n):
                    need(act, s_turned, i + 1)
                    need(act, s_gates, 2 * i - 2)
                    act.activation(mht[:, p], ps_t[:], ACT.Copy).then_inc(s_evacuated, 1)

                def squash(i, p, n):
                    need(act, s_mixed, i - 1)
                    for h in range(2):
                        need(act, s_gates, 2 * i + (h + 1))
                        act.activation(rz[sub(p, h)], ps_g[:, h * H:(h + 1) * H, 0:2 * D], ACT.Tanh, scale=0.5
                                       ).then_inc(s_tanh_rz, 1)
                    need(act, s_reset2, 2 * i + 2)
                    act.activation(cand[:, p], cand[:, p], ACT.Tanh).then_inc(s_cand, 1)

                def square(i, p, n):
                    need(act, s_centred, i + 1)
                    act.activation(diff[:, p], centred[:, p], ACT.Square).then_inc(s_squared, 1)

                def evacuate2(i, p, n):
                    need(act, s_turned2, i + 1)
                    need(act, s_projected, i - 1)
                    act.activation(nt[:, p].rearrange("p q e -> p (q e)"), ps_x[:], ACT.Copy).then_inc(s_evacuated2, 1)

                pipelined(act, exp, evacuate, squash, square, None, evacuate2 if logits is not None else None)

            @block.tensor
            def _(pe):
                def turn(i, p, n):
                    need(pe, s_celu, i + 1)
                    need(pe, loaded[p], n * 16 + 16)
                    need(pe, s_evacuated, i)
                    for t in range(J):
                        ins = pe.transpose(ps_t[:, t, :], mh[:, p, t, :], g.ident[:])
                    ins.then_inc(s_turned, 1)

                def gates(i, p, n):
                    need(pe, s_evacuated, i + 1)
                    for h in range(2):
                        need(pe, s_reset2, 2 * i + (h - 1))
                        need(pe, s_tanh_rz, 2 * i + (h - 1))
                        for t in range(h * H, (h + 1) * H):
                            pe.matmul(ps_g[:, t, :], mht[:, p, t, :], g.wg[:], start=True, stop=False)
                            ins = pe.matmul(ps_g[:, t, :], g.ones2[:], g.bg[:], start=False, stop=True)
                        ins.then_inc(s_gates, 1)

                def turn2(i, p, n):
                    need(pe, s_shifted, i + 1)
                    need(pe, s_evacuated2, i)
                    for q in range(Q):
                        ins = pe.transpose(ps_x[:, q * P:(q + 1) * P],
                                           normal[:, p, 2 * q:2 * q + 2, :].rearrange("p t d -> p (t d)"), g.ident[:])
                    ins.then_inc(s_turned2, 1)

                def project(i, p, n):
                    need(pe, s_evacuated2, i + 1)
                    need(pe, s_logits_out, i)
                    for q in range(Q):
                        ins = pe.matmul(ps_l[:, q * 2 * HEADS:(q + 1) * 2 * HEADS], nt[:, p, q, :],
                                        g.w_dst[:].rearrange("p s h -> p (s h)"), start=True, stop=True)
                    ins.then_inc(s_projected, 1)

                more = (turn2, project) if logits is not None else ()
                pipelined(pe, None, turn, gates, None, *more)


def norm_phase(nc, g, name, sources, times, out, first, again=None, relation=False, node_out=None):
    with phase(nc, name) as ph:
        (s_carry1, s_carry2, s_share, s_kept, s_relu, s_added, s_sum1, s_mean, s_centred, s_squared,
         s_sum2, s_spread, s_power, s_scaled, s_sum1b, s_meanb, s_centredb, s_squaredb, s_sum2b,
         s_spreadb, s_powerb, s_scaledb, s_idx) = (
            ph.sem(n) for n in ("carry1", "carry2", "share", "kept", "relu", "added", "sum1", "mean", "centred", "squared",
            "sum2", "spread", "power", "scaled", "sum1b", "meanb", "centredb", "squaredb",
            "sum2b", "spreadb", "powerb", "scaledb", "idx"))
        loaded, saved, saved2 = ([ph.sem(f"{n}{p}") for p in range(2)] for n in ("loaded", "saved", "saved2"))
        shape = [P, 2, J, D]
        a, b, c, sq, y = (ph.sb(n, shape) for n in ("a", "b", "c", "sq", "y"))
        c2, sq2, y2 = (ph.sb(n, shape) for n in ("c2", "sq2", "y2"))
        part = ph.sb("part", shape)
        small, small2 = ph.sb("small", [P, 2, 5, J]), ph.sb("small2", [P, 2, 5, J])
        idx = ph.sb("idx", [P, 2, J], I32)
        several = 16 * len(sources)

        def wide(t, k, p):
            return t[:, p, k].unsqueeze(2).to_broadcast([P, J, D])

        with nc.Block() as block:
            @block.sync
            def _(sp):
                def load(i, p, n):
                    need(sp, s_added, i - 1)
                    if relation:
                        need(sp, s_kept, i - 1)
                    for source, into in zip(sources, (a, b)):
                        sp.dma_start(into[:, p], rows(*source(i))).then_inc(loaded[p], 16)

                def store(i, p, n):
                    need(sp, s_scaled, i + 1)
                    sp.dma_start(rows(out, i, first), y[:, p]).then_inc(saved[p], 16)

                def store2(i, p, n):
                    need(sp, s_scaledb, i + 1)
                    sp.dma_start(rows(again, i), y2[:, p]).then_inc(saved2[p], 16)

                pipelined(sp, load, None, None if relation else store, store2 if again is not None else None)
                for q in ([] if relation else [saved]) + ([saved2] if again is not None else []):
                    sp.wait_ge(q[0], 16 * (NB - NB // 2))
                    sp.wait_ge(q[1], 16 * (NB // 2))

            @block.gpsimd
            def _(pool):
                def carries(i, p, n):
                    need(pool, s_carry2, i - 1)
                    pool.tensor_tensor(part[:, p], cols(g.head, i).unsqueeze(2).to_broadcast([P, J, D]),
                                       g.carry[:].unsqueeze(1).to_broadcast([P, J, D]), ALU.mult).then_inc(s_carry1, 1)

                def power(i, p, n):
                    need(pool, s_spread, i + 1)
                    pool.tensor_tensor(small[:, p, 4], small[:, p, 3], g.half_power[:], ALU.pow).then_inc(s_power, 1)

                def power2(i, p, n):
                    need(pool, s_spreadb, i + 1)
                    pool.tensor_tensor(small2[:, p, 4], small2[:, p, 3], g.half_power[:], ALU.pow).then_inc(s_powerb, 1)

                def scatter(i, p, n):
                    need(pool, g.scattered[p], n * P)
                    pool.tensor_copy(idx[:, p, :], cols(g.out_idx, i)).then_inc(s_idx, 1)
                    need(pool, s_idx, i + 1)
                    need(pool, s_scaled, i + 1)
                    for u in range(J):
                        pool.indirect_dma_start(node_out, bass.IndirectOffsetOnAxis(ap=idx[:, p, u:u + 1], axis=0),
                                                y[:, p, u, :], None, bounds_check=N - 1, oob_is_err=False
                                                ).then_inc(g.scattered[p], 16)

                pipelined(pool, carries if relation else None, None, power,
                          scatter if relation else power2 if again is not None else None)
                if relation:
                    pool.wait_ge(g.scattered[0], P * (NB - NB // 2))
                    pool.wait_ge(g.scattered[1], P * (NB // 2))

            @block.vector
            def _(dve):
                def add(i, p, n):
                    need(dve, loaded[p], several * (n + 1))
                    if relation:
                        need(dve, s_carry1, i + 1)
                        dve.tensor_tensor(b[:, p], g.big[:, bass.ds(i * (J * D), J * D)].rearrange("p (j f) -> p j f", f=D),
                                          part[:, p], ALU.add).then_inc(s_carry2, 1)
                        need(dve, s_carry2, i + 1)
                        dve.tensor_tensor(b[:, p], b[:, p], cols(g.share, i).unsqueeze(2).to_broadcast([P, J, D]),
                                          ALU.mult).then_inc(s_share, 1)
                        need(dve, s_share, i + 1)
                        dve.scalar_tensor_tensor(b[:, p], a[:, p], 0.2, b[:, p], ALU.mult, ALU.add).then_inc(s_kept, 1)
                        need(dve, s_kept, i + 1)
                        dve.scalar_tensor_tensor(a[:, p], b[:, p], 0.0, a[:, p], ALU.max, ALU.add).then_inc(s_relu, 1)
                        need(dve, s_relu, i + 1)
                        total = a
                    else:
                        dve.tensor_tensor(a[:, p], a[:, p], b[:, p], ALU.add).then_inc(s_relu, 1)
                        need(dve, s_relu, i + 1)
                        total = a
                    dve.tensor_reduce(small[:, p, 0], total[:, p], AX, ALU.add).then_inc(s_sum1, 1)
                    need(dve, s_sum1, i + 1)
                    dve.tensor_scalar(small[:, p, 1], small[:, p, 0], 1.0 / D, None, ALU.mult).then_inc(s_mean, 1)
                    need(dve, s_mean, i + 1)
                    dve.tensor_tensor(c[:, p], total[:, p], wide(small, 1, p), ALU.subtract).then_inc(s_added, 1)

                def scale(i, p, n):
                    need(dve, s_squared, i + 1)
                    dve.tensor_reduce(small[:, p, 2], sq[:, p], AX, ALU.add).then_inc(s_sum2, 1)
                    need(dve, s_sum2, i + 1)
                    dve.tensor_scalar(small[:, p, 3], small[:, p, 2], 1.0 / D, 1.0e-5, ALU.mult, ALU.add
                                      ).then_inc(s_spread, 1)
                    need(dve, s_power, i + 1)
                    if relation:
                        need(dve, g.scattered[p], n * P)
                    else:
                        need(dve, saved[p], n * 16)
                    dve.tensor_tensor(y[:, p], c[:, p], wide(small, 4, p), ALU.mult).then_inc(s_scaled, 1)
                    if again is not None:
                        need(dve, s_scaled, i + 1)
                        dve.tensor_reduce(small2[:, p, 0], y[:, p], AX, ALU.add).then_inc(s_sum1b, 1)
                        need(dve, s_sum1b, i + 1)
                        dve.tensor_scalar(small2[:, p, 1], small2[:, p, 0], 1.0 / D, None, ALU.mult).then_inc(s_meanb, 1)
                        need(dve, s_meanb, i + 1)
                        dve.tensor_tensor(c2[:, p], y[:, p], wide(small2, 1, p), ALU.subtract).then_inc(s_centredb, 1)

                def scale2(i, p, n):
                    need(dve, s_squaredb, i + 1)
                    dve.tensor_reduce(small2[:, p, 2], sq2[:, p], AX, ALU.add).then_inc(s_sum2b, 1)
                    need(dve, s_sum2b, i + 1)
                    dve.tensor_scalar(small2[:, p, 3], small2[:, p, 2], 1.0 / D, 0.25e-5, ALU.mult, ALU.add
                                      ).then_inc(s_spreadb, 1)
                    need(dve, s_powerb, i + 1)
                    need(dve, saved2[p], n * 16)
                    dve.tensor_tensor(y2[:, p], c2[:, p], wide(small2, 4, p), ALU.mult).then_inc(s_scaledb, 1)

                pipelined(dve, None, add, scale, scale2 if again is not None else None)

            @block.scalar
            def _(act):
                def square(i, p, n):
                    need(act, s_added, i + 1)
                    need(act, s_sum2, i - 1)
                    act.activation(sq[:, p], c[:, p], ACT.Square).then_inc(s_squared, 1)

                def square2(i, p, n):
                    need(act, s_centredb, i + 1)
                    need(act, s_sum2b, i - 1)
                    act.activation(sq2[:, p], c2[:, p], ACT.Square).then_inc(s_squaredb, 1)

                pipelined(act, None, square, square2 if again is not None else None)


def relation_phase(nc, g, dram, table):
    with phase(nc, "relation") as ph:
        copied, turned, evacuated = ph.sem("idx_copied"), ph.sem("turned"), ph.sem("evacuated")
        multiplied, masked, chosen = ph.sem("multiplied"), ph.sem("masked"), ph.sem("chosen")
        stage_idx = ph.sb("stage_idx", [P, 2, J], I32)
        stage = ph.sb("stage", [P, 2, J, D])
        xt = ph.sb("xt", [P, 2, Q, P])
        mine = ph.sb("mine", [P, 2, RELS, D])
        wr = ph.sb("wr", [P, 2, RELS * D])
        mask = ph.sb("mask", [P, TILES, RELS])
        relf = ph.sb("relf", [P, TILES])
        wr_loaded, rel_done = ph.sem("wr_loaded"), ph.sem("rel_done")
        ps_x, ps_r = ph.pb("ps_x", [P, 2, Q * P]), ph.pb("ps_r", [P, 4, RELS * D])
        done = list(g.gathered_count)
        g.gathered_count[0] += P * (NB - NB // 2)
        g.gathered_count[1] += P * (NB // 2)
        big3 = g.big[:].rearrange("p (j f) -> p j f", f=D)

        with nc.Block() as block:
            @block.gpsimd
            def _(pool):
                def gather(i, p, n):
                    need(pool, g.gathered[p], n * P + done[p])
                    pool.tensor_copy(stage_idx[:, p, :], cols(g.src_slot, i)).then_inc(copied, 1)
                    need(pool, copied, i + 1)
                    need(pool, turned, i - 1)
                    for u in range(J):
                        pool.indirect_dma_start(stage[:, p, u, :], None, table,
                                                bass.IndirectOffsetOnAxis(ap=stage_idx[:, p, u:u + 1], axis=0)
                                                ).then_inc(g.gathered[p], 16)

                pipelined(pool, gather)

            @block.sync
            def _(sp):
                sp.dma_start(wr[:], dram["wr"]).then_inc(wr_loaded, 16)

            @block.tensor
            def _(pe):
                pe.wait_ge(wr_loaded, 16)

                def turn(i, p, n):
                    need(pe, g.gathered[p], n * P + (P + done[p]))
                    need(pe, evacuated, i - 1)
                    for q in range(Q):
                        ins = pe.transpose(ps_x[:, p, q * P:(q + 1) * P], stage[:, p, 2 * q:2 * q + 2, :], g.ident[:])
                    ins.then_inc(turned, 1)

                def multiply(i, p, n):
                    need(pe, evacuated, i + 1)
                    for t in range(J):
                        need(pe, masked, i * J + (t - 3))
                        pe.matmul(ps_r[:, t % 4, :], xt[:, p, t // 2, :], wr[:, t % 2, :], start=True, stop=True
                                  ).then_inc(multiplied, 1)

                pipelined(pe, turn, multiply)

            @block.scalar
            def _(act):
                def evacuate(i, p, n):
                    need(act, turned, i + 1)
                    need(act, multiplied, (i - 1) * J)
                    act.activation(xt[:, p, :, :].rearrange("p q e -> p (q e)"), ps_x[:, p, :], ACT.Copy
                                   ).then_inc(evacuated, 1)

                pipelined(act, evacuate)

            @block.vector
            def _(dve):
                def choose(i, p, n):
                    for t in range(J):
                        need(dve, multiplied, i * J + (t + 1))
                        need(dve, chosen, i * J + (t - 1))
                        here = mask[:, bass.ds(i * J + t, 1), :].rearrange("p j r -> p (j r)")
                        dve.tensor_tensor(mine[:, t % 2], ps_r[:, t % 4, :].rearrange("p (r d) -> p r d", r=RELS),
                                          here.unsqueeze(2).to_broadcast([P, RELS, D]), ALU.mult).then_inc(masked, 1)
                        need(dve, masked, i * J + (t + 1))
                        dve.tensor_reduce(big3[:, bass.ds(i * J + t, 1), :].rearrange("p j f -> p (j f)"),
                                          mine[:, t % 2].rearrange("p r d -> p d r"), AX, ALU.add).then_inc(chosen, 1)

                dve.tensor_copy(relf[:], g.rel[:]).then_inc(rel_done, 1)
                dve.wait_ge(rel_done, 1)
                for r in range(RELS):
                    dve.tensor_scalar(mask[:, :, r], relf[:], float(r), None, ALU.is_equal).then_inc(rel_done, 1)
                dve.wait_ge(rel_done, 1 + RELS)
                pipelined(dve, None, choose)


def position_phase(nc, g, dram):
    with phase(nc, "position") as ph:
        (s_chain, s_iota, s_hi, s_lo, s_count, s_split) = (
            ph.sem(n) for n in ("chain", "iota", "hi", "lo", "count", "split"))
        nlo = ph.sb("nlo", [P, TILES])
        iota_i, iota_f = ph.sb("iota_i", [P, TILES], I32), ph.sb("iota_f", [P, TILES])
        node_i, node_f = ph.sb("node_i", [P, TILES], I32), ph.sb("node_f", [P, TILES])
        hi_i, hi, lo, fix = ph.sb("hi_i", [P, TILES], I32), ph.sb("hi", [P, TILES]), ph.sb("lo", [P, TILES]), ph.sb("fix", [P, TILES])
        hot_hi, hot_lo = ph.sb("hot_hi", [P, 2, J, P], F16), ph.sb("hot_lo", [P, 2, J, TILES], F16)
        ps = ph.pb("ps", [P, 512])
        with nc.Block() as block:
            @block.gpsimd
            def _(pool):
                pool.iota(iota_i[:], [[1, TILES]], base=0, channel_multiplier=0).then_inc(s_iota, 1)
                pool.iota(node_i[:], [[1, TILES]], base=SLOTS, channel_multiplier=TILES).then_inc(s_iota, 1)

            @block.vector
            def _(dve):
                n = [0]

                def link(ins):
                    n[0] += 1
                    ins.then_inc(s_chain, 1)
                    dve.wait_ge(s_chain, n[0])

                dve.wait_ge(s_iota, 2)
                link(dve.tensor_copy(iota_f[:], iota_i[:]))
                link(dve.tensor_copy(g.own_row[:], node_i[:]))
                link(dve.tensor_copy(lo[:], g.dst_idx[:]))
                link(dve.tensor_scalar(hi[:], lo[:], 1.0 / TILES, None, ALU.mult))
                link(dve.tensor_copy(hi_i[:], hi[:]))
                link(dve.tensor_copy(hi[:], hi_i[:]))
                link(dve.scalar_tensor_tensor(lo[:], hi[:], -float(TILES), lo[:], ALU.mult, ALU.add))
                link(dve.tensor_scalar(fix[:], lo[:], 0.0, None, ALU.is_lt))
                link(dve.tensor_tensor(hi[:], hi[:], fix[:], ALU.subtract))
                link(dve.scalar_tensor_tensor(lo[:], fix[:], float(TILES), lo[:], ALU.mult, ALU.add))
                link(dve.tensor_scalar(fix[:], lo[:], float(TILES), None, ALU.is_ge))
                link(dve.tensor_tensor(hi[:], hi[:], fix[:], ALU.add))
                link(dve.scalar_tensor_tensor(lo[:], fix[:], -float(TILES), lo[:], ALU.mult, ALU.add))

                def hot(i, p, k):
                    need(dve, s_count, i - 1)
                    dve.tensor_tensor(hot_hi[:, p], iota_f[:, 0:P].unsqueeze(1).to_broadcast([P, J, P]),
                                      cols(hi, i).unsqueeze(2).to_broadcast([P, J, P]), ALU.is_equal).then_inc(s_hi, 1)
                    dve.tensor_tensor(hot_lo[:, p], iota_f[:].unsqueeze(1).to_broadcast([P, J, TILES]),
                                      cols(lo, i).unsqueeze(2).to_broadcast([P, J, TILES]), ALU.is_equal).then_inc(s_lo, 1)

                pipelined(dve, hot)
                dve.wait_ge(s_count, NB)
                link(dve.tensor_copy(g.count[:], ps[:, 0:TILES]))

            @block.tensor
            def _(pe):
                def count(i, p, k):
                    need(pe, s_hi, i + 1)
                    need(pe, s_lo, i + 1)
                    for t in range(J):
                        edge = isinstance(i, int)
                        ins = pe.matmul(ps[:, 0:TILES], hot_hi[:, p, t, :], hot_lo[:, p, t, :],
                                        start=(edge and i == 0 and t == 0), stop=(edge and i == NB - 1 and t == J - 1),
                                        skip_group_check=True)
                    ins.then_inc(s_count, 1)

                pipelined(pe, count)


def plain_cumulation_phase(nc, g):
    with phase(nc, "cumulate") as ph:
        chain, asked, got, asked2, got2 = (ph.sem(n) for n in ("chain", "asked", "got", "asked2", "got2"))
        ones = ph.sb("ones", [P, TILES])
        cum, has = ph.sb("cum", [P, TILES]), ph.sb("has", [P, TILES])
        last = ph.sb("last", [P, 1])
        carried, carry = ph.sb("carried", [1, P + 1]), ph.sb("carry", [P, 1])
        one1 = ph.sb("one1", [1, 1])
        ps = ph.pb("ps", [P, 2, 512])
        with nc.Block() as block:
            @block.vector
            def _(dve):
                n = [0]

                def link(ins):
                    n[0] += 1
                    ins.then_inc(chain, 1)
                    dve.wait_ge(chain, n[0])

                link(dve.memset(ones[:], 1.0))
                link(dve.memset(one1[:], 1.0))
                link(dve.memset(carried[:], 0.0))
                link(dve.tensor_tensor_scan(cum[:], ones[:], g.count[:], 0.0, ALU.mult, ALU.add))
                dve.tensor_copy(last[:], cum[:, TILES - 1:TILES]).then_inc(asked, 1)
                dve.wait_ge(got, 1)
                dve.tensor_tensor_scan(carried[:, 1:P + 1], ones[0:1, 0:P], ps[0:1, 0, 0:P], 0.0, ALU.mult, ALU.add
                                       ).then_inc(asked2, 1)
                dve.wait_ge(got2, 1)
                link(dve.tensor_copy(carry[:], ps[:, 1, 0:1]))
                link(dve.tensor_scalar(cum[:], cum[:], carry[:, 0:1], -1.0, ALU.add, ALU.add))
                link(dve.tensor_scalar(has[:], g.count[:], 0.0, None, ALU.is_gt))
                link(dve.tensor_tensor(cum[:], cum[:], g.own_row[:], ALU.subtract))
                link(dve.tensor_tensor(cum[:], cum[:], has[:], ALU.mult))
                link(dve.tensor_tensor(g.own_row[:], g.own_row[:], cum[:], ALU.add))

            @block.tensor
            def _(pe):
                pe.wait_ge(asked, 1)
                pe.transpose(ps[0:1, 0, 0:P], last[:], g.ident[:]).then_inc(got, 1)
                pe.wait_ge(asked2, 1)
                pe.wait_ge(chain, 2)
                pe.matmul(ps[:, 1, 0:1], carried[:, 0:P], one1[:], start=True, stop=True).then_inc(got2, 1)


def table_phase(nc, g, x, table):
    with phase(nc, "table") as ph:
        loaded, saved = ([ph.sem(f"{n}{p}") for p in range(2)] for n in ("loaded", "saved"))
        filled, numbered = ph.sem("filled"), ph.sem("numbered")
        a, w = ph.sb("a", [P, 2, J, D]), ph.sb("w", [P, 2, J, D + 1])
        with nc.Block() as block:
            @block.sync
            def _(sp):
                def load(i, p, n):
                    need(sp, filled, i - 1)
                    sp.dma_start(a[:, p], rows(x, i)).then_inc(loaded[p], 16)

                def store(i, p, n):
                    need(sp, filled, i + 1)
                    need(sp, numbered, i + 1)
                    sp.dma_start(rows(table, i), w[:, p]).then_inc(saved[p], 16)

                pipelined(sp, load, None, store)
                sp.wait_ge(saved[0], 16 * (NB - NB // 2))
                sp.wait_ge(saved[1], 16 * (NB // 2))

            @block.vector
            def _(dve):
                def fill(i, p, n):
                    need(dve, loaded[p], n * 16 + 16)
                    need(dve, saved[p], n * 16)
                    dve.tensor_copy(w[:, p, :, 0:D], a[:, p]).then_inc(filled, 1)
                    dve.tensor_copy(w[:, p, :, D], cols(g.own_row, i)).then_inc(numbered, 1)

                pipelined(dve, None, fill)


def build(nc, dram, out, trace=None):
    with ExitStack() as ctx:
        def sb(name, shape, dtype=F32):
            return ctx.enter_context(nc.sbuf_tensor(name, shape, dtype))

        for k, eng in enumerate((nc.sync, nc.scalar, nc.tensor, nc.vector, nc.gpsimd)):
            TO_GATE[eng.engine] = ctx.enter_context(nc.semaphore(f"passed_{k}"))
        g = Shared()
        g.big = sb("big", [P, TILES * D])
        g.src = sb("src", [P, TILES], I32)
        g.src_slot = sb("src_slot", [P, TILES], I32)
        g.dst_idx = sb("dst_idx", [P, TILES], I32)
        g.out_idx = sb("out_idx", [P, TILES], I32)
        g.goes_on = sb("goes_on", [P, TILES])
        g.not_end = sb("not_end", [P, TILES])
        g.shut = sb("shut", [P, TILES])
        g.is_end = sb("is_end", [P, TILES])
        g.head = sb("head", [P, TILES])
        g.share = sb("share", [P, TILES])
        g.count = sb("count", [P, TILES])
        g.own_row = sb("own_row", [P, TILES])
        g.rel = sb("rel", [P, TILES], I32)
        g.l_edge = sb("l_edge", [P, HEADS, TILES])
        g.l_dst = sb("l_dst", [P, HEADS, TILES])
        g.work = sb("work", [P, 3 * HEADS * TILES])
        g.wn = sb("wn", [P, 2, HC])
        g.we = sb("we", [P, 2, HC])
        g.ws = sb("ws", [P, 2, D])
        g.wg = sb("wg", [P, 4 * D])
        g.bg = sb("bg", [2, 4 * D])
        g.ones2 = sb("ones2", [2, P])
        g.ident = sb("ident", [P, P])
        g.b = sb("b", [P, D])
        g.gamma = sb("gamma", [P, D])
        g.beta = sb("beta", [P, D])
        g.w_dst = sb("w_dst", [P, 2, HEADS])
        g.w_src = sb("w_src", [P, 2, HEADS])
        g.w_edge = sb("w_edge", [P, J, HEADS])
        g.half_power = sb("half_power", [P, J])
        g.carry = sb("carry", [P, D])
        g.whole64 = sb("whole64", [P, 3, D])
        g.whole_t = sb("whole_t", [D, 3, P])
        g.l_src, g.tmp, g.alpha = (g.work[:, k * HEADS * TILES:(k + 1) * HEADS * TILES].rearrange("p (h j) -> p h j", h=HEADS)
                                   for k in range(3))
        g.gathered = [ctx.enter_context(nc.semaphore(f"gathered{p}")) for p in range(2)]
        g.scattered = [ctx.enter_context(nc.semaphore(f"scattered{p}")) for p in range(2)]
        g.gathered_count = [0, 0]

        def scratch(name, count, width=D):
            return nc.dram_tensor(name, (count, width), F32, kind="ExternalOutput" if trace else "Internal").ap()

        x_slot = scratch("x_slot", SLOTS)
        table0 = scratch("table0", SLOTS, D + 1)
        h_slot = [scratch(f"h_slot{t}", SLOTS) for t in range(2)]
        h_node = [scratch(f"h_node{t}", SLOTS) for t in range(2)]
        tables = [scratch(f"normed{t}", 2 * SLOTS) for t in range(STEPS)]
        x1 = scratch("x1", 2 * SLOTS)

        setup_phase(nc, g, dram)
        position_phase(nc, g, dram)
        plain_cumulation_phase(nc, g)
        table_phase(nc, g, dram["x"], table0)
        edge_logit_phase(nc, g, dram)
        gather_phase(nc, g, "dst", dram["x"][:, :], D, g.dst_idx, g.w_dst, g.l_dst, save=x_slot)
        for t in range(STEPS):
            if t == 0:
                gather_phase(nc, g, "src0", table0[:, :], D + 1, g.src, g.w_src, g.l_src, keep=g.big, pos=g.src_slot)
            else:
                gather_phase(nc, g, f"src{t}", tables[t - 1][:, :], D, g.src_slot, g.w_src, g.l_src, keep=g.big)
            softmax_phase(nc, g, f"softmax{t}")
            message_phase(nc, g, f"message{t}", dram)
            segment_sum_phase(nc, g, f"sum{t}")
            gru_phase(nc, g, f"gru_slots{t}", True, h_slot[(t - 1) % 2] if t else x_slot, h_slot[t % 2],
                      tables[t], 0, g.l_dst if t < STEPS - 1 else None)
            gru_phase(nc, g, f"gru_nodes{t}", False, h_node[(t - 1) % 2] if t else dram["x"], h_node[t % 2],
                      tables[t], SLOTS, None)
        norm_phase(nc, g, "x1_slots", [lambda i: (x_slot, i), lambda i: (tables[2], i)], 1, x1, 0)
        norm_phase(nc, g, "x1_nodes", [lambda i: (dram["x"], i), lambda i: (tables[2], i, SLOTS)], 1, x1, SLOTS,
                   again=out)
        relation_phase(nc, g, dram, x1[:, :])
        degree_phase(nc, g)
        segment_sum_phase(nc, g, "sum_rel")
        norm_phase(nc, g, "final", [lambda i: (x1, i)], 1, None, 0, relation=True, node_out=out[:, :])


def kernel(**inputs):
    import numpy as np
    import concourse.bacc as bacc
    from concourse import mybir as mb
    from concourse.bass_utils import run_bass_kernel_spmd as run

    a = {k: np.ascontiguousarray(v) for k, v in inputs.items()}
    pad = SLOTS - N

    def padded(v, fill=0):
        return np.concatenate([v, np.full((pad,) + v.shape[1:], fill, v.dtype)])

    def split(v):
        return np.ascontiguousarray(v.reshape(P, TILES))

    def on_all(v):
        return np.ascontiguousarray(np.broadcast_to(v.reshape(1, -1), (P, v.size)))

    f = np.float32
    dst = padded(a["dst"], N)
    edge = np.array([-1], dst.dtype)
    wn, we, wsum = a["L0_gnn_Wn"], a["L0_gnn_We"], a["L0_gnn_Ws"]
    wn_two = np.zeros((P, 2, HC), f)
    we_two = np.zeros((P, 2, HC), f)
    wr_two = np.zeros((P, 2, RELS * D), f)
    for s in range(2):
        wn_two[s * D:(s + 1) * D, s] = wn
        wr_two[s * D:(s + 1) * D, s] = a["L1_gnn_weight_r"].transpose(1, 0, 2).reshape(D, RELS * D)
        for h in range(HEADS):
            we_two[s * D + h * K:s * D + (h + 1) * K, s, h * D:(h + 1) * D] = we[:, h * D:(h + 1) * D]
    wih, whh = a["L0_gnn_Wih"].T, a["L0_gnn_Whh"].T
    wg = np.zeros((P, 4 * D), f)
    wg[0:D, 0:3 * D] = wih
    wg[D:, 0:2 * D] = whh[:, 0:2 * D]
    wg[D:, 3 * D:] = whh[:, 2 * D:]
    bg = np.zeros((2, 4 * D), f)
    bg[0, 0:3 * D] = a["L0_gnn_bih"]
    bg[1, 0:2 * D] = a["L0_gnn_bhh"][0:2 * D]
    bg[1, 3 * D:] = a["L0_gnn_bhh"][2 * D:]
    wa = a["L0_gnn_Wa"].reshape(HEADS, 3, D).transpose(1, 0, 2).reshape(-1)
    half, eighth = np.zeros((P, 2), f), np.zeros((P, J), f)
    half[np.arange(P), np.arange(P) // D] = 1
    eighth[np.arange(P), np.arange(P) // K] = 1
    arrays = dict(
        x=padded(a["x"]), edge=padded(a["edge_attr_16"]), src=split(padded(a["src"])),
        dst_cur=split(dst), dst_prev=split(np.concatenate([edge, dst[:-1]])), dst_next=split(np.concatenate([dst[1:], edge])),
        rel=split(padded(a["edge_type_8"])), wn_twice=np.concatenate([wn, wn]), we_eight=np.tile(we, (P // K, 1)),
        wa=on_all(wa).reshape(P, 3, HC), half=half, eighth=eighth, wn=wn_two, we=we_two,
        ws=np.ascontiguousarray(wsum.reshape(2, P, D).transpose(1, 0, 2)), wg=wg, bg=bg, wr=wr_two,
        ident=np.eye(P, dtype=f), b=on_all(a["L0_gnn_b"]), gamma=on_all(a["L0_gnn_gamma"]), beta=on_all(a["L0_gnn_beta"]))
    nc = bacc.Bacc("TRN2", target_bir_lowering=False, num_devices=1)
    dram = {n: nc.dram_tensor(f"in_{n}", v.shape, mb.dt.from_np(v.dtype), kind="ExternalInput").ap()
            for n, v in arrays.items()}
    out = nc.dram_tensor("result", (SLOTS, D), F32, kind="ExternalOutput").ap()
    build(nc, dram, out)
    r = run(nc, [{f"in_{n}": v for n, v in arrays.items()}], core_ids=[0])
    return r.results[0]["result"][0:N]
```

```python
from contextlib import ExitStack, contextmanager

import concourse.bass as bass
from concourse import mybir

F32 = mybir.dt.float32
F16 = mybir.dt.float16
BF16 = mybir.dt.bfloat16
I32 = mybir.dt.int32
ALU = mybir.AluOpType
ACT = mybir.ActivationFunctionType
AX = mybir.AxisListType.X

P = 128
N = 50000
D = 64
K = 16
HEADS = 4
HC = HEADS * D
RELS = 8
TILES = -(-N // P) + 1
J = 8
NB = TILES // J
SLOTS = P * TILES
Q = J // 2
BIG = 1.0e30
STEPS = 3
assert TILES % J == 0 and SLOTS >= N

TO_GATE = {}


class Shared:
    pass


class Phase:
    def __init__(self, sem, sb, pb):
        self.sem, self.sb, self.pb = sem, sb, pb


def need(eng, sem, value):
    if isinstance(value, int):
        if value > 0:
            eng.wait_ge(sem, value)
    else:
        eng.wait_ge(sem, value)
        eng.sem_inc(TO_GATE[eng.engine], 1)


def interleaved(eng, *steps):
    depth = 1 + max(lag for lag, _ in steps)

    def at(time, parity, half):
        for lag, program in steps:
            if isinstance(time, int):
                if 0 <= time - lag < NB:
                    program(time - lag, (time - lag) % 2, (time - lag) // 2)
            else:
                program(time - lag, (parity - lag) % 2, half + (parity - lag) // 2)

    first = depth + 1 + (depth + 1) % 2
    pairs = (NB - first) // 2
    for time in range(first):
        at(time, 0, 0)
    with eng.Fori(0, pairs) as it:
        at(it * 2 + first, 0, it + first // 2)
        at(it * 2 + (first + 1), 1, it + first // 2)
    for time in range(first + 2 * pairs, NB + depth - 1):
        at(time, 0, 0)


def pipelined(eng, *stages):
    interleaved(eng, *[(k, f) for k, f in reversed(list(enumerate(stages))) if f is not None])


def listed(*steps):
    return [(lag, program) for lag, program in steps if program is not None]


@contextmanager
def phase(nc, name):
    with ExitStack() as ctx:
        used = []

        def sem(what):
            s = ctx.enter_context(nc.semaphore(f"{name}_{what}"))
            used.append(s)
            return s

        def sb(what, shape, dtype=F32):
            return ctx.enter_context(nc.sbuf_tensor(f"{name}_{what}", shape, dtype))

        def pb(what, shape):
            return ctx.enter_context(nc.psum_tensor(f"{name}_{what}", shape, F32))

        yield Phase(sem, sb, pb)

        with nc.Block() as block:
            @block.gpsimd
            def _(pool):
                for s in used:
                    pool.sem_clear(s)


def rows(table, blk, first=0):
    return table[first:first + SLOTS, :].rearrange("(p j) d -> p j d", p=P)[:, bass.ds(blk * J, J), :]


def cols(t, blk):
    return t[:, bass.ds(blk * J, J)]


def hcols(t, blk):
    return t[:, :, bass.ds(blk * J, J)].rearrange("p h t -> p t h")


def setup_phase(nc, g, dram):
    with phase(nc, "setup") as ph:
        loaded, made, chain, widened = (ph.sem(n) for n in ("loaded", "made", "chain", "widened"))
        prev, cur, nxt = (ph.sb(n, [P, TILES]) for n in ("prev", "cur", "nxt"))
        iprev, icur, inxt = (ph.sb("i" + n, [P, TILES], I32) for n in ("prev", "cur", "nxt"))
        wn, we = ph.sb("wn", [P, HC]), ph.sb("we", [P, HC])
        wa = ph.sb("wa", [P, 3, HC])
        prod = ph.sb("prod", [P, 3, HC])
        w4 = ph.sb("w4", [P, 3, HEADS])
        half, eighth = ph.sb("half", [P, 2]), ph.sb("eighth", [P, J])
        ones = ph.sb("ones", [P, TILES])
        whole = ph.sb("whole", [P, 3, HEADS])
        bg, minus = ph.sb("bg", [2, 4 * D]), ph.sb("minus", [P, 1])
        bias, part = ph.sb("bias", [1, 4 * D]), ph.sb("part", [1, 3, 4 * D], BF16)
        e = ph.sb("e", [P, D])
        exp_asked, exp_done, rows_done, biased, parts_done = (
            ph.sem(n) for n in ("exp_asked", "exp_done", "rows_done", "biased", "parts_done"))
        ones_pair = ph.sb("ones_pair", [2, 1])
        ps_b = ph.pb("ps_b", [1, 4 * D])
        loads = [(icur, dram["dst_cur"]), (iprev, dram["dst_prev"]), (inxt, dram["dst_next"]), (g.src, dram["src"]),
                 (g.rel, dram["rel"]), (wn, dram["wn_twice"]), (we, dram["we_eight"]), (wa, dram["wa"]), (half, dram["half"]),
                 (eighth, dram["eighth"]), (g.wn, dram["wn"]), (g.we, dram["we"]), (g.ws, dram["ws"]), (g.wg, dram["wg"]),
                 (bg, dram["bg"]), (g.gamma_col, dram["gamma_col"]), (g.beta_col, dram["beta_col"]),
                 (g.ident, dram["ident"]), (g.b, dram["b"]), (g.gamma, dram["gamma"]),
                 (g.beta, dram["beta"])]
        ps = ph.pb("ps", [P, 3, P])

        with nc.Block() as block:
            @block.sync
            def _(sp):
                for dst, src in loads:
                    sp.dma_start(dst[:], src).then_inc(loaded, 16)
                sp.wait_ge(loaded, 16 * len(loads))
                sp.wait_ge(parts_done, 1)
                for k in range(3):
                    sp.dma_start(g.bias3[k:k + 1, :], part[:, k, :]).then_inc(rows_done, 16)
                sp.wait_ge(rows_done, 48)

            @block.scalar
            def _(act):
                act.wait_ge(exp_asked, 1)
                act.activation(e[:], e[:], ACT.Exp).then_inc(exp_done, 1)

            @block.vector
            def _(dve):
                n = [0]

                def link(ins):
                    n[0] += 1
                    ins.then_inc(chain, 1)
                    dve.wait_ge(chain, n[0])

                dve.wait_ge(loaded, 16 * len(loads))
                link(dve.memset(ones[:], 1.0))
                link(dve.memset(g.half_power[:], -0.5))
                link(dve.memset(g.ones3[:], 1.0))
                link(dve.memset(g.node_bias[:], 0.0))
                link(dve.tensor_copy(g.dst_idx[:], icur[:]))
                for f, i in ((cur, icur), (prev, iprev), (nxt, inxt)):
                    link(dve.tensor_copy(f[:], i[:]))
                link(dve.tensor_tensor(g.goes_on[:], cur[:], prev[:], ALU.is_equal))
                link(dve.tensor_tensor(g.not_end[:], cur[:], nxt[:], ALU.is_equal))
                link(dve.tensor_scalar(g.shut[:], g.goes_on[:], -1.0, BIG, ALU.add, ALU.mult))
                link(dve.tensor_scalar(g.is_end[:], g.not_end[:], -1.0, 1.0, ALU.mult, ALU.add))
                link(dve.tensor_tensor_scan(g.head[:], g.goes_on[:], ones[:], 1.0, ALU.mult, ALU.mult))
                link(dve.tensor_scalar(prev[:], g.not_end[:], float(1 << 20), None, ALU.mult))
                link(dve.tensor_tensor(cur[:], cur[:], prev[:], ALU.add))
                link(dve.tensor_copy(g.out_idx[:], cur[:]))
                dve.tensor_scalar(e[:], g.b[:], 0.0, None, ALU.min).then_inc(exp_asked, 1)
                dve.wait_ge(exp_done, 1)
                link(dve.scalar_tensor_tensor(g.m_empty[:], g.b[:], 0.0, e[:], ALU.max, ALU.add))
                link(dve.memset(ones_pair[:], 1.0))
                link(dve.memset(minus[:], 0.0))
                dve.memset(minus[0:D, :], -1.0).then_inc(biased, 1)
                dve.wait_ge(biased, 2)
                link(dve.tensor_copy(bias[:], ps_b[:]))
                for k in range(3):
                    link(dve.tensor_copy(part[:, k, :], bias[:]))
                    link(dve.tensor_tensor(bias[:], bias[:], part[:, k, :], ALU.subtract))
                dve.sem_inc(parts_done, 1)
                for k in range(3):
                    link(dve.tensor_tensor(prod[:, k, :], (we if k == 1 else wn)[:], wa[:, k, :], ALU.mult))
                link(dve.tensor_reduce(w4[:], prod[:].rearrange("p k (h c) -> p k h c", h=HEADS), AX, ALU.add))
                for out, k, mask, m in ((g.w_dst, 0, half, 2), (g.w_src, 2, half, 2), (g.w_edge, 1, eighth, J)):
                    link(dve.tensor_tensor(out[:], mask[:].unsqueeze(2).to_broadcast([P, m, HEADS]),
                                           w4[:, k, :].unsqueeze(1).to_broadcast([P, m, HEADS]), ALU.mult))
                link(dve.tensor_reduce(whole[:, 0, 0:1], g.goes_on[:], AX, ALU.min))
                link(dve.tensor_reduce(whole[:, 1, 0:1], g.shut[:], AX, ALU.min))
                link(dve.tensor_reduce(whole[:, 2, 0:1], g.not_end[:], AX, ALU.min))
                for k in range(3):
                    dve.tensor_copy(g.whole64[:, k, :], whole[:, k, 0:1].to_broadcast([P, D])).then_inc(widened, 1)
                dve.wait_ge(made, 1)
                link(dve.tensor_copy(g.whole_t[:], ps[0:D, :, :]))

            @block.tensor
            def _(pe):
                pe.wait_ge(loaded, 16 * len(loads))
                pe.wait_ge(biased, 1)
                pe.matmul(ps_b[:], minus[:], g.wg[:], start=True, stop=False)
                pe.matmul(ps_b[:], ones_pair[:], bg[:], start=False, stop=True).then_inc(biased, 1)
                pe.wait_ge(widened, 3)
                for k in range(3):
                    ins = pe.transpose(ps[0:D, k, :], g.whole64[:, k, :], g.ident[:])
                ins.then_inc(made, 1)


def gather_phase(nc, g, name, table, width, idx, weights, logits, keep=None, save=None, pos=None, nodes=None):
    with phase(nc, name) as ph:
        copied, gathered, compact = ph.sem("idx_copied"), g.gathered, ph.sem("compact")
        turned, evacuated, kept = ph.sem("turned"), ph.sem("evacuated"), ph.sem("kept")
        projected, logits_out = ph.sem("projected"), ph.sem("logits_out")
        saved = [ph.sem("saved0"), ph.sem("saved1")]
        pos_out = ph.sem("pos_out")
        stage_idx = ph.sb("stage_idx", [P, 2, J], I32)
        stage = ph.sb("stage", [P, 2, J, width])
        tight = ph.sb("tight", [P, 1, J, D]) if pos is not None else None
        xt = ph.sb("xt", [P, 2, Q, P])
        ps_x, ps_l = ph.pb("ps_x", [P, 1, Q * P]), ph.pb("ps_l", [P, 512])
        done = list(g.gathered_count)
        g.gathered_count[0] += P * (NB - NB // 2)
        g.gathered_count[1] += P * (NB // 2)
        gru = None
        if nodes is not None:
            state, normed = nodes
            spare = 2 * HEADS * TILES - 6 * J * D
            free = g.work[:, HEADS * TILES:HEADS * TILES + 6 * J * D]
            assert spare >= 0
            mh = free[:, 0:4 * J * D].rearrange("p (s j f) -> p s j f", s=2, j=J)
            hx = free[:, 4 * J * D:6 * J * D].rearrange("p (s j f) -> p s j f", s=2, j=J)
            gru = Gru(nc, g, ph, state, normed, SLOTS, False, None, mh, hx)

        with nc.Block() as block:
            @block.gpsimd
            def _(pool):
                def gather(i, p, n):
                    need(pool, gathered[p], n * P + done[p])
                    pool.tensor_copy(stage_idx[:, p, :], cols(idx, i)).then_inc(copied, 1)
                    need(pool, copied, i + 1)
                    need(pool, turned if pos is None else pos_out, i - 1)
                    if save is not None:
                        need(pool, saved[p], n * 16)
                    for u in range(J):
                        pool.indirect_dma_start(stage[:, p, u, :], None, table,
                                                bass.IndirectOffsetOnAxis(ap=stage_idx[:, p, u:u + 1], axis=0)
                                                ).then_inc(gathered[p], 16)

                interleaved(pool, (0, gather), *(gru.pool(pool) if gru else ()))

            @block.sync
            def _(sp):
                def store(i, p, n):
                    need(sp, gathered[p], n * P + (P + done[p]))
                    sp.dma_start(rows(save, i), stage[:, p, :, :]).then_inc(saved[p], 16)

                if save is not None:
                    interleaved(sp, (0, store))
                    sp.wait_ge(saved[0], 16 * (NB - NB // 2))
                    sp.wait_ge(saved[1], 16 * (NB // 2))
                if gru:
                    interleaved(sp, *gru.sync(sp))
                    gru.sync_end(sp)

            @block.tensor
            def _(pe):
                if gru:
                    pe.wait_ge(gru.filled, 2)

                def turn(i, p, n):
                    need(pe, gathered[p], n * P + (P + done[p]))
                    if pos is not None:
                        need(pe, compact, i + 1)
                    need(pe, evacuated, i)
                    rows_in = stage[:, p] if pos is None else tight[:, 0]
                    for q in range(Q):
                        ins = pe.transpose(ps_x[:, 0, q * P:(q + 1) * P], rows_in[:, 2 * q:2 * q + 2, :], g.ident[:])
                    ins.then_inc(turned, 1)

                def project(i, p, n):
                    need(pe, evacuated, i + 1)
                    need(pe, logits_out, i)
                    for q in range(Q):
                        ins = pe.matmul(ps_l[:, q * 2 * HEADS:(q + 1) * 2 * HEADS], xt[:, p, q, :],
                                        weights[:].rearrange("p s h -> p (s h)"), start=True, stop=True)
                    ins.then_inc(projected, 1)

                interleaved(pe, (1, project), (0, turn), *(gru.tensor(pe) if gru else ()))

            @block.scalar
            def _(act):
                def evacuate(i, p, n):
                    need(act, turned, i + 1)
                    need(act, projected, i - 1)
                    if keep is not None:
                        need(act, kept, i - 1)
                    act.activation(xt[:, p, :, :].rearrange("p q e -> p (q e)"), ps_x[:, 0, :], ACT.Copy
                                   ).then_inc(evacuated, 1)

                interleaved(act, (0, evacuate), *(gru.scalar(act) if gru else ()))

            @block.vector
            def _(dve):
                if gru:
                    gru.vector_start(dve)

                def tighten(i, p, n):
                    need(dve, gathered[p], n * P + (P + done[p]))
                    need(dve, turned, i)
                    dve.tensor_copy(tight[:, 0], stage[:, p, :, 0:D]).then_inc(compact, 1)
                    need(dve, compact, i + 1)
                    dve.tensor_copy(cols(pos, i), stage[:, p, :, D]).then_inc(pos_out, 1)

                def hold(i, p, n):
                    need(dve, evacuated, i + 1)
                    dve.tensor_copy(keep[:, bass.ds(i * (J * D), J * D)], xt[:, p, :, :].rearrange("p q e -> p (q e)")
                                    ).then_inc(kept, 1)

                def out(i, p, n):
                    need(dve, projected, i + 1)
                    dve.tensor_copy(hcols(logits, i), ps_l[:, 0:J * HEADS].rearrange("p (t h) -> p t h", h=HEADS)
                                    ).then_inc(logits_out, 1)

                interleaved(dve, *listed((0, tighten if pos is not None else None), (2, out),
                                         (1, hold if keep is not None else None)), *(gru.vector(dve) if gru else ()))


def edge_logit_phase(nc, g, dram):
    with phase(nc, "edge_logit") as ph:
        loaded = [ph.sem("loaded0"), ph.sem("loaded1")]
        turned, evacuated, projected, out_done = (ph.sem(n) for n in ("turned", "evacuated", "projected", "out"))
        ea, et = ph.sb("ea", [P, 2, J, K]), ph.sb("et", [P, 2, P])
        ps_t, ps_l = ph.pb("ps_t", [P, 2, 512]), ph.pb("ps_l", [P, 2, 512])
        with nc.Block() as block:
            @block.sync
            def _(sp):
                def load(i, p, n):
                    need(sp, turned, i - 1)
                    sp.dma_start(ea[:, p, :, :], rows(dram["edge"], i)).then_inc(loaded[p], 16)

                pipelined(sp, load)

            @block.tensor
            def _(pe):
                def turn(i, p, n):
                    need(pe, loaded[p], n * 16 + 16)
                    need(pe, evacuated, i - 1)
                    pe.transpose(ps_t[:, p, 0:P], ea[:, p, :, :].rearrange("p t k -> p (t k)"), g.ident[:]
                                 ).then_inc(turned, 1)

                def project(i, p, n):
                    need(pe, evacuated, i + 1)
                    need(pe, out_done, i - 1)
                    pe.matmul(ps_l[:, p, 0:J * HEADS], et[:, p, :], g.w_edge[:].rearrange("p t h -> p (t h)"),
                              start=True, stop=True).then_inc(projected, 1)

                pipelined(pe, turn, project)

            @block.scalar
            def _(act):
                def evacuate(i, p, n):
                    need(act, turned, i + 1)
                    need(act, projected, i - 1)
                    act.activation(et[:, p, :], ps_t[:, p, 0:P], ACT.Copy).then_inc(evacuated, 1)

                pipelined(act, evacuate)

            @block.vector
            def _(dve):
                def out(i, p, n):
                    need(dve, projected, i + 1)
                    dve.tensor_copy(hcols(g.l_edge, i), ps_l[:, p, 0:J * HEADS].rearrange("p (t h) -> p t h", h=HEADS)
                                    ).then_inc(out_done, 1)

                pipelined(dve, out)


def scans_phase(nc, g, name, plan, width, program, exp_wanted):
    with phase(nc, name) as ph:
        chain, ends, ends_out, back = (ph.sem(n) for n in ("chain", "ends_turned", "ends_out", "carry_turned"))
        exp_asked, exp_done = ph.sem("exp_asked"), ph.sem("exp_done")
        last = ph.sb("last", [P, width])
        carried = ph.sb("carried", [width, P + 1])
        carry = ph.sb("carry", [P, width])
        ps_e, ps_c = ph.pb("ps_e", [P, 512]), ph.pb("ps_c", [P, 512])

        with nc.Block() as block:
            @block.tensor
            def _(pe):
                for k, (kind, backward) in enumerate(plan):
                    pe.wait_ge(ends, k + 1)
                    pe.transpose(ps_e[0:width, 0:P], last[:], g.ident[:]).then_inc(ends_out, 1)
                    pe.wait_ge(back, k + 1)
                    into = carried[:, 1:P + 1] if backward else carried[:, 0:P]
                    pe.transpose(ps_c[:, 0:width], into, g.ident[0:width, 0:width]).then_inc(ends_out, 1)

            @block.scalar
            def _(act):
                if exp_wanted:
                    act.wait_ge(exp_asked, 1)
                    act.activation(g.alpha[:], g.alpha[:], ACT.Exp).then_inc(exp_done, 1)

            @block.vector
            def _(dve):
                n, k = [0], [0]

                def link(*instructions):
                    for ins in instructions:
                        n[0] += 1
                        ins.then_inc(chain, 1)
                    dve.wait_ge(chain, n[0])

                def scan(out, data):
                    kind, backward = plan[k[0]]
                    flag = g.not_end if backward else g.shut if kind == "max" else g.goes_on
                    ops = (ALU.add, ALU.max) if kind == "max" else (ALU.mult, ALU.add)
                    low = -BIG if kind == "max" else 0.0
                    turn = slice(None, None, -1) if backward else slice(None)

                    def level(start):
                        link(*[dve.tensor_tensor_scan(out[:, h, turn], flag[:, turn], data[:, h, turn], start(h), *ops)
                               for h in range(width)])

                    level(lambda h: low)
                    end = 0 if backward else TILES - 1
                    dve.tensor_copy(last[:], out[:, :, end]).then_inc(ends, 1)
                    whole = g.whole_t[0:width, 2 if backward else 1 if kind == "max" else 0, :]
                    link(dve.memset(carried[:], low))
                    dve.wait_ge(ends_out, 2 * k[0] + 1)
                    into = carried[:, 0:P] if backward else carried[:, 1:P + 1]
                    dve.tensor_tensor_scan(into[:, turn], whole[:, turn], ps_e[0:width, 0:P][:, turn], low, *ops
                                           ).then_inc(back, 1)
                    dve.wait_ge(ends_out, 2 * k[0] + 2)
                    link(dve.tensor_copy(carry[:], ps_c[:, 0:width]))
                    level(lambda h: carry[:, h:h + 1])
                    k[0] += 1

                def exp():
                    dve.sem_inc(exp_asked, 1)
                    dve.wait_ge(exp_done, 1)

                program(dve, scan, link, exp)


def softmax_phase(nc, g, name):
    ends4 = g.is_end[:].unsqueeze(1).to_broadcast([P, HEADS, TILES])

    def program(dve, scan, link, exp):
        link(dve.tensor_tensor(g.tmp[:], g.l_dst[:], ends4, ALU.mult))
        scan(g.alpha, g.tmp)
        link(dve.tensor_tensor(g.alpha[:], g.alpha[:], g.l_edge[:], ALU.add))
        link(dve.tensor_tensor(g.alpha[:], g.alpha[:], g.l_src[:], ALU.add))
        link(dve.scalar_tensor_tensor(g.alpha[:], g.alpha[:], 0.2, g.alpha[:], ALU.mult, ALU.max))
        scan(g.tmp, g.alpha)
        link(dve.tensor_tensor(g.tmp[:], g.tmp[:], ends4, ALU.mult))
        scan(g.l_dst, g.tmp)
        link(dve.tensor_tensor(g.alpha[:], g.alpha[:], g.l_dst[:], ALU.subtract))
        exp()
        scan(g.tmp, g.alpha)
        link(dve.tensor_tensor(g.tmp[:], g.tmp[:], ends4, ALU.mult))
        scan(g.l_dst, g.tmp)
        link(dve.tensor_scalar(g.l_dst[:], g.l_dst[:], 1.0e-16, None, ALU.add))
        link(dve.reciprocal(g.l_dst[:], g.l_dst[:]))
        link(dve.tensor_tensor(g.alpha[:], g.alpha[:], g.l_dst[:], ALU.mult))

    plan = [("sum", True), ("max", False), ("sum", True), ("sum", False), ("sum", True)]
    scans_phase(nc, g, name, plan, HEADS, program, True)


def degree_phase(nc, g):
    def program(dve, scan, link, exp):
        link(dve.memset(g.tmp[:, 0:1, :], 1.0))
        scan(g.l_dst[:, 0:1, :], g.tmp[:, 0:1, :])
        link(dve.reciprocal(g.tmp[:, 0, :], g.l_dst[:, 0, :]))
        link(dve.tensor_scalar(g.share[:], g.tmp[:, 0, :], 0.8, None, ALU.mult))

    scans_phase(nc, g, "degree", [("sum", False)], 1, program, False)


def message_phase(nc, g, name, dram, norm_of=None):
    with phase(nc, name) as ph:
        loaded = [ph.sem("loaded0"), ph.sem("loaded1")]
        weighted, turned, evacuated = ph.sem("weighted"), ph.sem("turned"), ph.sem("evacuated")
        node_done, edge_done, node_out, joined = (ph.sem(n) for n in ("node_done", "edge_done", "node_out", "joined"))
        folded, out_done = ph.sem("folded"), ph.sem("out")
        ea = ph.sb("ea", [P, 2, J, K])
        u = ph.sb("u", [P, 2, J, HEADS, K])
        ut = ph.sb("ut", [P, 2, Q * P])
        node = ph.sb("node", [P, 2, Q * P])
        msg = ph.sb("msg", [P, 2, 4, Q * P])
        ps_u, ps_n = ph.pb("ps_u", [P, 2, 512]), ph.pb("ps_n", [P, 2, 512])
        ps_e, ps_m = ph.pb("ps_e", [P, 2, 512]), ph.pb("ps_m", [P, 2, 512])
        norm = None
        if norm_of is not None:
            free = [g.work[:, k * 2 * J * D:(k + 1) * 2 * J * D].rearrange("p (s j f) -> p s j f", s=2, j=J)
                    for k in range(2 * HEADS * TILES // (2 * J * D))]
            norm = Norm(nc, g, ph, *norm_of, free)
        units = [(par, c) for par in range(2) for c in range(2)]

        with nc.Block() as block:
            @block.sync
            def _(sp):
                def load(i, p, n):
                    need(sp, weighted, i - 1)
                    sp.dma_start(ea[:, p, :, :], rows(dram["edge"], i)).then_inc(loaded[p], 16)

                interleaved(sp, (0, load), *(norm.sync(sp) if norm else ()))
                if norm:
                    norm.sync_end(sp)

            @block.gpsimd
            def _(pool):
                if norm:
                    interleaved(pool, *norm.pool(pool))

            @block.tensor
            def _(pe):
                def turn(i, p, n):
                    need(pe, weighted, i + 1)
                    need(pe, evacuated, i - 1)
                    for q in range(Q):
                        ins = pe.transpose(ps_u[:, p, q * P:(q + 1) * P],
                                           u[:, p, 2 * q:2 * q + 2, :, :].rearrange("p t h k -> p (t h k)"), g.ident[:])
                    ins.then_inc(turned, 1)

                def products(i, p, n):
                    need(pe, evacuated, i + 1)
                    for k, (par, c) in enumerate(units):
                        need(pe, node_out, i * 4 + (k - 1))
                        pe.matmul(ps_n[:, k % 2, :], g.wn[:, par, c * P:(c + 1) * P],
                                  g.big[:, bass.ds(i * (J * D), J * D)], start=True, stop=True).then_inc(node_done, 1)
                        need(pe, joined, i * 4 + (k - 1))
                        pe.matmul(ps_e[:, k % 2, :], g.we[:, par, c * P:(c + 1) * P], ut[:, p, :],
                                  start=True, stop=True).then_inc(edge_done, 1)

                def fold(i, p, n):
                    need(pe, joined, i * 4 + 4)
                    need(pe, out_done, i - 1)
                    for t in range(J):
                        for c in range(2):
                            ins = pe.matmul(ps_m[:, p, t * D:(t + 1) * D],
                                            msg[:, p, 2 * (t % 2) + c, (t // 2) * P:(t // 2 + 1) * P], g.ws[:, c, :],
                                            start=(c == 0), stop=(c == 1))
                    ins.then_inc(folded, 1)

                interleaved(pe, (2, fold), (1, products), (0, turn))

            @block.scalar
            def _(act):
                def evacuate(i, p, n):
                    need(act, turned, i + 1)
                    need(act, edge_done, i * 4 - 4)
                    act.activation(ut[:, p, :], ps_u[:, p, :], ACT.Copy).then_inc(evacuated, 1)

                def node_part(i, p, n):
                    for k in range(4):
                        need(act, node_done, i * 4 + (k + 1))
                        need(act, joined, i * 4 + (k - 1))
                        act.activation(node[:, k % 2, :], ps_n[:, k % 2, :], ACT.Identity,
                                       bias=g.node_bias[:, k % 2:k % 2 + 1]).then_inc(node_out, 1)

                interleaved(act, (1, node_part), (0, evacuate), *(norm.scalar(act) if norm else ()))

            @block.vector
            def _(dve):
                def weigh(i, p, n):
                    need(dve, loaded[p], n * 16 + 16)
                    need(dve, turned, i - 1)
                    dve.tensor_tensor(u[:, p, :, :, :], hcols(g.alpha, i).unsqueeze(3).to_broadcast([P, J, HEADS, K]),
                                      ea[:, p, :, :].unsqueeze(2).to_broadcast([P, J, HEADS, K]), ALU.mult
                                      ).then_inc(weighted, 1)

                def join(i, p, n):
                    need(dve, folded, i - 1)
                    for k in range(4):
                        need(dve, node_out, i * 4 + (k + 1))
                        need(dve, edge_done, i * 4 + (k + 1))
                        dve.tensor_tensor(msg[:, p, k, :], ps_e[:, k % 2, :], node[:, k % 2, :], ALU.mult
                                          ).then_inc(joined, 1)

                def out(i, p, n):
                    need(dve, folded, i + 1)
                    dve.tensor_copy(g.big[:, bass.ds(i * (J * D), J * D)], ps_m[:, p, :]).then_inc(out_done, 1)

                interleaved(dve, (2, out), (1, join), (0, weigh), *(norm.vector(dve) if norm else ()))


def segment_sum_phase(nc, g, name):
    big3 = g.big[:].rearrange("p (j f) -> p j f", f=D)
    each = 4
    with phase(nc, name) as ph:
        summed, turned, carried_done, back = (ph.sem(n) for n in ("summed", "turned", "carried", "back"))
        cleared = ph.sem("cleared")
        last, carried = ph.sb("last", [P, D]), ph.sb("carried", [D, P + 1])
        copied, out_done = ph.sem("copied"), ph.sem("out")
        ps = ph.pb("ps", [P, 2, 512])
        with nc.Block() as block:
            @block.vector
            def _(dve):
                with dve.Fori(0, D // each) as f:
                    for k in range(each):
                        column = big3[:, :, bass.ds(f * each + k, 1)].rearrange("p j f -> p (j f)")
                        dve.tensor_tensor_scan(column, g.goes_on[:], column, 0.0, ALU.mult, ALU.add).then_inc(summed, 1)
                dve.memset(carried[:], 0.0).then_inc(cleared, 1)
                dve.wait_ge(summed, D)
                dve.tensor_copy(last[:], big3[:, TILES - 1, :]).then_inc(copied, 1)
                dve.wait_ge(cleared, 1)
                dve.wait_ge(turned, 1)
                dve.tensor_tensor_scan(carried[:, 1:P + 1], g.whole_t[:, 0, :], ps[0:D, 0, 0:P], 0.0, ALU.mult, ALU.add
                                       ).then_inc(carried_done, 1)
                dve.wait_ge(back, 1)
                dve.tensor_copy(g.carry[:], ps[:, 1, 0:D]).then_inc(out_done, 1)

            @block.tensor
            def _(pe):
                pe.wait_ge(copied, 1)
                pe.transpose(ps[0:D, 0, 0:P], last[:], g.ident[:]).then_inc(turned, 1)
                pe.wait_ge(carried_done, 1)
                pe.transpose(ps[:, 1, 0:D], carried[:, 0:P], g.ident[0:D, 0:D]).then_inc(back, 1)


class Gru:

    def __init__(self, nc, g, ph, state, normed, first, summed, logits, mh, hx):
        self.nc, self.g, self.summed, self.logits = nc, g, summed, logits
        self.state_in, self.state_out = state
        self.normed, self.first = normed, first
        sem, sb, pb = ph.sem, ph.sb, ph.pb
        self.carry1, self.carry2, self.total_done, self.low, self.expd = (
            sem(n) for n in ("carry1", "carry2", "total", "low", "expd"))
        self.celu_done, self.turned, self.evacuated, self.gates_done, self.squashed = (
            sem(n) for n in ("celu", "turned_mh", "evacuated_mh", "gates", "squashed"))
        self.reset1, self.reset2, self.cand_done, self.diff_done, self.mixed, self.h_done = (
            sem(n) for n in ("reset1", "reset2", "cand", "diff", "mixed", "h_new"))
        self.sum1, self.mean, self.centred_done, self.squared, self.sum2, self.spread = (
            sem(n) for n in ("sum1", "mean", "centred", "squared", "sum2", "spread"))
        self.power_done, self.scaled, self.turned2, self.evacuated2, self.projected, self.logits_out = (
            sem(n) for n in ("power", "scaled", "turned_x", "evacuated_x", "projected_x", "logits_x"))
        self.filled = sem("filled")
        self.loaded, self.loaded_x, self.h_saved, self.x_saved = (
            [sem(f"{n}{p}") for p in range(2)] for n in ("h_loaded", "hx_loaded", "h_saved", "x_saved"))
        shape = [P, 2, J, D]
        self.mh, self.hx = mh, hx
        self.mht = sb("mht", [P, 2, J, P])
        self.rz = sb("rz", [P, 2, J, 2 * D])
        self.cand, self.diff, self.centred, self.normal = (sb(n, shape) for n in ("cand", "diff", "centred", "normal"))
        if summed:
            self.part, self.total = sb("part", shape), sb("total", shape)
            self.expd_t = sb("expd_t", shape)
        if logits is not None:
            self.nt = sb("nt", [P, 2, Q, P])
        self.small = sb("small", [P, 2, 5, J])
        self.ps_t = pb("ps_t", [P, J // 2, P])
        self.ps_g = pb("ps_g", [P, J, 2 * P])
        if logits is not None:
            self.ps_x, self.ps_l = pb("ps_nx", [P, 512]), pb("ps_nl", [P, 512])

    def sync(self, sp):
        H = J // 2

        def load(i, p, n):
            need(sp, self.turned, 2 * i - 2)
            sp.dma_start(self.mh[:, p, :, D:2 * D], rows(self.state_in, i)).then_inc(self.loaded[p], 16)

        def load_x(i, p, n):
            need(sp, self.diff_done, i - 1)
            sp.dma_start(self.hx[:, p], rows(self.state_in, i)).then_inc(self.loaded_x[p], 16)

        def store_h(i, p, n):
            need(sp, self.h_done, i + 1)
            sp.dma_start(rows(self.state_out, i), self.cand[:, p]).then_inc(self.h_saved[p], 16)

        def store_x(i, p, n):
            need(sp, self.scaled, i + 1)
            sp.dma_start(rows(self.normed, i, self.first), self.normal[:, p]).then_inc(self.x_saved[p], 16)

        return listed((6, store_x), (0, load), (2, load_x), (4, store_h if self.state_out is not None else None))

    def sync_end(self, sp):
        for saved in [self.x_saved] + ([self.h_saved] if self.state_out is not None else []):
            sp.wait_ge(saved[0], 16 * (NB - NB // 2))
            sp.wait_ge(saved[1], 16 * (NB // 2))

    def pool(self, pool):
        g = self.g

        def carries(i, p, n):
            need(pool, self.total_done, i - 1)
            pool.tensor_tensor(self.part[:, p], cols(g.head, i).unsqueeze(2).to_broadcast([P, J, D]),
                               g.carry[:].unsqueeze(1).to_broadcast([P, J, D]), ALU.mult).then_inc(self.carry1, 1)
            need(pool, self.carry1, i + 1)
            pool.tensor_tensor(self.part[:, p], self.part[:, p], g.b[:].unsqueeze(1).to_broadcast([P, J, D]), ALU.add
                               ).then_inc(self.carry2, 1)

        def centre(i, p, n):
            need(pool, self.mean, i + 1)
            need(pool, self.scaled, i - 1)
            pool.tensor_tensor(self.centred[:, p], self.cand[:, p], self.wide(1, p), ALU.subtract
                               ).then_inc(self.centred_done, 1)

        def power(i, p, n):
            need(pool, self.spread, i + 1)
            pool.tensor_tensor(self.small[:, p, 4], self.small[:, p, 3], g.half_power[:], ALU.pow
                               ).then_inc(self.power_done, 1)
            if self.summed:
                need(pool, self.power_done, i + 1)
                self.scale(pool, i, p, n)

        return listed((5, power), (0, carries if self.summed else None), (3, centre if self.summed else None))

    def wide(self, k, p):
        return self.small[:, p, k].unsqueeze(2).to_broadcast([P, J, D])

    def scale(self, eng, i, p, n):
        need(eng, self.x_saved[p], n * 16)
        if self.logits is not None:
            need(eng, self.turned2, i - 1)
        eng.tensor_tensor(self.normal[:, p], self.centred[:, p], self.wide(4, p), ALU.mult).then_inc(self.scaled, 1)

    def vector(self, dve):
        g, H = self.g, J // 2
        cand, diff, small = self.cand, self.diff, self.small

        def total(i, p, n):
            need(dve, self.carry2, i + 1)
            need(dve, self.celu_done, i - 1)
            need(dve, self.expd, i - 1)
            dve.tensor_tensor(self.total[:, p], g.big[:, bass.ds(i * (J * D), J * D)].rearrange("p (j f) -> p j f", f=D),
                              self.part[:, p], ALU.add).then_inc(self.total_done, 1)

        def celu(i, p, n):
            need(dve, self.expd, i + 1)
            need(dve, self.turned, 2 * i - 2)
            dve.scalar_tensor_tensor(self.mh[:, p, :, 0:D], self.total[:, p], 0.0, self.expd_t[:, p], ALU.max, ALU.add
                                     ).then_inc(self.celu_done, 1)

        def reset(i, p, n):
            need(dve, self.h_saved[p], n * 16) if self.state_out is not None else None
            need(dve, self.centred_done, i - 1)
            for h in range(2):
                need(dve, self.squashed, 2 * i + (h + 1))
                at = (slice(None), p, slice(h * H, (h + 1) * H))
                dve.scalar_tensor_tensor(cand[at], self.rz[at][:, :, 0:D], 1.0,
                                         self.ps_g[:, h * H:(h + 1) * H, 3 * D:4 * D], ALU.add, ALU.mult
                                         ).then_inc(self.reset1, 1)
                need(dve, self.reset1, 2 * i + (h + 1))
                dve.scalar_tensor_tensor(cand[at], cand[at], 0.5, self.ps_g[:, h * H:(h + 1) * H, 2 * D:3 * D],
                                         ALU.mult, ALU.add).then_inc(self.reset2, 1)

        def mix(i, p, n):
            need(dve, self.cand_done, i + 1)
            need(dve, self.loaded_x[p], n * 16 + 16)
            need(dve, self.sum2, i - 1)
            dve.tensor_tensor(diff[:, p], self.hx[:, p], cand[:, p], ALU.subtract).then_inc(self.diff_done, 1)
            need(dve, self.diff_done, i + 1)
            dve.scalar_tensor_tensor(diff[:, p], self.rz[:, p, :, D:2 * D], 1.0, diff[:, p], ALU.add, ALU.mult
                                     ).then_inc(self.mixed, 1)
            need(dve, self.mixed, i + 1)
            dve.scalar_tensor_tensor(cand[:, p], diff[:, p], 0.5, cand[:, p], ALU.mult, ALU.add
                                     ).then_inc(self.h_done, 1)
            need(dve, self.h_done, i + 1)
            dve.tensor_reduce(small[:, p, 0], cand[:, p], AX, ALU.add).then_inc(self.sum1, 1)
            need(dve, self.sum1, i + 1)
            dve.tensor_scalar(small[:, p, 1], small[:, p, 0], 1.0 / D, None, ALU.mult).then_inc(self.mean, 1)
            if not self.summed:
                need(dve, self.mean, i + 1)
                dve.tensor_tensor(self.centred[:, p], cand[:, p], self.wide(1, p), ALU.subtract
                                  ).then_inc(self.centred_done, 1)

        def scale(i, p, n):
            need(dve, self.power_done, i + 1)
            self.scale(dve, i, p, n)

        def spread(i, p, n):
            need(dve, self.squared, i + 1)
            dve.tensor_reduce(small[:, p, 2], diff[:, p], AX, ALU.add).then_inc(self.sum2, 1)
            need(dve, self.sum2, i + 1)
            need(dve, self.power_done, i - 1)
            dve.tensor_scalar(small[:, p, 3], small[:, p, 2], 1.0 / D, 1.0e-5, ALU.mult, ALU.add
                              ).then_inc(self.spread, 1)

        def logit_out(i, p, n):
            need(dve, self.projected, i + 1)
            dve.tensor_copy(hcols(self.logits, i), self.ps_l[:, 0:J * HEADS].rearrange("p (t h) -> p t h", h=HEADS)
                            ).then_inc(self.logits_out, 1)

        s = self.summed
        return listed((3, reset), (1, celu if s else None), (0, total if s else None), (5, None if s else scale),
                      (3, mix), (4, spread), (7, logit_out if self.logits is not None else None))

    def vector_start(self, dve):
        for p in range(2):
            dve.tensor_copy(self.mh[:, p, :, 0:D], self.g.m_empty[:].unsqueeze(1).to_broadcast([P, J, D])
                            ).then_inc(self.filled, 1)

    def scalar(self, act):
        H = J // 2

        def exp(i, p, n):
            need(act, self.total_done, i + 1)
            need(act, self.celu_done, i - 1)
            act.activation(self.expd_t[:, p], self.total[:, p], ACT.Relu, scale=-1.0).then_inc(self.low, 1)
            need(act, self.low, i + 1)
            act.activation(self.expd_t[:, p], self.expd_t[:, p], ACT.Exp, scale=-1.0).then_inc(self.expd, 1)

        def evacuate(i, p, n):
            need(act, self.gates_done, 2 * i - 2)
            for h in range(2):
                need(act, self.turned, 2 * i + (h + 1))
                act.activation(self.mht[:, p, h * H:(h + 1) * H], self.ps_t[:], ACT.Copy).then_inc(self.evacuated, 1)

        def squash(i, p, n):
            need(act, self.mixed, i - 1)
            need(act, self.reset1, 2 * i - 2)
            for h in range(2):
                need(act, self.gates_done, 2 * i + (h + 1))
                act.activation(self.rz[:, p, h * H:(h + 1) * H], self.ps_g[:, h * H:(h + 1) * H, 0:2 * D], ACT.Tanh,
                               scale=0.5).then_inc(self.squashed, 1)

        def candidate(i, p, n):
            need(act, self.reset2, 2 * i + 2)
            act.activation(self.cand[:, p], self.cand[:, p], ACT.Tanh).then_inc(self.cand_done, 1)

        def square(i, p, n):
            need(act, self.centred_done, i + 1)
            act.activation(self.diff[:, p], self.centred[:, p], ACT.Square).then_inc(self.squared, 1)

        def evacuate2(i, p, n):
            need(act, self.turned2, i + 1)
            need(act, self.projected, i - 1)
            act.activation(self.nt[:, p].rearrange("p q e -> p (q e)"), self.ps_x[:], ACT.Copy
                           ).then_inc(self.evacuated2, 1)

        return listed((4, square), (6, evacuate2 if self.logits is not None else None), (3, candidate),
                      (0, exp if self.summed else None), (2, squash), (1, evacuate))

    def tensor(self, pe):
        g, H = self.g, J // 2

        def turn(i, p, n):
            if self.summed:
                need(pe, self.celu_done, i + 1)
            need(pe, self.loaded[p], n * 16 + 16)
            for h in range(2):
                need(pe, self.evacuated, 2 * i + h)
                for t in range(H):
                    ins = pe.transpose(self.ps_t[:, t, :], self.mh[:, p, h * H + t, :], g.ident[:])
                ins.then_inc(self.turned, 1)

        def gates(i, p, n):
            for h in range(2):
                need(pe, self.evacuated, 2 * i + (h + 1))
                need(pe, self.reset2, 2 * i + (h - 1))
                need(pe, self.squashed, 2 * i + (h - 1))
                for t in range(h * H, (h + 1) * H):
                    pe.matmul(self.ps_g[:, t, :], self.mht[:, p, t, :], g.wg[:], start=True, stop=False)
                    ins = pe.matmul(self.ps_g[:, t, :], g.ones3[:], g.bias3[:], start=False, stop=True)
                ins.then_inc(self.gates_done, 1)

        def turn2(i, p, n):
            need(pe, self.scaled, i + 1)
            need(pe, self.evacuated2, i)
            for q in range(Q):
                ins = pe.transpose(self.ps_x[:, q * P:(q + 1) * P],
                                   self.normal[:, p, 2 * q:2 * q + 2, :].rearrange("p t d -> p (t d)"), g.ident[:])
            ins.then_inc(self.turned2, 1)

        def project(i, p, n):
            need(pe, self.evacuated2, i + 1)
            need(pe, self.logits_out, i)
            for q in range(Q):
                ins = pe.matmul(self.ps_l[:, q * 2 * HEADS:(q + 1) * 2 * HEADS], self.nt[:, p, q, :],
                                g.w_dst[:].rearrange("p s h -> p (s h)"), start=True, stop=True)
            ins.then_inc(self.projected, 1)

        more = ((6, turn2), (7, project)) if self.logits is not None else ()
        return listed(*more, (2, gates), (1, turn))


def gru_phase(nc, g, name, state, normed, logits):
    with phase(nc, name) as ph:
        mh = g.work[:, 0:4 * J * D].rearrange("p (s j f) -> p s j f", s=2, j=J)
        hx = g.work[:, 4 * J * D:6 * J * D].rearrange("p (s j f) -> p s j f", s=2, j=J)
        gru = Gru(nc, g, ph, state, normed, 0, True, logits, mh, hx)
        with nc.Block() as block:
            @block.sync
            def _(sp):
                interleaved(sp, *gru.sync(sp))
                gru.sync_end(sp)

            @block.gpsimd
            def _(pool):
                interleaved(pool, *gru.pool(pool))

            @block.vector
            def _(dve):
                interleaved(dve, *gru.vector(dve))

            @block.scalar
            def _(act):
                interleaved(act, *gru.scalar(act))

            @block.tensor
            def _(pe):
                interleaved(pe, *gru.tensor(pe))


class Norm:

    def __init__(self, nc, g, ph, x, xc, first, out, again, bufs):
        self.g, self.x, self.xc, self.first, self.out, self.again = g, x, xc, first, out, again
        sem = ph.sem
        self.gained, self.shifted, self.added, self.sum1, self.mean, self.centred = (
            sem(n) for n in ("n_gained", "n_shifted", "n_added", "n_sum1", "n_mean", "n_centred"))
        self.squared, self.sum2, self.spread, self.power, self.scaled = (
            sem(n) for n in ("n_squared", "n_sum2", "n_spread", "n_power", "n_scaled"))
        self.sum1b, self.meanb, self.centredb, self.squaredb, self.sum2b, self.spreadb, self.powerb, self.scaledb = (
            sem(n) for n in ("n_sum1b", "n_meanb", "n_centredb", "n_squaredb", "n_sum2b", "n_spreadb", "n_powerb",
                             "n_scaledb"))
        self.loaded, self.saved, self.savedb = ([sem(f"{n}{p}") for p in range(2)]
                                                for n in ("n_loaded", "n_saved", "n_savedb"))
        shape = [P, 2, J, D]
        self.a, self.b, self.c, self.sq, self.y = (bufs.pop() if bufs else ph.sb(f"n_{k}", shape) for k in "abcsy")
        if again is not None:
            self.c2, self.sq2, self.y2 = (bufs.pop() if bufs else ph.sb(f"n_{k}2", shape) for k in "csy")
        self.small, self.small2 = ph.sb("n_small", [P, 2, 5, J]), ph.sb("n_small2", [P, 2, 5, J])

    def wide(self, small, k, p):
        return small[:, p, k].unsqueeze(2).to_broadcast([P, J, D])

    def sync(self, sp):
        def load(i, p, n):
            need(sp, self.centred, i - 1)
            sp.dma_start(self.a[:, p], rows(self.x, i)).then_inc(self.loaded[p], 16)
            sp.dma_start(self.b[:, p], rows(self.xc, i, self.first)).then_inc(self.loaded[p], 16)

        def store(i, p, n):
            need(sp, self.scaled, i + 1)
            sp.dma_start(rows(self.out, i, self.first), self.y[:, p]).then_inc(self.saved[p], 16)

        def store_b(i, p, n):
            need(sp, self.scaledb, i + 1)
            sp.dma_start(rows(self.again, i), self.y2[:, p]).then_inc(self.savedb[p], 16)

        return listed((0, load), (5, store), (8, store_b if self.again is not None else None))

    def sync_end(self, sp):
        for saved in [self.saved] + ([self.savedb] if self.again is not None else []):
            sp.wait_ge(saved[0], 16 * (NB - NB // 2))
            sp.wait_ge(saved[1], 16 * (NB // 2))

    def pool(self, pool):
        g = self.g

        def gain(i, p, n):
            need(pool, self.loaded[p], n * 32 + 32)
            b = self.b[:, p]
            pool.tensor_tensor(b, b, g.gamma[:].unsqueeze(1).to_broadcast([P, J, D]), ALU.mult).then_inc(self.gained, 1)
            need(pool, self.gained, i + 1)
            pool.tensor_tensor(b, b, g.beta[:].unsqueeze(1).to_broadcast([P, J, D]), ALU.add).then_inc(self.shifted, 1)

        def centre(i, p, n):
            need(pool, self.mean, i + 1)
            need(pool, self.scaled, i - 1)
            pool.tensor_tensor(self.c[:, p], self.a[:, p], self.wide(self.small, 1, p), ALU.subtract
                               ).then_inc(self.centred, 1)

        def scale(i, p, n):
            need(pool, self.spread, i + 1)
            pool.tensor_tensor(self.small[:, p, 4], self.small[:, p, 3], g.half_power[:], ALU.pow).then_inc(self.power, 1)
            need(pool, self.power, i + 1)
            need(pool, self.saved[p], n * 16)
            if self.again is not None:
                need(pool, self.centredb, i - 1)
            pool.tensor_tensor(self.y[:, p], self.c[:, p], self.wide(self.small, 4, p), ALU.mult).then_inc(self.scaled, 1)

        def centre_b(i, p, n):
            need(pool, self.meanb, i + 1)
            need(pool, self.scaledb, i - 1)
            pool.tensor_tensor(self.c2[:, p], self.y[:, p], self.wide(self.small2, 1, p), ALU.subtract
                               ).then_inc(self.centredb, 1)

        def scale_b(i, p, n):
            need(pool, self.spreadb, i + 1)
            pool.tensor_tensor(self.small2[:, p, 4], self.small2[:, p, 3], g.half_power[:], ALU.pow
                               ).then_inc(self.powerb, 1)
            need(pool, self.powerb, i + 1)
            need(pool, self.savedb[p], n * 16)
            pool.tensor_tensor(self.y2[:, p], self.c2[:, p], self.wide(self.small2, 4, p), ALU.mult
                               ).then_inc(self.scaledb, 1)

        more = ((7, scale_b), (5, centre_b)) if self.again is not None else ()
        return listed((4, scale), (2, centre), *more, (1, gain))

    def vector(self, dve):
        def reduce(small, k, source, sem, i, p):
            dve.tensor_reduce(small[:, p, k], source[:, p], AX, ALU.add).then_inc(sem, 1)
            need(dve, sem, i + 1)

        def add(i, p, n):
            need(dve, self.shifted, i + 1)
            dve.tensor_tensor(self.a[:, p], self.a[:, p], self.b[:, p], ALU.add).then_inc(self.added, 1)
            need(dve, self.added, i + 1)
            reduce(self.small, 0, self.a, self.sum1, i, p)
            dve.tensor_scalar(self.small[:, p, 1], self.small[:, p, 0], 1.0 / D, None, ALU.mult).then_inc(self.mean, 1)

        def spread(i, p, n):
            need(dve, self.squared, i + 1)
            reduce(self.small, 2, self.sq, self.sum2, i, p)
            dve.tensor_scalar(self.small[:, p, 3], self.small[:, p, 2], 1.0 / D, 1.0e-5, ALU.mult, ALU.add
                              ).then_inc(self.spread, 1)

        def mean_b(i, p, n):
            need(dve, self.scaled, i + 1)
            reduce(self.small2, 0, self.y, self.sum1b, i, p)
            dve.tensor_scalar(self.small2[:, p, 1], self.small2[:, p, 0], 1.0 / D, None, ALU.mult).then_inc(self.meanb, 1)

        def spread_b(i, p, n):
            need(dve, self.squaredb, i + 1)
            reduce(self.small2, 2, self.sq2, self.sum2b, i, p)
            dve.tensor_scalar(self.small2[:, p, 3], self.small2[:, p, 2], 1.0 / D, 0.25e-5, ALU.mult, ALU.add
                              ).then_inc(self.spreadb, 1)

        more = ((6, spread_b), (5, mean_b)) if self.again is not None else ()
        return listed(*more, (3, spread), (1, add))

    def scalar(self, act):
        def square(i, p, n):
            need(act, self.centred, i + 1)
            need(act, self.sum2, i - 1)
            act.activation(self.sq[:, p], self.c[:, p], ACT.Square).then_inc(self.squared, 1)

        def square_b(i, p, n):
            need(act, self.centredb, i + 1)
            need(act, self.sum2b, i - 1)
            act.activation(self.sq2[:, p], self.c2[:, p], ACT.Square).then_inc(self.squaredb, 1)

        return listed((6, square_b if self.again is not None else None), (3, square))


def norm_phase(nc, g, name, x, xc, first, out):
    with phase(nc, name) as ph:
        norm = Norm(nc, g, ph, x, xc, first, out, None, [])
        with nc.Block() as block:
            @block.sync
            def _(sp):
                interleaved(sp, *norm.sync(sp))
                norm.sync_end(sp)

            @block.gpsimd
            def _(pool):
                interleaved(pool, *norm.pool(pool))

            @block.vector
            def _(dve):
                interleaved(dve, *norm.vector(dve))

            @block.scalar
            def _(act):
                interleaved(act, *norm.scalar(act))


def final_phase(nc, g, x1, node_out):
    with phase(nc, "final") as ph:
        parted, whole, shared, kept, added, sum1, mean, centred, squared, sum2, spread, power, scaled, copied = (
            ph.sem(n) for n in ("parted", "whole", "shared", "kept", "added", "sum1", "mean", "centred", "squared",
                                "sum2", "spread", "power", "scaled", "copied"))
        loaded = [ph.sem(f"loaded{p}") for p in range(2)]
        shape = [P, 2, J, D]
        a, b, c, sq, y = (ph.sb(n, shape) for n in ("a", "b", "c", "sq", "y"))
        small = ph.sb("small", [P, 2, 5, J])
        idx = ph.sb("idx", [P, 2, J], I32)

        def wide(k, p):
            return small[:, p, k].unsqueeze(2).to_broadcast([P, J, D])

        with nc.Block() as block:
            @block.sync
            def _(sp):
                def load(i, p, n):
                    need(sp, centred, i - 1)
                    sp.dma_start(a[:, p], rows(x1, i)).then_inc(loaded[p], 16)

                interleaved(sp, (0, load))

            @block.gpsimd
            def _(pool):
                def power_of(i, p, n):
                    need(pool, spread, i + 1)
                    pool.tensor_tensor(small[:, p, 4], small[:, p, 3], g.half_power[:], ALU.pow).then_inc(power, 1)

                def scatter(i, p, n):
                    need(pool, g.scattered[p], n * P)
                    pool.tensor_copy(idx[:, p, :], cols(g.out_idx, i)).then_inc(copied, 1)
                    need(pool, copied, i + 1)
                    need(pool, scaled, i + 1)
                    for u in range(J):
                        pool.indirect_dma_start(node_out, bass.IndirectOffsetOnAxis(ap=idx[:, p, u:u + 1], axis=0),
                                                y[:, p, u, :], None, bounds_check=N - 1, oob_is_err=False
                                                ).then_inc(g.scattered[p], 16)

                interleaved(pool, (2, power_of), (3, scatter))
                pool.wait_ge(g.scattered[0], P * (NB - NB // 2))
                pool.wait_ge(g.scattered[1], P * (NB // 2))

            @block.vector
            def _(dve):
                def update(i, p, n):
                    dve.tensor_tensor(b[:, p], cols(g.head, i).unsqueeze(2).to_broadcast([P, J, D]),
                                      g.carry[:].unsqueeze(1).to_broadcast([P, J, D]), ALU.mult).then_inc(parted, 1)
                    need(dve, parted, i + 1)
                    dve.tensor_tensor(b[:, p], g.big[:, bass.ds(i * (J * D), J * D)].rearrange("p (j f) -> p j f", f=D),
                                      b[:, p], ALU.add).then_inc(whole, 1)
                    need(dve, whole, i + 1)
                    dve.tensor_tensor(b[:, p], b[:, p], cols(g.share, i).unsqueeze(2).to_broadcast([P, J, D]),
                                      ALU.mult).then_inc(shared, 1)
                    need(dve, shared, i + 1)
                    need(dve, loaded[p], n * 16 + 16)
                    dve.scalar_tensor_tensor(b[:, p], a[:, p], 0.2, b[:, p], ALU.mult, ALU.add).then_inc(kept, 1)
                    need(dve, kept, i + 1)
                    dve.scalar_tensor_tensor(a[:, p], b[:, p], 0.0, a[:, p], ALU.max, ALU.add).then_inc(added, 1)
                    need(dve, added, i + 1)
                    dve.tensor_reduce(small[:, p, 0], a[:, p], AX, ALU.add).then_inc(sum1, 1)
                    need(dve, sum1, i + 1)
                    dve.tensor_scalar(small[:, p, 1], small[:, p, 0], 1.0 / D, None, ALU.mult).then_inc(mean, 1)
                    need(dve, mean, i + 1)
                    dve.tensor_tensor(c[:, p], a[:, p], wide(1, p), ALU.subtract).then_inc(centred, 1)

                def spread_of(i, p, n):
                    need(dve, squared, i + 1)
                    dve.tensor_reduce(small[:, p, 2], sq[:, p], AX, ALU.add).then_inc(sum2, 1)
                    need(dve, sum2, i + 1)
                    dve.tensor_scalar(small[:, p, 3], small[:, p, 2], 1.0 / D, 1.0e-5, ALU.mult, ALU.add
                                      ).then_inc(spread, 1)

                def scale(i, p, n):
                    need(dve, power, i + 1)
                    need(dve, g.scattered[p], n * P)
                    dve.tensor_tensor(y[:, p], c[:, p], wide(4, p), ALU.mult).then_inc(scaled, 1)

                interleaved(dve, (2, scale), (1, spread_of), (0, update))

            @block.scalar
            def _(act):
                def square(i, p, n):
                    need(act, centred, i + 1)
                    need(act, sum2, i - 1)
                    act.activation(sq[:, p], c[:, p], ACT.Square).then_inc(squared, 1)

                interleaved(act, (0, square))


def relation_phase(nc, g, dram, table):
    with phase(nc, "relation") as ph:
        copied, turned, evacuated = ph.sem("idx_copied"), ph.sem("turned"), ph.sem("evacuated")
        multiplied, masked, chosen = ph.sem("multiplied"), ph.sem("masked"), ph.sem("chosen")
        stage_idx = ph.sb("stage_idx", [P, 2, J], I32)
        stage = ph.sb("stage", [P, 2, J, D])
        xt = ph.sb("xt", [P, 2, Q, P])
        mine = ph.sb("mine", [P, 2, RELS, D])
        wr = ph.sb("wr", [P, 2, RELS * D])
        mask = ph.sb("mask", [P, TILES, RELS])
        relf = ph.sb("relf", [P, TILES])
        wr_loaded, rel_done = ph.sem("wr_loaded"), ph.sem("rel_done")
        ps_x, ps_r = ph.pb("ps_x", [P, 2, Q * P]), ph.pb("ps_r", [P, 4, RELS * D])
        done = list(g.gathered_count)
        g.gathered_count[0] += P * (NB - NB // 2)
        g.gathered_count[1] += P * (NB // 2)
        big3 = g.big[:].rearrange("p (j f) -> p j f", f=D)

        with nc.Block() as block:
            @block.gpsimd
            def _(pool):
                def gather(i, p, n):
                    need(pool, g.gathered[p], n * P + done[p])
                    pool.tensor_copy(stage_idx[:, p, :], cols(g.src_slot, i)).then_inc(copied, 1)
                    need(pool, copied, i + 1)
                    need(pool, turned, i - 1)
                    for u in range(J):
                        pool.indirect_dma_start(stage[:, p, u, :], None, table,
                                                bass.IndirectOffsetOnAxis(ap=stage_idx[:, p, u:u + 1], axis=0)
                                                ).then_inc(g.gathered[p], 16)

                pipelined(pool, gather)

            @block.sync
            def _(sp):
                sp.dma_start(wr[:], dram["wr"]).then_inc(wr_loaded, 16)

            @block.tensor
            def _(pe):
                pe.wait_ge(wr_loaded, 16)

                def turn(i, p, n):
                    need(pe, g.gathered[p], n * P + (P + done[p]))
                    need(pe, evacuated, i - 1)
                    for q in range(Q):
                        ins = pe.transpose(ps_x[:, p, q * P:(q + 1) * P], stage[:, p, 2 * q:2 * q + 2, :], g.ident[:])
                    ins.then_inc(turned, 1)

                def multiply(i, p, n):
                    need(pe, evacuated, i + 1)
                    for t in range(J):
                        need(pe, masked, i * J + (t - 3))
                        pe.matmul(ps_r[:, t % 4, :], xt[:, p, t // 2, :], wr[:, t % 2, :], start=True, stop=True
                                  ).then_inc(multiplied, 1)

                pipelined(pe, turn, multiply)

            @block.scalar
            def _(act):
                def evacuate(i, p, n):
                    need(act, turned, i + 1)
                    need(act, multiplied, (i - 1) * J)
                    act.activation(xt[:, p, :, :].rearrange("p q e -> p (q e)"), ps_x[:, p, :], ACT.Copy
                                   ).then_inc(evacuated, 1)

                pipelined(act, evacuate)

            @block.vector
            def _(dve):
                def choose(i, p, n):
                    for t in range(J):
                        need(dve, multiplied, i * J + (t + 1))
                        need(dve, chosen, i * J + (t - 1))
                        here = mask[:, bass.ds(i * J + t, 1), :].rearrange("p j r -> p (j r)")
                        dve.tensor_tensor(mine[:, t % 2], ps_r[:, t % 4, :].rearrange("p (r d) -> p r d", r=RELS),
                                          here.unsqueeze(2).to_broadcast([P, RELS, D]), ALU.mult).then_inc(masked, 1)
                        need(dve, masked, i * J + (t + 1))
                        dve.tensor_reduce(big3[:, bass.ds(i * J + t, 1), :].rearrange("p j f -> p (j f)"),
                                          mine[:, t % 2].rearrange("p r d -> p d r"), AX, ALU.add).then_inc(chosen, 1)

                dve.tensor_copy(relf[:], g.rel[:]).then_inc(rel_done, 1)
                dve.wait_ge(rel_done, 1)
                for r in range(RELS):
                    dve.tensor_scalar(mask[:, :, r], relf[:], float(r), None, ALU.is_equal).then_inc(rel_done, 1)
                dve.wait_ge(rel_done, 1 + RELS)
                pipelined(dve, None, choose)


def position_phase(nc, g, dram):
    with phase(nc, "position") as ph:
        (s_chain, s_iota, s_hi, s_lo, s_count, s_split) = (
            ph.sem(n) for n in ("chain", "iota", "hi", "lo", "count", "split"))
        nlo = ph.sb("nlo", [P, TILES])
        iota_i, iota_f = ph.sb("iota_i", [P, TILES], I32), ph.sb("iota_f", [P, TILES])
        node_i, node_f = ph.sb("node_i", [P, TILES], I32), ph.sb("node_f", [P, TILES])
        hi_i, hi, lo, fix = ph.sb("hi_i", [P, TILES], I32), ph.sb("hi", [P, TILES]), ph.sb("lo", [P, TILES]), ph.sb("fix", [P, TILES])
        hot_hi, hot_lo = ph.sb("hot_hi", [P, 2, J, P], F16), ph.sb("hot_lo", [P, 2, J, TILES], F16)
        ps = ph.pb("ps", [P, 512])
        with nc.Block() as block:
            @block.gpsimd
            def _(pool):
                pool.iota(iota_i[:], [[1, TILES]], base=0, channel_multiplier=0).then_inc(s_iota, 1)
                pool.iota(node_i[:], [[1, TILES]], base=SLOTS, channel_multiplier=TILES).then_inc(s_iota, 1)

            @block.vector
            def _(dve):
                n = [0]

                def link(ins):
                    n[0] += 1
                    ins.then_inc(s_chain, 1)
                    dve.wait_ge(s_chain, n[0])

                dve.wait_ge(s_iota, 2)
                link(dve.tensor_copy(iota_f[:], iota_i[:]))
                link(dve.tensor_copy(g.own_row[:], node_i[:]))
                link(dve.tensor_copy(lo[:], g.dst_idx[:]))
                link(dve.tensor_scalar(hi[:], lo[:], 1.0 / TILES, None, ALU.mult))
                link(dve.tensor_copy(hi_i[:], hi[:]))
                link(dve.tensor_copy(hi[:], hi_i[:]))
                link(dve.scalar_tensor_tensor(lo[:], hi[:], -float(TILES), lo[:], ALU.mult, ALU.add))
                link(dve.tensor_scalar(fix[:], lo[:], 0.0, None, ALU.is_lt))
                link(dve.tensor_tensor(hi[:], hi[:], fix[:], ALU.subtract))
                link(dve.scalar_tensor_tensor(lo[:], fix[:], float(TILES), lo[:], ALU.mult, ALU.add))
                link(dve.tensor_scalar(fix[:], lo[:], float(TILES), None, ALU.is_ge))
                link(dve.tensor_tensor(hi[:], hi[:], fix[:], ALU.add))
                link(dve.scalar_tensor_tensor(lo[:], fix[:], -float(TILES), lo[:], ALU.mult, ALU.add))

                def hot(i, p, k):
                    need(dve, s_count, i - 1)
                    dve.tensor_tensor(hot_hi[:, p], iota_f[:, 0:P].unsqueeze(1).to_broadcast([P, J, P]),
                                      cols(hi, i).unsqueeze(2).to_broadcast([P, J, P]), ALU.is_equal).then_inc(s_hi, 1)
                    dve.tensor_tensor(hot_lo[:, p], iota_f[:].unsqueeze(1).to_broadcast([P, J, TILES]),
                                      cols(lo, i).unsqueeze(2).to_broadcast([P, J, TILES]), ALU.is_equal).then_inc(s_lo, 1)

                pipelined(dve, hot)
                dve.wait_ge(s_count, NB)
                link(dve.tensor_copy(g.count[:], ps[:, 0:TILES]))

            @block.tensor
            def _(pe):
                def count(i, p, k):
                    need(pe, s_hi, i + 1)
                    need(pe, s_lo, i + 1)
                    for t in range(J):
                        edge = isinstance(i, int)
                        ins = pe.matmul(ps[:, 0:TILES], hot_hi[:, p, t, :], hot_lo[:, p, t, :],
                                        start=(edge and i == 0 and t == 0), stop=(edge and i == NB - 1 and t == J - 1),
                                        skip_group_check=True)
                    ins.then_inc(s_count, 1)

                pipelined(pe, count)


def plain_cumulation_phase(nc, g):
    with phase(nc, "cumulate") as ph:
        chain, asked, got, asked2, got2 = (ph.sem(n) for n in ("chain", "asked", "got", "asked2", "got2"))
        ones = ph.sb("ones", [P, TILES])
        cum, has = ph.sb("cum", [P, TILES]), ph.sb("has", [P, TILES])
        last = ph.sb("last", [P, 1])
        carried, carry = ph.sb("carried", [1, P + 1]), ph.sb("carry", [P, 1])
        one1 = ph.sb("one1", [1, 1])
        ps = ph.pb("ps", [P, 2, 512])
        with nc.Block() as block:
            @block.vector
            def _(dve):
                n = [0]

                def link(ins):
                    n[0] += 1
                    ins.then_inc(chain, 1)
                    dve.wait_ge(chain, n[0])

                link(dve.memset(ones[:], 1.0))
                link(dve.memset(one1[:], 1.0))
                link(dve.memset(carried[:], 0.0))
                link(dve.tensor_tensor_scan(cum[:], ones[:], g.count[:], 0.0, ALU.mult, ALU.add))
                dve.tensor_copy(last[:], cum[:, TILES - 1:TILES]).then_inc(asked, 1)
                dve.wait_ge(got, 1)
                dve.tensor_tensor_scan(carried[:, 1:P + 1], ones[0:1, 0:P], ps[0:1, 0, 0:P], 0.0, ALU.mult, ALU.add
                                       ).then_inc(asked2, 1)
                dve.wait_ge(got2, 1)
                link(dve.tensor_copy(carry[:], ps[:, 1, 0:1]))
                link(dve.tensor_scalar(cum[:], cum[:], carry[:, 0:1], -1.0, ALU.add, ALU.add))
                link(dve.tensor_scalar(has[:], g.count[:], 0.0, None, ALU.is_gt))
                link(dve.tensor_tensor(cum[:], cum[:], g.own_row[:], ALU.subtract))
                link(dve.tensor_tensor(cum[:], cum[:], has[:], ALU.mult))
                link(dve.tensor_tensor(g.own_row[:], g.own_row[:], cum[:], ALU.add))

            @block.tensor
            def _(pe):
                pe.wait_ge(asked, 1)
                pe.transpose(ps[0:1, 0, 0:P], last[:], g.ident[:]).then_inc(got, 1)
                pe.wait_ge(asked2, 1)
                pe.wait_ge(chain, 2)
                pe.matmul(ps[:, 1, 0:1], carried[:, 0:P], one1[:], start=True, stop=True).then_inc(got2, 1)


def table_phase(nc, g, x, table):
    with phase(nc, "table") as ph:
        loaded, saved = ([ph.sem(f"{n}{p}") for p in range(2)] for n in ("loaded", "saved"))
        filled, numbered = ph.sem("filled"), ph.sem("numbered")
        a, w = ph.sb("a", [P, 2, J, D]), ph.sb("w", [P, 2, J, D + 1])
        with nc.Block() as block:
            @block.sync
            def _(sp):
                def load(i, p, n):
                    need(sp, filled, i - 1)
                    sp.dma_start(a[:, p], rows(x, i)).then_inc(loaded[p], 16)

                def store(i, p, n):
                    need(sp, filled, i + 1)
                    need(sp, numbered, i + 1)
                    sp.dma_start(rows(table, i), w[:, p]).then_inc(saved[p], 16)

                pipelined(sp, load, None, store)
                sp.wait_ge(saved[0], 16 * (NB - NB // 2))
                sp.wait_ge(saved[1], 16 * (NB // 2))

            @block.vector
            def _(dve):
                def fill(i, p, n):
                    need(dve, loaded[p], n * 16 + 16)
                    need(dve, saved[p], n * 16)
                    dve.tensor_copy(w[:, p, :, 0:D], a[:, p]).then_inc(filled, 1)
                    dve.tensor_copy(w[:, p, :, D], cols(g.own_row, i)).then_inc(numbered, 1)

                pipelined(dve, None, fill)


def weights_phase(nc, g):
    with phase(nc, "weights") as ph:
        chain, multiplied = ph.sem("chain"), ph.sem("multiplied")
        beta = ph.sb("beta", [P, P])
        both = ph.sb("both", [P, HEADS])
        lift = ph.sb("lift", [P, HEADS])
        ps = ph.pb("ps", [P, 2, 512])
        with nc.Block() as block:
            @block.vector
            def _(dve):
                n = [0]

                def link(ins):
                    n[0] += 1
                    ins.then_inc(chain, 1)
                    dve.wait_ge(chain, n[0])

                link(dve.tensor_copy(beta[:], g.beta_col[:].to_broadcast([P, P])))
                link(dve.tensor_tensor(both[:], g.w_src[:, 0, :], g.w_dst[:, 0, :], ALU.add))
                dve.wait_ge(multiplied, 1)
                link(dve.tensor_copy(g.node_bias[:], ps[:, 0, 0:2]))
                link(dve.tensor_copy(lift[:], ps[:, 1, 0:HEADS]))
                link(dve.tensor_tensor(g.l_edge[:], g.l_edge[:], lift[:].unsqueeze(2).to_broadcast([P, HEADS, TILES]),
                                       ALU.add))
                for w in (g.w_src, g.w_dst, g.wn):
                    link(dve.tensor_scalar(w[:], w[:], g.gamma_col[:, 0:1], None, ALU.mult))

            @block.tensor
            def _(pe):
                pe.wait_ge(chain, 2)
                for c in range(2):
                    pe.matmul(ps[:, 0, c:c + 1], g.wn[:, 0, c * P:(c + 1) * P], beta[:, 0:1], start=True, stop=True)
                pe.matmul(ps[:, 1, 0:HEADS], beta[:], both[:], start=True, stop=True).then_inc(multiplied, 1)


def build(nc, dram, out, trace=None):
    with ExitStack() as ctx:
        def sb(name, shape, dtype=F32):
            return ctx.enter_context(nc.sbuf_tensor(name, shape, dtype))

        for k, eng in enumerate((nc.sync, nc.scalar, nc.tensor, nc.vector, nc.gpsimd)):
            TO_GATE[eng.engine] = ctx.enter_context(nc.semaphore(f"passed_{k}"))
        g = Shared()
        g.big = sb("big", [P, TILES * D])
        g.src = sb("src", [P, TILES], I32)
        g.src_slot = sb("src_slot", [P, TILES], I32)
        g.dst_idx = sb("dst_idx", [P, TILES], I32)
        g.out_idx = sb("out_idx", [P, TILES], I32)
        g.goes_on = sb("goes_on", [P, TILES])
        g.not_end = sb("not_end", [P, TILES])
        g.shut = sb("shut", [P, TILES])
        g.is_end = sb("is_end", [P, TILES])
        g.head = sb("head", [P, TILES])
        g.share = sb("share", [P, TILES])
        g.rel = sb("rel", [P, TILES], I32)
        g.l_edge = sb("l_edge", [P, HEADS, TILES])
        g.l_dst = sb("l_dst", [P, HEADS, TILES])
        g.work = sb("work", [P, 3 * HEADS * TILES])
        g.wn = sb("wn", [P, 2, HC])
        g.we = sb("we", [P, 2, HC])
        g.ws = sb("ws", [P, 2, D])
        g.wg = sb("wg", [P, 4 * D])
        g.bias3 = sb("bias3", [3, 4 * D], BF16)
        g.ones3 = sb("ones3", [3, P], BF16)
        g.m_empty = sb("m_empty", [P, D])
        g.node_bias = sb("node_bias", [P, 2])
        g.gamma_col = sb("gamma_col", [P, 1])
        g.beta_col = sb("beta_col", [P, 1])
        g.ident = sb("ident", [P, P])
        g.b = sb("b", [P, D])
        g.gamma = sb("gamma", [P, D])
        g.beta = sb("beta", [P, D])
        g.w_dst = sb("w_dst", [P, 2, HEADS])
        g.w_src = sb("w_src", [P, 2, HEADS])
        g.w_edge = sb("w_edge", [P, J, HEADS])
        g.half_power = sb("half_power", [P, J])
        g.carry = sb("carry", [P, D])
        g.whole64 = sb("whole64", [P, 3, D])
        g.whole_t = sb("whole_t", [D, 3, P])
        g.l_src, g.tmp, g.alpha = (g.work[:, k * HEADS * TILES:(k + 1) * HEADS * TILES].rearrange("p (h j) -> p h j", h=HEADS)
                                   for k in range(3))
        g.count, g.own_row = g.big[:, 0:TILES], g.big[:, TILES:2 * TILES]
        g.gathered = [ctx.enter_context(nc.semaphore(f"gathered{p}")) for p in range(2)]
        g.scattered = [ctx.enter_context(nc.semaphore(f"scattered{p}")) for p in range(2)]
        g.gathered_count = [0, 0]

        def scratch(name, count, width=D):
            return nc.dram_tensor(name, (count, width), F32, kind="ExternalOutput" if trace else "Internal").ap()

        x_slot = scratch("x_slot", SLOTS)
        table0 = scratch("table0", SLOTS, D + 1)
        h_slot = [scratch(f"h_slot{t}", SLOTS) for t in range(2)]
        h_node = [scratch(f"h_node{t}", SLOTS) for t in range(2)]
        tables = [scratch(f"normed{t}", 2 * SLOTS) for t in range(STEPS)]
        x1 = scratch("x1", 2 * SLOTS)

        setup_phase(nc, g, dram)
        position_phase(nc, g, dram)
        plain_cumulation_phase(nc, g)
        table_phase(nc, g, dram["x"], table0)
        edge_logit_phase(nc, g, dram)
        gather_phase(nc, g, "dst", dram["x"][:, :], D, g.dst_idx, g.w_dst, g.l_dst, save=x_slot)
        for t in range(STEPS):
            last = t == STEPS - 1
            nodes = ((h_node[(t - 1) % 2] if t else dram["x"], None if last else h_node[t % 2]), tables[t])
            if t == 0:
                gather_phase(nc, g, "src0", table0[:, :], D + 1, g.src, g.w_src, g.l_src, keep=g.big, pos=g.src_slot,
                             nodes=nodes)
            else:
                gather_phase(nc, g, f"src{t}", tables[t - 1][:, :], D, g.src_slot, g.w_src, g.l_src, keep=g.big,
                             nodes=nodes)
            softmax_phase(nc, g, f"softmax{t}")
            message_phase(nc, g, f"message{t}", dram,
                          (dram["x"], tables[t], SLOTS, x1, out) if last else None)
            if t == 0:
                weights_phase(nc, g)
            segment_sum_phase(nc, g, f"sum{t}")
            gru_phase(nc, g, f"gru{t}", (h_slot[(t - 1) % 2] if t else x_slot, None if last else h_slot[t % 2]),
                      tables[t], None if last else g.l_dst)
        norm_phase(nc, g, "x1", x_slot, tables[STEPS - 1], 0, x1)
        relation_phase(nc, g, dram, x1[:, :])
        degree_phase(nc, g)
        segment_sum_phase(nc, g, "sum_rel")
        final_phase(nc, g, x1, out[:, :])


def kernel(**inputs):
    import numpy as np
    import concourse.bacc as bacc
    from concourse import mybir as mb
    from concourse.bass_utils import run_bass_kernel_spmd as run

    a = {k: np.ascontiguousarray(v) for k, v in inputs.items()}
    pad = SLOTS - N

    def padded(v, fill=0):
        return np.concatenate([v, np.full((pad,) + v.shape[1:], fill, v.dtype)])

    def split(v):
        return np.ascontiguousarray(v.reshape(P, TILES))

    def on_all(v):
        return np.ascontiguousarray(np.broadcast_to(v.reshape(1, -1), (P, v.size)))

    f = np.float32
    dst = padded(a["dst"], N)
    edge = np.array([-1], dst.dtype)
    wn, we, wsum = a["L0_gnn_Wn"], a["L0_gnn_We"], a["L0_gnn_Ws"]
    wn_two = np.zeros((P, 2, HC), f)
    we_two = np.zeros((P, 2, HC), f)
    wr_two = np.zeros((P, 2, RELS * D), f)
    for s in range(2):
        wn_two[s * D:(s + 1) * D, s] = wn
        wr_two[s * D:(s + 1) * D, s] = a["L1_gnn_weight_r"].transpose(1, 0, 2).reshape(D, RELS * D)
        for h in range(HEADS):
            we_two[s * D + h * K:s * D + (h + 1) * K, s, h * D:(h + 1) * D] = we[:, h * D:(h + 1) * D]
    wih, whh = a["L0_gnn_Wih"].T, a["L0_gnn_Whh"].T
    wg = np.zeros((P, 4 * D), f)
    wg[0:D, 0:3 * D] = wih
    wg[D:, 0:2 * D] = whh[:, 0:2 * D]
    wg[D:, 3 * D:] = whh[:, 2 * D:]
    bg = np.zeros((2, 4 * D), f)
    bg[0, 0:3 * D] = a["L0_gnn_bih"]
    bg[1, 0:2 * D] = a["L0_gnn_bhh"][0:2 * D]
    bg[1, 3 * D:] = a["L0_gnn_bhh"][2 * D:]
    wa = a["L0_gnn_Wa"].reshape(HEADS, 3, D).transpose(1, 0, 2).reshape(-1)
    half, eighth = np.zeros((P, 2), f), np.zeros((P, J), f)
    half[np.arange(P), np.arange(P) // D] = 1
    eighth[np.arange(P), np.arange(P) // K] = 1
    gamma_col = np.concatenate([a["L0_gnn_gamma"]] * 2).reshape(P, 1)
    beta_col = np.concatenate([a["L0_gnn_beta"]] * 2).reshape(P, 1)
    arrays = dict(
        gamma_col=gamma_col, beta_col=beta_col,
        x=padded(a["x"]), edge=padded(a["edge_attr_16"]), src=split(padded(a["src"])),
        dst_cur=split(dst), dst_prev=split(np.concatenate([edge, dst[:-1]])), dst_next=split(np.concatenate([dst[1:], edge])),
        rel=split(padded(a["edge_type_8"])), wn_twice=np.concatenate([wn, wn]), we_eight=np.tile(we, (P // K, 1)),
        wa=on_all(wa).reshape(P, 3, HC), half=half, eighth=eighth, wn=wn_two, we=we_two,
        ws=np.ascontiguousarray(wsum.reshape(2, P, D).transpose(1, 0, 2)), wg=wg, bg=bg, wr=wr_two,
        ident=np.eye(P, dtype=f), b=on_all(a["L0_gnn_b"]), gamma=on_all(a["L0_gnn_gamma"]), beta=on_all(a["L0_gnn_beta"]))
    nc = bacc.Bacc("TRN2", target_bir_lowering=False, num_devices=1)
    dram = {n: nc.dram_tensor(f"in_{n}", v.shape, mb.dt.from_np(v.dtype), kind="ExternalInput").ap()
            for n, v in arrays.items()}
    out = nc.dram_tensor("result", (SLOTS, D), F32, kind="ExternalOutput").ap()
    build(nc, dram, out)
    r = run(nc, [{f"in_{n}": v for n, v in arrays.items()}], core_ids=[0])
    return r.results[0]["result"][0:N]
```

```python
from contextlib import ExitStack, contextmanager

import concourse.bass as bass
from concourse import mybir

F32 = mybir.dt.float32
F16 = mybir.dt.float16
BF16 = mybir.dt.bfloat16
I32 = mybir.dt.int32
ALU = mybir.AluOpType
ACT = mybir.ActivationFunctionType
AX = mybir.AxisListType.X

P = 128
N = 50000
D = 64
K = 16
HEADS = 4
HC = HEADS * D
RELS = 8
TILES = -(-N // P) + 1
J = 8
NB = TILES // J
SLOTS = P * TILES
Q = J // 2
BIG = 1.0e30
STEPS = 3
assert TILES % J == 0 and SLOTS >= N

TO_GATE = {}


class Shared:
    pass


class Phase:
    def __init__(self, sem, sb, pb):
        self.sem, self.sb, self.pb = sem, sb, pb


def need(eng, sem, value):
    if isinstance(value, int):
        if value > 0:
            eng.wait_ge(sem, value)
    else:
        eng.wait_ge(sem, value)
        eng.sem_inc(TO_GATE[eng.engine], 1)


def interleaved(eng, *steps):
    depth = 1 + max(lag for lag, _ in steps)

    def at(time, parity, half):
        for lag, program in steps:
            if isinstance(time, int):
                if 0 <= time - lag < NB:
                    program(time - lag, (time - lag) % 2, (time - lag) // 2)
            else:
                program(time - lag, (parity - lag) % 2, half + (parity - lag) // 2)

    first = depth + 1 + (depth + 1) % 2
    pairs = (NB - first) // 2
    for time in range(first):
        at(time, 0, 0)
    with eng.Fori(0, pairs) as it:
        at(it * 2 + first, 0, it + first // 2)
        at(it * 2 + (first + 1), 1, it + first // 2)
    for time in range(first + 2 * pairs, NB + depth - 1):
        at(time, 0, 0)


def pipelined(eng, *stages):
    interleaved(eng, *[(k, f) for k, f in reversed(list(enumerate(stages))) if f is not None])


def listed(*steps):
    return [(lag, program) for lag, program in steps if program is not None]


@contextmanager
def phase(nc, name):
    with ExitStack() as ctx:
        used = []

        def sem(what):
            s = ctx.enter_context(nc.semaphore(f"{name}_{what}"))
            used.append(s)
            return s

        def sb(what, shape, dtype=F32):
            return ctx.enter_context(nc.sbuf_tensor(f"{name}_{what}", shape, dtype))

        def pb(what, shape):
            return ctx.enter_context(nc.psum_tensor(f"{name}_{what}", shape, F32))

        yield Phase(sem, sb, pb)

        with nc.Block() as block:
            @block.gpsimd
            def _(pool):
                for s in used:
                    pool.sem_clear(s)


def rows(table, blk, first=0):
    return table[first:first + SLOTS, :].rearrange("(p j) d -> p j d", p=P)[:, bass.ds(blk * J, J), :]


def cols(t, blk):
    return t[:, bass.ds(blk * J, J)]


def hcols(t, blk):
    return t[:, :, bass.ds(blk * J, J)].rearrange("p h t -> p t h")


def setup_phase(nc, g, dram):
    with phase(nc, "setup") as ph:
        loaded, made, chain, widened = (ph.sem(n) for n in ("loaded", "made", "chain", "widened"))
        prev, cur, nxt = (ph.sb(n, [P, TILES]) for n in ("prev", "cur", "nxt"))
        iprev, icur, inxt = (ph.sb("i" + n, [P, TILES], I32) for n in ("prev", "cur", "nxt"))
        wn, we = ph.sb("wn", [P, HC]), ph.sb("we", [P, HC])
        wa = ph.sb("wa", [P, 3, HC])
        prod = ph.sb("prod", [P, 3, HC])
        w4 = ph.sb("w4", [P, 3, HEADS])
        half, eighth = ph.sb("half", [P, 2]), ph.sb("eighth", [P, J])
        ones = ph.sb("ones", [P, TILES])
        whole = ph.sb("whole", [P, 3, HEADS])
        bg, minus = ph.sb("bg", [2, 4 * D]), ph.sb("minus", [P, 1])
        bias, part = ph.sb("bias", [1, 4 * D]), ph.sb("part", [1, 3, 4 * D], BF16)
        e = ph.sb("e", [P, D])
        exp_asked, exp_done, rows_done, biased, parts_done = (
            ph.sem(n) for n in ("exp_asked", "exp_done", "rows_done", "biased", "parts_done"))
        ones_pair = ph.sb("ones_pair", [2, 1])
        ps_b = ph.pb("ps_b", [1, 4 * D])
        loads = [(icur, dram["dst_cur"]), (iprev, dram["dst_prev"]), (inxt, dram["dst_next"]), (g.src, dram["src"]),
                 (g.rel, dram["rel"]), (wn, dram["wn_twice"]), (we, dram["we_eight"]), (wa, dram["wa"]), (half, dram["half"]),
                 (eighth, dram["eighth"]), (g.wn, dram["wn"]), (g.we, dram["we"]), (g.ws, dram["ws"]), (g.wg, dram["wg"]),
                 (bg, dram["bg"]), (g.gamma_col, dram["gamma_col"]), (g.beta_col, dram["beta_col"]),
                 (g.ident, dram["ident"]), (g.b, dram["b"]), (g.gamma, dram["gamma"]),
                 (g.beta, dram["beta"])]
        ps = ph.pb("ps", [P, 3, P])

        with nc.Block() as block:
            @block.sync
            def _(sp):
                for dst, src in loads:
                    sp.dma_start(dst[:], src).then_inc(loaded, 16)
                sp.wait_ge(loaded, 16 * len(loads))
                sp.wait_ge(parts_done, 1)
                for k in range(3):
                    sp.dma_start(g.bias3[k:k + 1, :], part[:, k, :]).then_inc(rows_done, 16)
                sp.wait_ge(rows_done, 48)

            @block.scalar
            def _(act):
                act.wait_ge(exp_asked, 1)
                act.activation(e[:], e[:], ACT.Exp).then_inc(exp_done, 1)

            @block.vector
            def _(dve):
                n = [0]

                def link(ins):
                    n[0] += 1
                    ins.then_inc(chain, 1)
                    dve.wait_ge(chain, n[0])

                dve.wait_ge(loaded, 16 * len(loads))
                link(dve.memset(ones[:], 1.0))
                link(dve.memset(g.half_power[:], -0.5))
                link(dve.memset(g.ones3[:], 1.0))
                link(dve.memset(g.node_bias[:], 0.0))
                link(dve.tensor_copy(g.dst_idx[:], icur[:]))
                for f, i in ((cur, icur), (prev, iprev), (nxt, inxt)):
                    link(dve.tensor_copy(f[:], i[:]))
                link(dve.tensor_tensor(g.goes_on[:], cur[:], prev[:], ALU.is_equal))
                link(dve.tensor_tensor(g.not_end[:], cur[:], nxt[:], ALU.is_equal))
                link(dve.tensor_scalar(g.shut[:], g.goes_on[:], -1.0, BIG, ALU.add, ALU.mult))
                link(dve.tensor_scalar(g.is_end[:], g.not_end[:], -1.0, 1.0, ALU.mult, ALU.add))
                link(dve.tensor_tensor_scan(g.head[:], g.goes_on[:], ones[:], 1.0, ALU.mult, ALU.mult))
                link(dve.tensor_scalar(prev[:], g.not_end[:], float(1 << 20), None, ALU.mult))
                link(dve.tensor_tensor(cur[:], cur[:], prev[:], ALU.add))
                link(dve.tensor_copy(g.out_idx[:], cur[:]))
                dve.tensor_scalar(e[:], g.b[:], 0.0, None, ALU.min).then_inc(exp_asked, 1)
                dve.wait_ge(exp_done, 1)
                link(dve.scalar_tensor_tensor(g.m_empty[:], g.b[:], 0.0, e[:], ALU.max, ALU.add))
                link(dve.memset(ones_pair[:], 1.0))
                link(dve.memset(minus[:], 0.0))
                dve.memset(minus[0:D, :], -1.0).then_inc(biased, 1)
                dve.wait_ge(biased, 2)
                link(dve.tensor_copy(bias[:], ps_b[:]))
                for k in range(3):
                    link(dve.tensor_copy(part[:, k, :], bias[:]))
                    link(dve.tensor_tensor(bias[:], bias[:], part[:, k, :], ALU.subtract))
                dve.sem_inc(parts_done, 1)
                for k in range(3):
                    link(dve.tensor_tensor(prod[:, k, :], (we if k == 1 else wn)[:], wa[:, k, :], ALU.mult))
                link(dve.tensor_reduce(w4[:], prod[:].rearrange("p k (h c) -> p k h c", h=HEADS), AX, ALU.add))
                for out, k, mask, m in ((g.w_dst, 0, half, 2), (g.w_src, 2, half, 2), (g.w_edge, 1, eighth, J)):
                    link(dve.tensor_tensor(out[:], mask[:].unsqueeze(2).to_broadcast([P, m, HEADS]),
                                           w4[:, k, :].unsqueeze(1).to_broadcast([P, m, HEADS]), ALU.mult))
                link(dve.tensor_reduce(whole[:, 0, 0:1], g.goes_on[:], AX, ALU.min))
                link(dve.tensor_reduce(whole[:, 1, 0:1], g.shut[:], AX, ALU.min))
                link(dve.tensor_reduce(whole[:, 2, 0:1], g.not_end[:], AX, ALU.min))
                for k in range(3):
                    dve.tensor_copy(g.whole64[:, k, :], whole[:, k, 0:1].to_broadcast([P, D])).then_inc(widened, 1)
                dve.wait_ge(made, 1)
                link(dve.tensor_copy(g.whole_t[:], ps[0:D, :, :]))

            @block.tensor
            def _(pe):
                pe.wait_ge(loaded, 16 * len(loads))
                pe.wait_ge(biased, 1)
                pe.matmul(ps_b[:], minus[:], g.wg[:], start=True, stop=False)
                pe.matmul(ps_b[:], ones_pair[:], bg[:], start=False, stop=True).then_inc(biased, 1)
                pe.wait_ge(widened, 3)
                for k in range(3):
                    ins = pe.transpose(ps[0:D, k, :], g.whole64[:, k, :], g.ident[:])
                ins.then_inc(made, 1)


class Beside:

    def pool_start(self, pool):
        pass

    def vector_start(self, dve):
        pass

    def vector_end(self, dve):
        pass

    def sync_end(self, sp):
        pass

    def sync(self, sp):
        return []

    def pool(self, pool):
        return []

    def vector(self, dve):
        return []

    def scalar(self, act):
        return []

    def tensor(self, pe):
        return []


def gather_phase(nc, g, name, table, width, idx, weights, logits, keep=None, save=None, pos=None, nodes=None,
                 beside=()):
    with phase(nc, name) as ph:
        copied, gathered, compact = ph.sem("idx_copied"), g.gathered, ph.sem("compact")
        turned, evacuated, kept = ph.sem("turned"), ph.sem("evacuated"), ph.sem("kept")
        projected, logits_out = ph.sem("projected"), ph.sem("logits_out")
        saved = [ph.sem("saved0"), ph.sem("saved1")]
        pos_out = ph.sem("pos_out")
        stage_idx = ph.sb("stage_idx", [P, 2, J], I32)
        stage = ph.sb("stage", [P, 2, J, width])
        tight = ph.sb("tight", [P, 1, J, D]) if pos is not None else None
        xt = ph.sb("xt", [P, 2, Q, P])
        ps_x, ps_l = ph.pb("ps_x", [P, 1, Q * P]), ph.pb("ps_l", [P, 512])
        done = list(g.gathered_count)
        g.gathered_count[0] += P * (NB - NB // 2)
        g.gathered_count[1] += P * (NB // 2)
        gru = None
        if nodes is not None:
            state, normed = nodes
            spare = 2 * HEADS * TILES - 6 * J * D
            free = g.work[:, HEADS * TILES:HEADS * TILES + 6 * J * D]
            assert spare >= 0
            mh = free[:, 0:4 * J * D].rearrange("p (s j f) -> p s j f", s=2, j=J)
            hx = free[:, 4 * J * D:6 * J * D].rearrange("p (s j f) -> p s j f", s=2, j=J)
            gru = Gru(nc, g, ph, state, normed, SLOTS, False, None, mh, hx)

        others = [gru] if gru else [make(nc, g, ph) for make in beside]

        with nc.Block() as block:
            @block.gpsimd
            def _(pool):
                def gather(i, p, n):
                    need(pool, gathered[p], n * P + done[p])
                    pool.tensor_copy(stage_idx[:, p, :], cols(idx, i)).then_inc(copied, 1)
                    need(pool, copied, i + 1)
                    need(pool, turned if pos is None else pos_out, i - 1)
                    if save is not None:
                        need(pool, saved[p], n * 16)
                    for u in range(J):
                        pool.indirect_dma_start(stage[:, p, u, :], None, table,
                                                bass.IndirectOffsetOnAxis(ap=stage_idx[:, p, u:u + 1], axis=0)
                                                ).then_inc(gathered[p], 16)

                for other in others:
                    other.pool_start(pool)
                interleaved(pool, (0, gather), *[step for other in others for step in other.pool(pool)])

            @block.sync
            def _(sp):
                def store(i, p, n):
                    need(sp, gathered[p], n * P + (P + done[p]))
                    sp.dma_start(rows(save, i), stage[:, p, :, :]).then_inc(saved[p], 16)

                own = [(1, store)] if save is not None else []
                interleaved(sp, *[step for other in others for step in other.sync(sp)], *own)
                if save is not None:
                    sp.wait_ge(saved[0], 16 * (NB - NB // 2))
                    sp.wait_ge(saved[1], 16 * (NB // 2))
                for other in others:
                    other.sync_end(sp)

            @block.tensor
            def _(pe):
                if gru:
                    pe.wait_ge(gru.filled, 2)

                def turn(i, p, n):
                    need(pe, gathered[p], n * P + (P + done[p]))
                    if pos is not None:
                        need(pe, compact, i + 1)
                    need(pe, evacuated, i)
                    rows_in = stage[:, p] if pos is None else tight[:, 0]
                    for q in range(Q):
                        ins = pe.transpose(ps_x[:, 0, q * P:(q + 1) * P], rows_in[:, 2 * q:2 * q + 2, :], g.ident[:])
                    ins.then_inc(turned, 1)

                def project(i, p, n):
                    need(pe, evacuated, i + 1)
                    need(pe, logits_out, i)
                    for q in range(Q):
                        ins = pe.matmul(ps_l[:, q * 2 * HEADS:(q + 1) * 2 * HEADS], xt[:, p, q, :],
                                        weights[:].rearrange("p s h -> p (s h)"), start=True, stop=True)
                    ins.then_inc(projected, 1)

                interleaved(pe, (2, project), (1, turn), *[step for other in others for step in other.tensor(pe)])

            @block.scalar
            def _(act):
                def evacuate(i, p, n):
                    need(act, turned, i + 1)
                    need(act, projected, i - 1)
                    if keep is not None:
                        need(act, kept, i - 1)
                    act.activation(xt[:, p, :, :].rearrange("p q e -> p (q e)"), ps_x[:, 0, :], ACT.Copy
                                   ).then_inc(evacuated, 1)

                interleaved(act, (1, evacuate), *[step for other in others for step in other.scalar(act)])

            @block.vector
            def _(dve):
                for other in others:
                    other.vector_start(dve)

                def tighten(i, p, n):
                    need(dve, gathered[p], n * P + (P + done[p]))
                    need(dve, turned, i)
                    dve.tensor_copy(tight[:, 0], stage[:, p, :, 0:D]).then_inc(compact, 1)
                    need(dve, compact, i + 1)
                    dve.tensor_copy(cols(pos, i), stage[:, p, :, D]).then_inc(pos_out, 1)

                def hold(i, p, n):
                    need(dve, evacuated, i + 1)
                    dve.tensor_copy(keep[:, bass.ds(i * (J * D), J * D)], xt[:, p, :, :].rearrange("p q e -> p (q e)")
                                    ).then_inc(kept, 1)

                def out(i, p, n):
                    need(dve, projected, i + 1)
                    dve.tensor_copy(hcols(logits, i), ps_l[:, 0:J * HEADS].rearrange("p (t h) -> p t h", h=HEADS)
                                    ).then_inc(logits_out, 1)

                interleaved(dve, *listed((1, tighten if pos is not None else None), (3, out),
                                         (2, hold if keep is not None else None)), *[step for other in others for step in other.vector(dve)])
                for other in others:
                    other.vector_end(dve)


def scans_phase(nc, g, name, plan, width, program, exp_wanted):
    with phase(nc, name) as ph:
        chain, ends, ends_out, back = (ph.sem(n) for n in ("chain", "ends_turned", "ends_out", "carry_turned"))
        exp_asked, exp_done = ph.sem("exp_asked"), ph.sem("exp_done")
        last = ph.sb("last", [P, width])
        carried = ph.sb("carried", [width, P + 1])
        carry = ph.sb("carry", [P, width])
        ps_e, ps_c = ph.pb("ps_e", [P, 512]), ph.pb("ps_c", [P, 512])

        with nc.Block() as block:
            @block.tensor
            def _(pe):
                for k, (kind, backward) in enumerate(plan):
                    pe.wait_ge(ends, k + 1)
                    pe.transpose(ps_e[0:width, 0:P], last[:], g.ident[:]).then_inc(ends_out, 1)
                    pe.wait_ge(back, k + 1)
                    into = carried[:, 1:P + 1] if backward else carried[:, 0:P]
                    pe.transpose(ps_c[:, 0:width], into, g.ident[0:width, 0:width]).then_inc(ends_out, 1)

            @block.scalar
            def _(act):
                if exp_wanted:
                    act.wait_ge(exp_asked, 1)
                    act.activation(g.alpha[:], g.alpha[:], ACT.Exp).then_inc(exp_done, 1)

            @block.vector
            def _(dve):
                n, k = [0], [0]

                def link(*instructions):
                    for ins in instructions:
                        n[0] += 1
                        ins.then_inc(chain, 1)
                    dve.wait_ge(chain, n[0])

                def scan(out, data):
                    kind, backward = plan[k[0]]
                    flag = g.not_end if backward else g.shut if kind == "max" else g.goes_on
                    ops = (ALU.add, ALU.max) if kind == "max" else (ALU.mult, ALU.add)
                    low = -BIG if kind == "max" else 0.0
                    turn = slice(None, None, -1) if backward else slice(None)

                    def level(start):
                        link(*[dve.tensor_tensor_scan(out[:, h, turn], flag[:, turn], data[:, h, turn], start(h), *ops)
                               for h in range(width)])

                    level(lambda h: low)
                    end = 0 if backward else TILES - 1
                    dve.tensor_copy(last[:], out[:, :, end]).then_inc(ends, 1)
                    whole = g.whole_t[0:width, 2 if backward else 1 if kind == "max" else 0, :]
                    link(dve.memset(carried[:], low))
                    dve.wait_ge(ends_out, 2 * k[0] + 1)
                    into = carried[:, 0:P] if backward else carried[:, 1:P + 1]
                    dve.tensor_tensor_scan(into[:, turn], whole[:, turn], ps_e[0:width, 0:P][:, turn], low, *ops
                                           ).then_inc(back, 1)
                    dve.wait_ge(ends_out, 2 * k[0] + 2)
                    link(dve.tensor_copy(carry[:], ps_c[:, 0:width]))
                    level(lambda h: carry[:, h:h + 1])
                    k[0] += 1

                def exp():
                    dve.sem_inc(exp_asked, 1)
                    dve.wait_ge(exp_done, 1)

                program(dve, scan, link, exp)


def softmax_phase(nc, g, name):
    ends4 = g.is_end[:].unsqueeze(1).to_broadcast([P, HEADS, TILES])

    def program(dve, scan, link, exp):
        link(dve.tensor_tensor(g.tmp[:], g.l_dst[:], ends4, ALU.mult))
        scan(g.alpha, g.tmp)
        link(dve.tensor_tensor(g.alpha[:], g.alpha[:], g.l_edge[:], ALU.add))
        link(dve.tensor_tensor(g.alpha[:], g.alpha[:], g.l_src[:], ALU.add))
        link(dve.scalar_tensor_tensor(g.alpha[:], g.alpha[:], 0.2, g.alpha[:], ALU.mult, ALU.max))
        scan(g.tmp, g.alpha)
        link(dve.tensor_tensor(g.tmp[:], g.tmp[:], ends4, ALU.mult))
        scan(g.l_dst, g.tmp)
        link(dve.tensor_tensor(g.alpha[:], g.alpha[:], g.l_dst[:], ALU.subtract))
        exp()
        scan(g.tmp, g.alpha)
        link(dve.tensor_tensor(g.tmp[:], g.tmp[:], ends4, ALU.mult))
        scan(g.l_dst, g.tmp)
        link(dve.tensor_scalar(g.l_dst[:], g.l_dst[:], 1.0e-16, None, ALU.add))
        link(dve.reciprocal(g.l_dst[:], g.l_dst[:]))
        link(dve.tensor_tensor(g.alpha[:], g.alpha[:], g.l_dst[:], ALU.mult))

    plan = [("sum", True), ("max", False), ("sum", True), ("sum", False), ("sum", True)]
    scans_phase(nc, g, name, plan, HEADS, program, True)


def degree_phase(nc, g):
    def program(dve, scan, link, exp):
        link(dve.memset(g.tmp[:, 0:1, :], 1.0))
        scan(g.l_dst[:, 0:1, :], g.tmp[:, 0:1, :])
        link(dve.reciprocal(g.tmp[:, 0, :], g.l_dst[:, 0, :]))
        link(dve.tensor_scalar(g.share[:], g.tmp[:, 0, :], 0.8, None, ALU.mult))

    scans_phase(nc, g, "degree", [("sum", False)], 1, program, False)


def message_phase(nc, g, name, dram, norm_of=None):
    with phase(nc, name) as ph:
        loaded = [ph.sem("loaded0"), ph.sem("loaded1")]
        weighted, turned, evacuated = ph.sem("weighted"), ph.sem("turned"), ph.sem("evacuated")
        node_done, edge_done, node_out, joined = (ph.sem(n) for n in ("node_done", "edge_done", "node_out", "joined"))
        folded, out_done = ph.sem("folded"), ph.sem("out")
        ea = ph.sb("ea", [P, 2, J, K])
        u = ph.sb("u", [P, 2, J, HEADS, K])
        ut = ph.sb("ut", [P, 2, Q * P])
        node = ph.sb("node", [P, 2, Q * P])
        msg = ph.sb("msg", [P, 2, 4, Q * P])
        ps_u, ps_n = ph.pb("ps_u", [P, 2, 512]), ph.pb("ps_n", [P, 2, 512])
        ps_e, ps_m = ph.pb("ps_e", [P, 2, 512]), ph.pb("ps_m", [P, 2, 512])
        norm = None
        if norm_of is not None:
            free = [g.work[:, k * 2 * J * D:(k + 1) * 2 * J * D].rearrange("p (s j f) -> p s j f", s=2, j=J)
                    for k in range(2 * HEADS * TILES // (2 * J * D))]
            norm = Norm(nc, g, ph, *norm_of, free)
        units = [(par, c) for par in range(2) for c in range(2)]

        with nc.Block() as block:
            @block.sync
            def _(sp):
                def load(i, p, n):
                    need(sp, weighted, i - 1)
                    sp.dma_start(ea[:, p, :, :], rows(dram["edge"], i)).then_inc(loaded[p], 16)

                interleaved(sp, (0, load), *(norm.sync(sp) if norm else ()))
                if norm:
                    norm.sync_end(sp)

            @block.gpsimd
            def _(pool):
                if norm:
                    interleaved(pool, *norm.pool(pool))

            @block.tensor
            def _(pe):
                def turn(i, p, n):
                    need(pe, weighted, i + 1)
                    need(pe, evacuated, i - 1)
                    for q in range(Q):
                        ins = pe.transpose(ps_u[:, p, q * P:(q + 1) * P],
                                           u[:, p, 2 * q:2 * q + 2, :, :].rearrange("p t h k -> p (t h k)"), g.ident[:])
                    ins.then_inc(turned, 1)

                def products(i, p, half):
                    for k in (2 * half, 2 * half + 1):
                        par, c = units[k]
                        need(pe, node_out, i * 4 + (k - 1))
                        pe.matmul(ps_n[:, k % 2, :], g.wn[:, par, c * P:(c + 1) * P],
                                  g.big[:, bass.ds(i * (J * D), J * D)], start=True, stop=True).then_inc(node_done, 1)
                        need(pe, joined, i * 4 + (k - 1))
                        pe.matmul(ps_e[:, k % 2, :], g.we[:, par, c * P:(c + 1) * P], ut[:, p, :],
                                  start=True, stop=True).then_inc(edge_done, 1)

                def products_a(i, p, n):
                    need(pe, evacuated, i + 1)
                    products(i, p, 0)

                def products_b(i, p, n):
                    products(i, p, 1)

                def fold(i, p, n):
                    need(pe, joined, i * 4 + 4)
                    need(pe, out_done, i - 1)
                    for t in range(J):
                        for c in range(2):
                            ins = pe.matmul(ps_m[:, p, t * D:(t + 1) * D],
                                            msg[:, p, 2 * (t % 2) + c, (t // 2) * P:(t // 2 + 1) * P], g.ws[:, c, :],
                                            start=(c == 0), stop=(c == 1))
                    ins.then_inc(folded, 1)

                interleaved(pe, (2, products_a), (3, fold), (1, turn), (2, products_b))

            @block.scalar
            def _(act):
                def evacuate(i, p, n):
                    need(act, turned, i + 1)
                    need(act, edge_done, i * 4 - 4)
                    act.activation(ut[:, p, :], ps_u[:, p, :], ACT.Copy).then_inc(evacuated, 1)

                def node_part(i, p, half):
                    for k in (2 * half, 2 * half + 1):
                        need(act, node_done, i * 4 + (k + 1))
                        need(act, joined, i * 4 + (k - 1))
                        act.activation(node[:, k % 2, :], ps_n[:, k % 2, :], ACT.Identity,
                                       bias=g.node_bias[:, k % 2:k % 2 + 1]).then_inc(node_out, 1)

                def node_part_a(i, p, n):
                    node_part(i, p, 0)

                def node_part_b(i, p, n):
                    node_part(i, p, 1)

                interleaved(act, *(norm.scalar_first(act) if norm else ()), (2, node_part_a), (1, evacuate), (2, node_part_b), *(norm.scalar(act) if norm else ()))

            @block.vector
            def _(dve):
                def weigh(i, p, n):
                    need(dve, loaded[p], n * 16 + 16)
                    need(dve, turned, i - 1)
                    dve.tensor_tensor(u[:, p, :, :, :], hcols(g.alpha, i).unsqueeze(3).to_broadcast([P, J, HEADS, K]),
                                      ea[:, p, :, :].unsqueeze(2).to_broadcast([P, J, HEADS, K]), ALU.mult
                                      ).then_inc(weighted, 1)

                def join(i, p, half):
                    for k in (2 * half, 2 * half + 1):
                        need(dve, node_out, i * 4 + (k + 1))
                        need(dve, edge_done, i * 4 + (k + 1))
                        dve.tensor_tensor(msg[:, p, k, :], ps_e[:, k % 2, :], node[:, k % 2, :], ALU.mult
                                          ).then_inc(joined, 1)

                def join_a(i, p, n):
                    need(dve, folded, i - 1)
                    join(i, p, 0)

                def join_b(i, p, n):
                    join(i, p, 1)

                def out(i, p, n):
                    need(dve, folded, i + 1)
                    dve.tensor_copy(g.big[:, bass.ds(i * (J * D), J * D)], ps_m[:, p, :]).then_inc(out_done, 1)

                interleaved(dve, *(norm.vector_first(dve) if norm else ()), (2, join_a), (3, out), (2, join_b), (0, weigh), *(norm.vector(dve) if norm else ()))


def segment_sum_phase(nc, g, name):
    big3 = g.big[:].rearrange("p (j f) -> p j f", f=D)
    each = 4
    with phase(nc, name) as ph:
        summed, turned, carried_done, back = (ph.sem(n) for n in ("summed", "turned", "carried", "back"))
        cleared = ph.sem("cleared")
        last, carried = ph.sb("last", [P, D]), ph.sb("carried", [D, P + 1])
        copied, out_done = ph.sem("copied"), ph.sem("out")
        ps = ph.pb("ps", [P, 2, 512])
        with nc.Block() as block:
            @block.vector
            def _(dve):
                with dve.Fori(0, D // each) as f:
                    for k in range(each):
                        column = big3[:, :, bass.ds(f * each + k, 1)].rearrange("p j f -> p (j f)")
                        dve.tensor_tensor_scan(column, g.goes_on[:], column, 0.0, ALU.mult, ALU.add).then_inc(summed, 1)
                dve.memset(carried[:], 0.0).then_inc(cleared, 1)
                dve.wait_ge(summed, D)
                dve.tensor_copy(last[:], big3[:, TILES - 1, :]).then_inc(copied, 1)
                dve.wait_ge(cleared, 1)
                dve.wait_ge(turned, 1)
                dve.tensor_tensor_scan(carried[:, 1:P + 1], g.whole_t[:, 0, :], ps[0:D, 0, 0:P], 0.0, ALU.mult, ALU.add
                                       ).then_inc(carried_done, 1)
                dve.wait_ge(back, 1)
                dve.tensor_copy(g.carry[:], ps[:, 1, 0:D]).then_inc(out_done, 1)

            @block.tensor
            def _(pe):
                pe.wait_ge(copied, 1)
                pe.transpose(ps[0:D, 0, 0:P], last[:], g.ident[:]).then_inc(turned, 1)
                pe.wait_ge(carried_done, 1)
                pe.transpose(ps[:, 1, 0:D], carried[:, 0:P], g.ident[0:D, 0:D]).then_inc(back, 1)


class Gru(Beside):

    def __init__(self, nc, g, ph, state, normed, first, summed, logits, mh, hx):
        self.gained, self.between, self.between_dve = None, (), ()
        self.nc, self.g, self.summed, self.logits = nc, g, summed, logits
        self.state_in, self.state_out = state
        self.normed, self.first = normed, first
        sem, sb, pb = ph.sem, ph.sb, ph.pb
        self.carry1, self.carry2, self.total_done, self.low, self.expd = (
            sem(n) for n in ("carry1", "carry2", "total", "low", "expd"))
        self.celu_done, self.turned, self.evacuated, self.gates_done, self.squashed = (
            sem(n) for n in ("celu", "turned_mh", "evacuated_mh", "gates", "squashed"))
        self.reset1, self.reset2, self.cand_done, self.diff_done, self.mixed, self.h_done = (
            sem(n) for n in ("reset1", "reset2", "cand", "diff", "mixed", "h_new"))
        self.sum1, self.mean, self.centred_done, self.squared, self.sum2, self.spread = (
            sem(n) for n in ("sum1", "mean", "centred", "squared", "sum2", "spread"))
        self.power_done, self.scaled, self.turned2, self.evacuated2, self.projected, self.logits_out = (
            sem(n) for n in ("power", "scaled", "turned_x", "evacuated_x", "projected_x", "logits_x"))
        self.filled = sem("filled")
        self.loaded, self.loaded_x, self.h_saved, self.x_saved = (
            [sem(f"{n}{p}") for p in range(2)] for n in ("h_loaded", "hx_loaded", "h_saved", "x_saved"))
        shape = [P, 2, J, D]
        self.mh, self.hx = mh, hx
        self.mht = sb("mht", [P, 2, J, P])
        self.rz = sb("rz", [P, 2, J, 2 * D])
        self.cand, self.diff, self.centred, self.normal = (sb(n, shape) for n in ("cand", "diff", "centred", "normal"))
        if summed:
            self.part, self.total = sb("part", shape), sb("total", shape)
            self.expd_t = sb("expd_t", shape)
        if logits is not None:
            self.nt = sb("nt", [P, 2, Q, P])
        self.small = sb("small", [P, 2, 5, J])
        self.ps_t = pb("ps_t", [P, J // 2, P])
        self.ps_g = pb("ps_g", [P, J, 2 * P])
        if logits is not None:
            self.ps_x, self.ps_l = pb("ps_nx", [P, 512]), pb("ps_nl", [P, 512])

    def sync(self, sp):
        H = J // 2

        def load(i, p, n):
            need(sp, self.turned, 2 * i - 2)
            sp.dma_start(self.mh[:, p, :, D:2 * D], rows(self.state_in, i)).then_inc(self.loaded[p], 16)

        def load_x(i, p, n):
            need(sp, self.diff_done, i - 1)
            sp.dma_start(self.hx[:, p], rows(self.state_in, i)).then_inc(self.loaded_x[p], 16)

        def store_h(i, p, n):
            need(sp, self.h_done, i + 1)
            sp.dma_start(rows(self.state_out, i), self.cand[:, p]).then_inc(self.h_saved[p], 16)

        def store_x(i, p, n):
            need(sp, self.scaled, i + 1)
            sp.dma_start(rows(self.normed, i, self.first), self.normal[:, p]).then_inc(self.x_saved[p], 16)

        return listed((6, store_x if self.normed is not None else None), (0, load), (2, load_x), (4, store_h if self.state_out is not None else None))

    def sync_end(self, sp):
        for saved in ([self.x_saved] if self.normed is not None else []) + ([self.h_saved] if self.state_out is not None else []):
            sp.wait_ge(saved[0], 16 * (NB - NB // 2))
            sp.wait_ge(saved[1], 16 * (NB // 2))

    def pool(self, pool):
        g = self.g

        def carries(i, p, n):
            need(pool, self.total_done, i - 1)
            pool.tensor_tensor(self.part[:, p], cols(g.head, i).unsqueeze(2).to_broadcast([P, J, D]),
                               g.carry[:].unsqueeze(1).to_broadcast([P, J, D]), ALU.mult).then_inc(self.carry1, 1)
            need(pool, self.carry1, i + 1)
            pool.tensor_tensor(self.part[:, p], self.part[:, p], g.b[:].unsqueeze(1).to_broadcast([P, J, D]), ALU.add
                               ).then_inc(self.carry2, 1)

        def centre(i, p, n):
            need(pool, self.mean, i + 1)
            need(pool, self.scaled, i - 1)
            pool.tensor_tensor(self.centred[:, p], self.cand[:, p], self.wide(1, p), ALU.subtract
                               ).then_inc(self.centred_done, 1)

        def power(i, p, n):
            need(pool, self.spread, i + 1)
            pool.tensor_tensor(self.small[:, p, 4], self.small[:, p, 3], g.half_power[:], ALU.pow
                               ).then_inc(self.power_done, 1)
            if self.summed:
                need(pool, self.power_done, i + 1)
                self.scale(pool, i, p, n)

        return listed((0, carries), (6, power), *self.between, (4, centre)) if self.summed else listed((5, power))

    def wide(self, k, p):
        return self.small[:, p, k].unsqueeze(2).to_broadcast([P, J, D])

    def scale(self, eng, i, p, n):
        if self.normed is not None:
            need(eng, self.x_saved[p], n * 16)
        if self.gained is not None:
            need(eng, self.gained, i - 1)
        if self.logits is not None:
            need(eng, self.turned2, i - 1)
        eng.tensor_tensor(self.normal[:, p], self.centred[:, p], self.wide(4, p), ALU.mult).then_inc(self.scaled, 1)

    def vector(self, dve):
        g, H = self.g, J // 2
        cand, diff, small = self.cand, self.diff, self.small

        def total(i, p, n):
            need(dve, self.carry2, i + 1)
            need(dve, self.celu_done, i - 1)
            dve.tensor_tensor(self.total[:, p], g.big[:, bass.ds(i * (J * D), J * D)].rearrange("p (j f) -> p j f", f=D),
                              self.part[:, p], ALU.add).then_inc(self.total_done, 1)

        def celu(i, p, n):
            need(dve, self.expd, i + 1)
            need(dve, self.turned, 2 * i - 2)
            dve.scalar_tensor_tensor(self.mh[:, p, :, 0:D], self.total[:, p], 0.0, self.expd_t[:, p], ALU.max, ALU.add
                                     ).then_inc(self.celu_done, 1)

        def reset(i, p, n):
            need(dve, self.h_saved[p], n * 16) if self.state_out is not None else None
            need(dve, self.centred_done, i - 1)
            for h in range(2):
                need(dve, self.squashed, 2 * i + (h + 1))
                at = (slice(None), p, slice(h * H, (h + 1) * H))
                dve.scalar_tensor_tensor(cand[at], self.rz[at][:, :, 0:D], 1.0,
                                         self.ps_g[:, h * H:(h + 1) * H, 3 * D:4 * D], ALU.add, ALU.mult
                                         ).then_inc(self.reset1, 1)
                need(dve, self.reset1, 2 * i + (h + 1))
                dve.scalar_tensor_tensor(cand[at], cand[at], 0.5, self.ps_g[:, h * H:(h + 1) * H, 2 * D:3 * D],
                                         ALU.mult, ALU.add).then_inc(self.reset2, 1)

        def mix(i, p, n):
            need(dve, self.cand_done, i + 1)
            need(dve, self.loaded_x[p], n * 16 + 16)
            need(dve, self.sum2, i - 1)
            dve.tensor_tensor(diff[:, p], self.hx[:, p], cand[:, p], ALU.subtract).then_inc(self.diff_done, 1)
            need(dve, self.diff_done, i + 1)
            dve.scalar_tensor_tensor(diff[:, p], self.rz[:, p, :, D:2 * D], 1.0, diff[:, p], ALU.add, ALU.mult
                                     ).then_inc(self.mixed, 1)
            need(dve, self.mixed, i + 1)
            dve.scalar_tensor_tensor(cand[:, p], diff[:, p], 0.5, cand[:, p], ALU.mult, ALU.add
                                     ).then_inc(self.h_done, 1)
            need(dve, self.h_done, i + 1)
            dve.tensor_reduce(small[:, p, 0], cand[:, p], AX, ALU.add).then_inc(self.sum1, 1)
            need(dve, self.sum1, i + 1)
            if self.summed:
                dve.tensor_scalar(small[:, p, 1], small[:, p, 0], 1.0 / D, None, ALU.mult).then_inc(self.mean, 1)
            else:
                dve.scalar_tensor_tensor(self.centred[:, p], self.wide(0, p), -1.0 / D, cand[:, p], ALU.mult, ALU.add
                                         ).then_inc(self.centred_done, 1)

        def scale(i, p, n):
            need(dve, self.power_done, i + 1)
            self.scale(dve, i, p, n)

        def spread(i, p, n):
            need(dve, self.squared, i + 1)
            dve.tensor_reduce(small[:, p, 2], diff[:, p], AX, ALU.add).then_inc(self.sum2, 1)
            need(dve, self.sum2, i + 1)
            need(dve, self.power_done, i - 1)
            dve.tensor_scalar(small[:, p, 3], small[:, p, 2], 1.0 / D, 1.0e-5, ALU.mult, ALU.add
                              ).then_inc(self.spread, 1)

        def logit_out(i, p, n):
            need(dve, self.projected, i + 1)
            dve.tensor_copy(hcols(self.logits, i), self.ps_l[:, 0:J * HEADS].rearrange("p (t h) -> p t h", h=HEADS)
                            ).then_inc(self.logits_out, 1)

        s = self.summed
        return listed((1, celu if s else None), (3, reset), *self.between_dve, (0, total if s else None), (5, None if s else scale),
                      (3, mix), (4, spread), (7, logit_out if self.logits is not None else None))

    def vector_start(self, dve):
        for p in range(2):
            dve.tensor_copy(self.mh[:, p, :, 0:D], self.g.m_empty[:].unsqueeze(1).to_broadcast([P, J, D])
                            ).then_inc(self.filled, 1)

    def scalar(self, act):
        H = J // 2

        def exp(i, p, n):
            need(act, self.total_done, i + 1)
            act.activation(self.expd_t[:, p], self.total[:, p], ACT.Relu, scale=-1.0).then_inc(self.low, 1)
            need(act, self.low, i + 1)
            act.activation(self.expd_t[:, p], self.expd_t[:, p], ACT.Exp, scale=-1.0).then_inc(self.expd, 1)

        def evacuate(i, p, h):
            need(act, self.turned, 2 * i + (h + 1))
            act.activation(self.mht[:, p, h * H:(h + 1) * H], self.ps_t[:], ACT.Copy).then_inc(self.evacuated, 1)

        def evacuate_a(i, p, n):
            need(act, self.gates_done, 2 * i - 2)
            evacuate(i, p, 0)

        def evacuate_b(i, p, n):
            evacuate(i, p, 1)

        def squash(i, p, h):
            need(act, self.gates_done, 2 * i + (h + 1))
            act.activation(self.rz[:, p, h * H:(h + 1) * H], self.ps_g[:, h * H:(h + 1) * H, 0:2 * D], ACT.Tanh,
                           scale=0.5).then_inc(self.squashed, 1)

        def squash_a(i, p, n):
            need(act, self.mixed, i - 1)
            squash(i, p, 0)

        def squash_b(i, p, n):
            squash(i, p, 1)

        def candidate(i, p, n):
            need(act, self.reset2, 2 * i + 2)
            act.activation(self.cand[:, p], self.cand[:, p], ACT.Tanh).then_inc(self.cand_done, 1)

        def square(i, p, n):
            need(act, self.centred_done, i + 1)
            act.activation(self.diff[:, p], self.centred[:, p], ACT.Square).then_inc(self.squared, 1)

        def evacuate2(i, p, n):
            need(act, self.turned2, i + 1)
            need(act, self.projected, i - 1)
            act.activation(self.nt[:, p].rearrange("p q e -> p (q e)"), self.ps_x[:], ACT.Copy
                           ).then_inc(self.evacuated2, 1)

        return listed((4, square), (1, evacuate_a), (6, evacuate2 if self.logits is not None else None),
                      (3, candidate), (2, squash_a), (0, exp if self.summed else None), (1, evacuate_b), (2, squash_b))

    def tensor(self, pe):
        g, H = self.g, J // 2

        def turn(i, p, h):
            need(pe, self.evacuated, 2 * i + h)
            for t in range(H):
                ins = pe.transpose(self.ps_t[:, t, :], self.mh[:, p, h * H + t, :], g.ident[:])
            ins.then_inc(self.turned, 1)

        def turn_a(i, p, n):
            if self.summed:
                need(pe, self.celu_done, i + 1)
            need(pe, self.loaded[p], n * 16 + 16)
            turn(i, p, 0)

        def turn_b(i, p, n):
            turn(i, p, 1)

        def gates(i, p, h):
            need(pe, self.evacuated, 2 * i + (h + 1))
            need(pe, self.reset2, 2 * i + (h - 1))
            for t in range(h * H, (h + 1) * H):
                pe.matmul(self.ps_g[:, t, :], self.mht[:, p, t, :], g.wg[:], start=True, stop=False)
                ins = pe.matmul(self.ps_g[:, t, :], g.ones3[:], g.bias3[:], start=False, stop=True)
            ins.then_inc(self.gates_done, 1)

        def gates_a(i, p, n):
            gates(i, p, 0)

        def gates_b(i, p, n):
            gates(i, p, 1)

        def turn2(i, p, n):
            need(pe, self.scaled, i + 1)
            need(pe, self.evacuated2, i)
            for q in range(Q):
                ins = pe.transpose(self.ps_x[:, q * P:(q + 1) * P],
                                   self.normal[:, p, 2 * q:2 * q + 2, :].rearrange("p t d -> p (t d)"), g.ident[:])
            ins.then_inc(self.turned2, 1)

        def project(i, p, n):
            need(pe, self.evacuated2, i + 1)
            need(pe, self.logits_out, i)
            for q in range(Q):
                ins = pe.matmul(self.ps_l[:, q * 2 * HEADS:(q + 1) * 2 * HEADS], self.nt[:, p, q, :],
                                g.w_dst[:].rearrange("p s h -> p (s h)"), start=True, stop=True)
            ins.then_inc(self.projected, 1)

        more = ((6, turn2), (7, project)) if self.logits is not None else ()
        return listed(*more, (1, turn_a), (2, gates_a), (1, turn_b), (2, gates_b))


class FirstNorm(Beside):

    def __init__(self, g, ph, gru, x, out, bufs):
        self.g, self.gru, self.x, self.out = g, gru, x, out
        self.loaded, self.saved = ([ph.sem(f"{n}{p}") for p in range(2)] for n in ("n_loaded", "n_saved"))
        self.shifted, self.gained, self.added, self.sum1, self.centred = (
            ph.sem(n) for n in ("n_shifted", "n_gained", "n_added", "n_sum1", "n_centred"))
        self.squared, self.sum2, self.spread, self.power, self.scaled = (
            ph.sem(n) for n in ("n_squared", "n_sum2", "n_spread", "n_power", "n_scaled"))
        self.xb, self.a, self.sq, self.y = (bufs.pop() if bufs else ph.sb(f"n_{k}", [P, 2, J, D]) for k in "xasy")
        self.small = ph.sb("n_small", [P, 2, 5, J])
        gru.gained = self.gained

    def wide(self, k, p):
        return self.small[:, p, k].unsqueeze(2).to_broadcast([P, J, D])

    def sync(self, sp):
        def load(i, p, n):
            need(sp, self.added, i - 1)
            sp.dma_start(self.xb[:, p], rows(self.x, i)).then_inc(self.loaded[p], 16)

        def store(i, p, n):
            need(sp, self.scaled, i + 1)
            sp.dma_start(rows(self.out, i), self.y[:, p]).then_inc(self.saved[p], 16)

        return [(9, store), (5, load)]

    def sync_end(self, sp):
        sp.wait_ge(self.saved[0], 16 * (NB - NB // 2))
        sp.wait_ge(self.saved[1], 16 * (NB // 2))

    def pool_between(self, pool):
        def power(i, p, n):
            need(pool, self.spread, i + 1)
            pool.tensor_tensor(self.small[:, p, 4], self.small[:, p, 3], self.g.half_power[:], ALU.pow
                               ).then_inc(self.power, 1)

        return [(9, power)]

    def pool(self, pool):
        def shift(i, p, n):
            need(pool, self.loaded[p], n * 16 + 16)
            pool.tensor_tensor(self.xb[:, p], self.xb[:, p], self.g.beta[:].unsqueeze(1).to_broadcast([P, J, D]), ALU.add
                               ).then_inc(self.shifted, 1)

        return [(6, shift)]

    def vector(self, dve):
        small = self.small

        def gain(i, p, n):
            need(dve, self.gru.scaled, i + 1)
            need(dve, self.scaled, i - 1)
            dve.tensor_tensor(self.a[:, p], self.gru.normal[:, p], self.g.gamma[:].unsqueeze(1).to_broadcast([P, J, D]),
                              ALU.mult).then_inc(self.gained, 1)
            need(dve, self.gained, i + 1)
            need(dve, self.shifted, i + 1)
            dve.tensor_tensor(self.a[:, p], self.a[:, p], self.xb[:, p], ALU.add).then_inc(self.added, 1)
            need(dve, self.added, i + 1)
            dve.tensor_reduce(small[:, p, 0], self.a[:, p], AX, ALU.add).then_inc(self.sum1, 1)
            need(dve, self.sum1, i + 1)
            dve.scalar_tensor_tensor(self.a[:, p], self.wide(0, p), -1.0 / D, self.a[:, p], ALU.mult, ALU.add
                                     ).then_inc(self.centred, 1)

        def scale(i, p, n):
            need(dve, self.power, i + 1)
            need(dve, self.saved[p], n * 16)
            dve.tensor_tensor(self.y[:, p], self.a[:, p], self.wide(4, p), ALU.mult).then_inc(self.scaled, 1)

        return [(9, scale), (7, gain)]

    def vector_between(self, dve):
        small = self.small

        def spread(i, p, n):
            need(dve, self.squared, i + 1)
            dve.tensor_reduce(small[:, p, 2], self.sq[:, p], AX, ALU.add).then_inc(self.sum2, 1)
            need(dve, self.sum2, i + 1)
            dve.tensor_scalar(small[:, p, 3], small[:, p, 2], 1.0 / D, 1.0e-5, ALU.mult, ALU.add
                              ).then_inc(self.spread, 1)

        return [(8, spread)]

    def scalar_first(self, act):
        def square(i, p, n):
            need(act, self.centred, i + 1)
            need(act, self.sum2, i - 1)
            act.activation(self.sq[:, p], self.a[:, p], ACT.Square).then_inc(self.squared, 1)

        return [(8, square)]


def gru_phase(nc, g, name, state, normed, logits, norm_of=None):
    with phase(nc, name) as ph:
        mh = g.work[:, 0:4 * J * D].rearrange("p (s j f) -> p s j f", s=2, j=J)
        hx = g.work[:, 4 * J * D:6 * J * D].rearrange("p (s j f) -> p s j f", s=2, j=J)
        gru = Gru(nc, g, ph, state, normed, 0, True, logits, mh, hx)
        norm = None
        if norm_of is not None:
            free = [flat[:, 0:2 * J * D].rearrange("p (s j f) -> p s j f", s=2, j=J) for flat in
                    (g.work[:, 6 * J * D:8 * J * D], g.l_dst[:].rearrange("p h j -> p (h j)"),
                     g.l_edge[:].rearrange("p h j -> p (h j)"))]
            norm = FirstNorm(g, ph, gru, *norm_of, free)
        with nc.Block() as block:
            @block.sync
            def _(sp):
                interleaved(sp, *gru.sync(sp), *(norm.sync(sp) if norm else ()))
                gru.sync_end(sp)
                if norm:
                    norm.sync_end(sp)

            @block.gpsimd
            def _(pool):
                if norm:
                    gru.between = norm.pool_between(pool)
                interleaved(pool, *gru.pool(pool), *(norm.pool(pool) if norm else ()))

            @block.vector
            def _(dve):
                if norm:
                    gru.between_dve = norm.vector_between(dve)
                interleaved(dve, *gru.vector(dve), *(norm.vector(dve) if norm else ()))

            @block.scalar
            def _(act):
                interleaved(act, *(norm.scalar_first(act) if norm else ()), *gru.scalar(act))

            @block.tensor
            def _(pe):
                interleaved(pe, *gru.tensor(pe))


class Norm:

    def __init__(self, nc, g, ph, x, xc, first, out, again, bufs):
        self.g, self.x, self.xc, self.first, self.out, self.again = g, x, xc, first, out, again
        sem = ph.sem
        self.gained, self.shifted, self.added, self.sum1, self.mean, self.centred = (
            sem(n) for n in ("n_gained", "n_shifted", "n_added", "n_sum1", "n_mean", "n_centred"))
        self.squared, self.sum2, self.spread, self.power, self.scaled = (
            sem(n) for n in ("n_squared", "n_sum2", "n_spread", "n_power", "n_scaled"))
        self.sum1b, self.meanb, self.centredb, self.squaredb, self.sum2b, self.spreadb, self.powerb, self.scaledb = (
            sem(n) for n in ("n_sum1b", "n_meanb", "n_centredb", "n_squaredb", "n_sum2b", "n_spreadb", "n_powerb",
                             "n_scaledb"))
        self.rooted, self.rootedb = sem("n_rooted"), sem("n_rootedb")
        self.loaded, self.saved, self.savedb = ([sem(f"{n}{p}") for p in range(2)]
                                                for n in ("n_loaded", "n_saved", "n_savedb"))
        shape = [P, 2, J, D]
        self.a, self.b, self.c, self.sq, self.y = (bufs.pop() if bufs else ph.sb(f"n_{k}", shape) for k in "abcsy")
        if again is not None:
            self.c2, self.sq2, self.y2 = (bufs.pop() if bufs else ph.sb(f"n_{k}2", shape) for k in "csy")
        self.small, self.small2 = ph.sb("n_small", [P, 2, 5, J]), ph.sb("n_small2", [P, 2, 5, J])

    def wide(self, small, k, p):
        return small[:, p, k].unsqueeze(2).to_broadcast([P, J, D])

    def sync(self, sp):
        def load(i, p, n):
            need(sp, self.centred, i - 1)
            sp.dma_start(self.a[:, p], rows(self.x, i)).then_inc(self.loaded[p], 16)
            sp.dma_start(self.b[:, p], rows(self.xc, i, self.first)).then_inc(self.loaded[p], 16)

        def store(i, p, n):
            need(sp, self.scaled, i + 1)
            sp.dma_start(rows(self.out, i, self.first), self.y[:, p]).then_inc(self.saved[p], 16)

        def store_b(i, p, n):
            need(sp, self.scaledb, i + 1)
            sp.dma_start(rows(self.again, i), self.y2[:, p]).then_inc(self.savedb[p], 16)

        return listed((0, load), (5, store), (8, store_b if self.again is not None else None))

    def sync_end(self, sp):
        for saved in [self.saved] + ([self.savedb] if self.again is not None else []):
            sp.wait_ge(saved[0], 16 * (NB - NB // 2))
            sp.wait_ge(saved[1], 16 * (NB // 2))

    def pool(self, pool):
        g = self.g

        def gain(i, p, n):
            need(pool, self.loaded[p], n * 32 + 32)
            b = self.b[:, p]
            pool.tensor_tensor(b, b, g.gamma[:].unsqueeze(1).to_broadcast([P, J, D]), ALU.mult).then_inc(self.gained, 1)
            need(pool, self.gained, i + 1)
            pool.tensor_tensor(b, b, g.beta[:].unsqueeze(1).to_broadcast([P, J, D]), ALU.add).then_inc(self.shifted, 1)

        def centre(i, p, n):
            need(pool, self.mean, i + 1)
            need(pool, self.scaled, i - 1)
            pool.tensor_tensor(self.c[:, p], self.a[:, p], self.wide(self.small, 1, p), ALU.subtract
                               ).then_inc(self.centred, 1)

        def scale(i, p, n):
            need(pool, self.power, i + 1)
            need(pool, self.saved[p], n * 16)
            if self.again is not None:
                need(pool, self.centredb, i - 1)
            pool.tensor_tensor(self.y[:, p], self.c[:, p], self.wide(self.small, 4, p), ALU.mult).then_inc(self.scaled, 1)

        def centre_b(i, p, n):
            need(pool, self.meanb, i + 1)
            need(pool, self.scaledb, i - 1)
            pool.tensor_tensor(self.c2[:, p], self.y[:, p], self.wide(self.small2, 1, p), ALU.subtract
                               ).then_inc(self.centredb, 1)

        def scale_b(i, p, n):
            need(pool, self.powerb, i + 1)
            need(pool, self.savedb[p], n * 16)
            pool.tensor_tensor(self.y2[:, p], self.c2[:, p], self.wide(self.small2, 4, p), ALU.mult
                               ).then_inc(self.scaledb, 1)

        more = ((7, scale_b), (5, centre_b)) if self.again is not None else ()
        return listed((1, gain), (4, scale), (2, centre), *more)

    def vector(self, dve):
        def reduce(small, k, source, sem, i, p):
            dve.tensor_reduce(small[:, p, k], source[:, p], AX, ALU.add).then_inc(sem, 1)
            need(dve, sem, i + 1)

        def add(i, p, n):
            need(dve, self.shifted, i + 1)
            dve.tensor_tensor(self.a[:, p], self.a[:, p], self.b[:, p], ALU.add).then_inc(self.added, 1)
            need(dve, self.added, i + 1)
            reduce(self.small, 0, self.a, self.sum1, i, p)
            dve.tensor_scalar(self.small[:, p, 1], self.small[:, p, 0], 1.0 / D, None, ALU.mult).then_inc(self.mean, 1)

        def spread(i, p, n):
            need(dve, self.squared, i + 1)
            reduce(self.small, 2, self.sq, self.sum2, i, p)
            dve.tensor_scalar(self.small[:, p, 3], self.small[:, p, 2], 1.0 / D, 1.0e-5, ALU.mult, ALU.add
                              ).then_inc(self.spread, 1)

        def mean_b(i, p, n):
            need(dve, self.scaled, i + 1)
            reduce(self.small2, 0, self.y, self.sum1b, i, p)
            dve.tensor_scalar(self.small2[:, p, 1], self.small2[:, p, 0], 1.0 / D, None, ALU.mult).then_inc(self.meanb, 1)

        def spread_b(i, p, n):
            need(dve, self.squaredb, i + 1)
            reduce(self.small2, 2, self.sq2, self.sum2b, i, p)
            dve.tensor_scalar(self.small2[:, p, 3], self.small2[:, p, 2], 1.0 / D, 0.25e-5, ALU.mult, ALU.add
                              ).then_inc(self.spreadb, 1)

        more = ((6, spread_b), (5, mean_b)) if self.again is not None else ()
        return listed(*more, (3, spread), (1, add))

    def vector_first(self, dve):
        def turn_over(i, p, n):
            need(dve, self.rooted, i + 1)
            dve.reciprocal(self.small[:, p, 4], self.small[:, p, 4]).then_inc(self.power, 1)

        def turn_over_b(i, p, n):
            need(dve, self.rootedb, i + 1)
            dve.reciprocal(self.small2[:, p, 4], self.small2[:, p, 4]).then_inc(self.powerb, 1)

        return listed((4, turn_over), (7, turn_over_b if self.again is not None else None))

    def scalar(self, act):
        def square(i, p, n):
            need(act, self.centred, i + 1)
            need(act, self.sum2, i - 1)
            act.activation(self.sq[:, p], self.c[:, p], ACT.Square).then_inc(self.squared, 1)

        def square_b(i, p, n):
            need(act, self.centredb, i + 1)
            need(act, self.sum2b, i - 1)
            act.activation(self.sq2[:, p], self.c2[:, p], ACT.Square).then_inc(self.squaredb, 1)

        return listed((6, square_b if self.again is not None else None), (3, square))

    def scalar_first(self, act):
        def root(i, p, n):
            need(act, self.spread, i + 1)
            act.activation(self.small[:, p, 4], self.small[:, p, 3], ACT.Sqrt).then_inc(self.rooted, 1)

        def root_b(i, p, n):
            need(act, self.spreadb, i + 1)
            act.activation(self.small2[:, p, 4], self.small2[:, p, 3], ACT.Sqrt).then_inc(self.rootedb, 1)

        return listed((4, root), (7, root_b if self.again is not None else None))


def final_phase(nc, g, x1, node_out):
    with phase(nc, "final") as ph:
        parted, whole, shared, kept, added, sum1, centred, squared, sum2, spread, rooted, power, scaled, copied = (
            ph.sem(n) for n in ("parted", "whole", "shared", "kept", "added", "sum1", "centred", "squared",
                                "sum2", "spread", "rooted", "power", "scaled", "copied"))
        loaded = [ph.sem(f"loaded{p}") for p in range(2)]
        shape = [P, 2, J, D]
        a, b, c, sq, y = (ph.sb(n, shape) for n in ("a", "b", "c", "sq", "y"))
        small = ph.sb("small", [P, 2, 5, J])
        idx = ph.sb("idx", [P, 2, J], I32)

        def wide(k, p):
            return small[:, p, k].unsqueeze(2).to_broadcast([P, J, D])

        with nc.Block() as block:
            @block.sync
            def _(sp):
                def load(i, p, n):
                    need(sp, centred, i - 1)
                    sp.dma_start(a[:, p], rows(x1, i)).then_inc(loaded[p], 16)

                interleaved(sp, (0, load))

            @block.gpsimd
            def _(pool):
                def scatter(i, p, n):
                    need(pool, g.scattered[p], n * P)
                    pool.tensor_copy(idx[:, p, :], cols(g.out_idx, i)).then_inc(copied, 1)
                    need(pool, copied, i + 1)
                    need(pool, scaled, i + 1)
                    for u in range(J):
                        pool.indirect_dma_start(node_out, bass.IndirectOffsetOnAxis(ap=idx[:, p, u:u + 1], axis=0),
                                                y[:, p, u, :], None, bounds_check=N - 1, oob_is_err=False
                                                ).then_inc(g.scattered[p], 16)

                interleaved(pool, (0, scatter))
                pool.wait_ge(g.scattered[0], P * (NB - NB // 2))
                pool.wait_ge(g.scattered[1], P * (NB // 2))

            @block.vector
            def _(dve):
                def update(i, p, n):
                    dve.tensor_tensor(b[:, p], cols(g.head, i).unsqueeze(2).to_broadcast([P, J, D]),
                                      g.carry[:].unsqueeze(1).to_broadcast([P, J, D]), ALU.mult).then_inc(parted, 1)
                    need(dve, parted, i + 1)
                    dve.tensor_tensor(b[:, p], g.big[:, bass.ds(i * (J * D), J * D)].rearrange("p (j f) -> p j f", f=D),
                                      b[:, p], ALU.add).then_inc(whole, 1)
                    need(dve, whole, i + 1)
                    dve.tensor_tensor(b[:, p], b[:, p], cols(g.share, i).unsqueeze(2).to_broadcast([P, J, D]),
                                      ALU.mult).then_inc(shared, 1)
                    need(dve, shared, i + 1)
                    need(dve, loaded[p], n * 16 + 16)
                    dve.scalar_tensor_tensor(b[:, p], a[:, p], 0.2, b[:, p], ALU.mult, ALU.add).then_inc(kept, 1)
                    need(dve, kept, i + 1)
                    dve.scalar_tensor_tensor(a[:, p], b[:, p], 0.0, a[:, p], ALU.max, ALU.add).then_inc(added, 1)
                    need(dve, added, i + 1)
                    dve.tensor_reduce(small[:, p, 0], a[:, p], AX, ALU.add).then_inc(sum1, 1)
                    need(dve, sum1, i + 1)
                    dve.scalar_tensor_tensor(c[:, p], wide(0, p), -1.0 / D, a[:, p], ALU.mult, ALU.add
                                             ).then_inc(centred, 1)

                def spread_of(i, p, n):
                    need(dve, squared, i + 1)
                    dve.tensor_reduce(small[:, p, 2], sq[:, p], AX, ALU.add).then_inc(sum2, 1)
                    need(dve, sum2, i + 1)
                    dve.tensor_scalar(small[:, p, 3], small[:, p, 2], 1.0 / D, 1.0e-5, ALU.mult, ALU.add
                                      ).then_inc(spread, 1)

                def scale(i, p, n):
                    need(dve, rooted, i + 1)
                    dve.reciprocal(small[:, p, 4], small[:, p, 4]).then_inc(power, 1)
                    need(dve, power, i + 1)
                    need(dve, g.scattered[p], n * P)
                    dve.tensor_tensor(y[:, p], c[:, p], wide(4, p), ALU.mult).then_inc(scaled, 1)

                interleaved(dve, (2, scale), (1, spread_of), (0, update))

            @block.scalar
            def _(act):
                def square(i, p, n):
                    need(act, centred, i + 1)
                    need(act, sum2, i - 1)
                    act.activation(sq[:, p], c[:, p], ACT.Square).then_inc(squared, 1)

                def root(i, p, n):
                    need(act, spread, i + 1)
                    act.activation(small[:, p, 4], small[:, p, 3], ACT.Sqrt).then_inc(rooted, 1)

                interleaved(act, (1, root), (0, square))


def relation_phase(nc, g, dram, table):
    pairs = RELS // 2
    with phase(nc, "relation") as ph:
        copied, spreaded, turned, evacuated = (ph.sem(n) for n in ("idx_copied", "spread", "turned", "evacuated"))
        multiplied, out_done = ph.sem("multiplied"), ph.sem("out")
        stage_idx = ph.sb("stage_idx", [P, 2, J], I32)
        stage = ph.sb("stage", [P, 2, J, D])
        xm = ph.sb("xm", [P, 2, 2, RELS, D])
        xmt = ph.sb("xmt", [P, 2, 2, pairs, P])
        wr = ph.sb("wr", [P, pairs, D])
        mask = ph.sb("mask", [P, TILES, RELS])
        relf = ph.sb("relf", [P, TILES])
        wr_loaded, rel_done = ph.sem("wr_loaded"), ph.sem("rel_done")
        ps_x, ps_r = ph.pb("ps_x", [P, 2, 2, pairs * P]), ph.pb("ps_r", [P, 2, J * D])
        done = list(g.gathered_count)
        g.gathered_count[0] += P * (NB - NB // 2)
        g.gathered_count[1] += P * (NB // 2)

        with nc.Block() as block:
            @block.gpsimd
            def _(pool):
                def gather(i, p, n):
                    need(pool, g.gathered[p], n * P + done[p])
                    pool.tensor_copy(stage_idx[:, p, :], cols(g.src_slot, i)).then_inc(copied, 1)
                    need(pool, copied, i + 1)
                    need(pool, spreaded, (i - 1) * Q)
                    for u in range(J):
                        pool.indirect_dma_start(stage[:, p, u, :], None, table,
                                                bass.IndirectOffsetOnAxis(ap=stage_idx[:, p, u:u + 1], axis=0)
                                                ).then_inc(g.gathered[p], 16)

                interleaved(pool, (0, gather))

            @block.sync
            def _(sp):
                sp.dma_start(wr[:], dram["wr"]).then_inc(wr_loaded, 16)

            @block.tensor
            def _(pe):
                pe.wait_ge(wr_loaded, 16)

                def turn(i, t):
                    need(pe, spreaded, i * Q + (t + 1))
                    need(pe, evacuated, i * Q + (t - 1))
                    for s in range(2):
                        for q in range(pairs):
                            ins = pe.transpose(ps_x[:, t % 2, s, q * P:(q + 1) * P],
                                               xm[:, t % 2, s, 2 * q:2 * q + 2, :].rearrange("p r d -> p (r d)"),
                                               g.ident[:])
                    ins.then_inc(turned, 1)

                def multiply(i, p, t):
                    need(pe, evacuated, i * Q + (t + 1))
                    for s in range(2):
                        for q in range(pairs):
                            ins = pe.matmul(ps_r[:, p, (2 * t + s) * D:(2 * t + s + 1) * D], xmt[:, t % 2, s, q, :],
                                            wr[:, q, :], start=(q == 0), stop=(q == pairs - 1))
                    ins.then_inc(multiplied, 1)

                def turn_first(i, p, n):
                    turn(i, 0)

                def multiply_last(i, p, n):
                    multiply(i, p, Q - 1)

                def others(i, p, n):
                    need(pe, out_done, i - 1)
                    for t in range(1, Q):
                        turn(i, t)
                        multiply(i, p, t - 1)

                interleaved(pe, (0, turn_first), (1, multiply_last), (0, others))

            @block.scalar
            def _(act):
                def evacuate(i, p, n):
                    for t in range(Q):
                        need(act, turned, i * Q + (t + 1))
                        need(act, multiplied, i * Q + (t - 1))
                        act.activation(xmt[:, t % 2].rearrange("p s q e -> p (s q e)"),
                                       ps_x[:, t % 2].rearrange("p s e -> p (s e)"), ACT.Copy).then_inc(evacuated, 1)

                interleaved(act, (0, evacuate))

            @block.vector
            def _(dve):
                def spread(i, p, n):
                    need(dve, g.gathered[p], n * P + (P + done[p]))
                    for t in range(Q):
                        need(dve, turned, i * Q + (t - 1))
                        here = mask[:, bass.ds(i * J + 2 * t, 2), :]
                        dve.tensor_tensor(xm[:, t % 2],
                                          stage[:, p, 2 * t:2 * t + 2, :].unsqueeze(2).to_broadcast([P, 2, RELS, D]),
                                          here.unsqueeze(3).to_broadcast([P, 2, RELS, D]), ALU.mult
                                          ).then_inc(spreaded, 1)

                def out(i, p, n):
                    need(dve, multiplied, i * Q + Q)
                    dve.tensor_copy(g.big[:, bass.ds(i * (J * D), J * D)], ps_r[:, p, :]).then_inc(out_done, 1)

                dve.tensor_copy(relf[:], g.rel[:]).then_inc(rel_done, 1)
                dve.wait_ge(rel_done, 1)
                for r in range(RELS):
                    dve.tensor_scalar(mask[:, :, r], relf[:], float(r), None, ALU.is_equal).then_inc(rel_done, 1)
                dve.wait_ge(rel_done, 1 + RELS)
                interleaved(dve, (0, spread), (1, out))


class EdgeLogits(Beside):

    def __init__(self, nc, g, ph, edge):
        self.g, self.edge = g, edge
        self.loaded = [ph.sem("e_loaded0"), ph.sem("e_loaded1")]
        self.turned, self.evacuated, self.projected, self.out_done = (
            ph.sem(n) for n in ("e_turned", "e_evacuated", "e_projected", "e_out"))
        self.ea, self.et = ph.sb("ea", [P, 2, J, K]), ph.sb("et", [P, 2, P])
        self.ps_t, self.ps_l = ph.pb("ps_et", [P, 2, 512]), ph.pb("ps_el", [P, 2, 512])

    def sync(self, sp):
        def load(i, p, n):
            need(sp, self.turned, i - 1)
            sp.dma_start(self.ea[:, p, :, :], rows(self.edge, i)).then_inc(self.loaded[p], 16)

        return [(0, load)]

    def tensor(self, pe):
        def turn(i, p, n):
            need(pe, self.loaded[p], n * 16 + 16)
            need(pe, self.evacuated, i - 1)
            pe.transpose(self.ps_t[:, p, 0:P], self.ea[:, p, :, :].rearrange("p t k -> p (t k)"), self.g.ident[:]
                         ).then_inc(self.turned, 1)

        def project(i, p, n):
            need(pe, self.evacuated, i + 1)
            need(pe, self.out_done, i - 1)
            pe.matmul(self.ps_l[:, p, 0:J * HEADS], self.et[:, p, :], self.g.w_edge[:].rearrange("p t h -> p (t h)"),
                      start=True, stop=True).then_inc(self.projected, 1)

        return [(1, project), (0, turn)]

    def scalar(self, act):
        def evacuate(i, p, n):
            need(act, self.turned, i + 1)
            need(act, self.projected, i - 1)
            act.activation(self.et[:, p, :], self.ps_t[:, p, 0:P], ACT.Copy).then_inc(self.evacuated, 1)

        return [(0, evacuate)]

    def vector(self, dve):
        def out(i, p, n):
            need(dve, self.projected, i + 1)
            dve.tensor_copy(hcols(self.g.l_edge, i), self.ps_l[:, p, 0:J * HEADS].rearrange("p (t h) -> p t h", h=HEADS)
                            ).then_inc(self.out_done, 1)

        return [(2, out)]


class Position(Beside):

    def __init__(self, nc, g, ph):
        self.g = g
        self.s_chain, self.s_iota, self.s_hi, self.s_lo, self.s_count = (
            ph.sem(n) for n in ("p_chain", "p_iota", "p_hi", "p_lo", "p_count"))
        self.iota_i, self.iota_f = ph.sb("iota_i", [P, TILES], I32), ph.sb("iota_f", [P, TILES])
        self.node_i, self.hi_i = ph.sb("node_i", [P, TILES], I32), ph.sb("hi_i", [P, TILES], I32)
        self.hi, self.lo, self.fix = (ph.sb(n, [P, TILES]) for n in ("hi", "lo", "fix"))
        self.hot_hi, self.hot_lo = ph.sb("hot_hi", [P, 2, J, P], F16), ph.sb("hot_lo", [P, 2, J, TILES], F16)
        self.ps = ph.pb("ps_count", [P, 512])
        self.links = 0

    def link(self, dve, ins):
        self.links += 1
        ins.then_inc(self.s_chain, 1)
        dve.wait_ge(self.s_chain, self.links)

    def pool_start(self, pool):
        pool.iota(self.iota_i[:], [[1, TILES]], base=0, channel_multiplier=0).then_inc(self.s_iota, 1)
        pool.iota(self.node_i[:], [[1, TILES]], base=SLOTS, channel_multiplier=TILES).then_inc(self.s_iota, 1)

    def vector_start(self, dve):
        g, hi, lo, fix, hi_i = self.g, self.hi, self.lo, self.fix, self.hi_i
        dve.wait_ge(self.s_iota, 2)
        self.link(dve, dve.tensor_copy(self.iota_f[:], self.iota_i[:]))
        self.link(dve, dve.tensor_copy(g.own_row[:], self.node_i[:]))
        self.link(dve, dve.tensor_copy(lo[:], g.dst_idx[:]))
        self.link(dve, dve.tensor_scalar(hi[:], lo[:], 1.0 / TILES, None, ALU.mult))
        self.link(dve, dve.tensor_copy(hi_i[:], hi[:]))
        self.link(dve, dve.tensor_copy(hi[:], hi_i[:]))
        self.link(dve, dve.scalar_tensor_tensor(lo[:], hi[:], -float(TILES), lo[:], ALU.mult, ALU.add))
        self.link(dve, dve.tensor_scalar(fix[:], lo[:], 0.0, None, ALU.is_lt))
        self.link(dve, dve.tensor_tensor(hi[:], hi[:], fix[:], ALU.subtract))
        self.link(dve, dve.scalar_tensor_tensor(lo[:], fix[:], float(TILES), lo[:], ALU.mult, ALU.add))
        self.link(dve, dve.tensor_scalar(fix[:], lo[:], float(TILES), None, ALU.is_ge))
        self.link(dve, dve.tensor_tensor(hi[:], hi[:], fix[:], ALU.add))
        self.link(dve, dve.scalar_tensor_tensor(lo[:], fix[:], -float(TILES), lo[:], ALU.mult, ALU.add))

    def vector(self, dve):
        def hot(i, p, n):
            need(dve, self.s_count, i - 1)
            dve.tensor_tensor(self.hot_hi[:, p], self.iota_f[:, 0:P].unsqueeze(1).to_broadcast([P, J, P]),
                              cols(self.hi, i).unsqueeze(2).to_broadcast([P, J, P]), ALU.is_equal).then_inc(self.s_hi, 1)
            dve.tensor_tensor(self.hot_lo[:, p], self.iota_f[:].unsqueeze(1).to_broadcast([P, J, TILES]),
                              cols(self.lo, i).unsqueeze(2).to_broadcast([P, J, TILES]), ALU.is_equal
                              ).then_inc(self.s_lo, 1)

        return [(0, hot)]

    def vector_end(self, dve):
        dve.wait_ge(self.s_count, NB)
        self.link(dve, dve.tensor_copy(self.g.count[:], self.ps[:, 0:TILES]))

    def tensor(self, pe):
        def count(i, p, n):
            need(pe, self.s_hi, i + 1)
            need(pe, self.s_lo, i + 1)
            for t in range(J):
                edge = isinstance(i, int)
                ins = pe.matmul(self.ps[:, 0:TILES], self.hot_hi[:, p, t, :], self.hot_lo[:, p, t, :],
                                start=(edge and i == 0 and t == 0), stop=(edge and i == NB - 1 and t == J - 1),
                                skip_group_check=True)
            ins.then_inc(self.s_count, 1)

        return [(0, count)]


def plain_cumulation_phase(nc, g):
    with phase(nc, "cumulate") as ph:
        chain, asked, got, asked2, got2 = (ph.sem(n) for n in ("chain", "asked", "got", "asked2", "got2"))
        ones = ph.sb("ones", [P, TILES])
        cum, has = ph.sb("cum", [P, TILES]), ph.sb("has", [P, TILES])
        last = ph.sb("last", [P, 1])
        carried, carry = ph.sb("carried", [1, P + 1]), ph.sb("carry", [P, 1])
        one1 = ph.sb("one1", [1, 1])
        ps = ph.pb("ps", [P, 2, 512])
        with nc.Block() as block:
            @block.vector
            def _(dve):
                n = [0]

                def link(ins):
                    n[0] += 1
                    ins.then_inc(chain, 1)
                    dve.wait_ge(chain, n[0])

                link(dve.memset(ones[:], 1.0))
                link(dve.memset(one1[:], 1.0))
                link(dve.memset(carried[:], 0.0))
                link(dve.tensor_tensor_scan(cum[:], ones[:], g.count[:], 0.0, ALU.mult, ALU.add))
                dve.tensor_copy(last[:], cum[:, TILES - 1:TILES]).then_inc(asked, 1)
                dve.wait_ge(got, 1)
                dve.tensor_tensor_scan(carried[:, 1:P + 1], ones[0:1, 0:P], ps[0:1, 0, 0:P], 0.0, ALU.mult, ALU.add
                                       ).then_inc(asked2, 1)
                dve.wait_ge(got2, 1)
                link(dve.tensor_copy(carry[:], ps[:, 1, 0:1]))
                link(dve.tensor_scalar(cum[:], cum[:], carry[:, 0:1], -1.0, ALU.add, ALU.add))
                link(dve.tensor_scalar(has[:], g.count[:], 0.0, None, ALU.is_gt))
                link(dve.tensor_tensor(cum[:], cum[:], g.own_row[:], ALU.subtract))
                link(dve.tensor_tensor(cum[:], cum[:], has[:], ALU.mult))
                link(dve.tensor_tensor(g.own_row[:], g.own_row[:], cum[:], ALU.add))

            @block.tensor
            def _(pe):
                pe.wait_ge(asked, 1)
                pe.transpose(ps[0:1, 0, 0:P], last[:], g.ident[:]).then_inc(got, 1)
                pe.wait_ge(asked2, 1)
                pe.wait_ge(chain, 2)
                pe.matmul(ps[:, 1, 0:1], carried[:, 0:P], one1[:], start=True, stop=True).then_inc(got2, 1)


def table_phase(nc, g, x, table):
    with phase(nc, "table") as ph:
        loaded, saved = ([ph.sem(f"{n}{p}") for p in range(2)] for n in ("loaded", "saved"))
        filled, numbered = ph.sem("filled"), ph.sem("numbered")
        a, w = ph.sb("a", [P, 2, J, D]), ph.sb("w", [P, 2, J, D + 1])
        with nc.Block() as block:
            @block.sync
            def _(sp):
                def load(i, p, n):
                    need(sp, filled, i - 1)
                    sp.dma_start(a[:, p], rows(x, i)).then_inc(loaded[p], 16)

                pipelined(sp, load)

            @block.scalar
            def _(act):
                def store(i, p, n):
                    need(act, filled, i + 1)
                    need(act, numbered, i + 1)
                    act.dma_start(rows(table, i), w[:, p]).then_inc(saved[p], 16)

                pipelined(act, store)
                act.wait_ge(saved[0], 16 * (NB - NB // 2))
                act.wait_ge(saved[1], 16 * (NB // 2))

            @block.vector
            def _(dve):
                def fill(i, p, n):
                    need(dve, loaded[p], n * 16 + 16)
                    need(dve, saved[p], n * 16)
                    dve.tensor_copy(w[:, p, :, 0:D], a[:, p]).then_inc(filled, 1)
                    dve.tensor_copy(w[:, p, :, D], cols(g.own_row, i)).then_inc(numbered, 1)

                pipelined(dve, fill)


def weights_phase(nc, g):
    with phase(nc, "weights") as ph:
        chain, multiplied = ph.sem("chain"), ph.sem("multiplied")
        beta = ph.sb("beta", [P, P])
        both = ph.sb("both", [P, HEADS])
        lift = ph.sb("lift", [P, HEADS])
        ps = ph.pb("ps", [P, 2, 512])
        with nc.Block() as block:
            @block.vector
            def _(dve):
                n = [0]

                def link(ins):
                    n[0] += 1
                    ins.then_inc(chain, 1)
                    dve.wait_ge(chain, n[0])

                link(dve.tensor_copy(beta[:], g.beta_col[:].to_broadcast([P, P])))
                link(dve.tensor_tensor(both[:], g.w_src[:, 0, :], g.w_dst[:, 0, :], ALU.add))
                dve.wait_ge(multiplied, 1)
                link(dve.tensor_copy(g.node_bias[:], ps[:, 0, 0:2]))
                link(dve.tensor_copy(lift[:], ps[:, 1, 0:HEADS]))
                link(dve.tensor_tensor(g.l_edge[:], g.l_edge[:], lift[:].unsqueeze(2).to_broadcast([P, HEADS, TILES]),
                                       ALU.add))
                for w in (g.w_src, g.w_dst, g.wn):
                    link(dve.tensor_scalar(w[:], w[:], g.gamma_col[:, 0:1], None, ALU.mult))

            @block.tensor
            def _(pe):
                pe.wait_ge(chain, 2)
                for c in range(2):
                    pe.matmul(ps[:, 0, c:c + 1], g.wn[:, 0, c * P:(c + 1) * P], beta[:, 0:1], start=True, stop=True)
                pe.matmul(ps[:, 1, 0:HEADS], beta[:], both[:], start=True, stop=True).then_inc(multiplied, 1)


def build(nc, dram, out, trace=None):
    with ExitStack() as ctx:
        def sb(name, shape, dtype=F32):
            return ctx.enter_context(nc.sbuf_tensor(name, shape, dtype))

        for k, eng in enumerate((nc.sync, nc.scalar, nc.tensor, nc.vector, nc.gpsimd)):
            TO_GATE[eng.engine] = ctx.enter_context(nc.semaphore(f"passed_{k}"))
        g = Shared()
        g.big = sb("big", [P, TILES * D])
        g.src = sb("src", [P, TILES], I32)
        g.src_slot = sb("src_slot", [P, TILES], I32)
        g.dst_idx = sb("dst_idx", [P, TILES], I32)
        g.out_idx = sb("out_idx", [P, TILES], I32)
        g.goes_on = sb("goes_on", [P, TILES])
        g.not_end = sb("not_end", [P, TILES])
        g.shut = sb("shut", [P, TILES])
        g.is_end = sb("is_end", [P, TILES])
        g.head = sb("head", [P, TILES])
        g.share = sb("share", [P, TILES])
        g.rel = sb("rel", [P, TILES], I32)
        g.l_edge = sb("l_edge", [P, HEADS, TILES])
        g.l_dst = sb("l_dst", [P, HEADS, TILES])
        g.work = sb("work", [P, 3 * HEADS * TILES])
        g.wn = sb("wn", [P, 2, HC])
        g.we = sb("we", [P, 2, HC])
        g.ws = sb("ws", [P, 2, D])
        g.wg = sb("wg", [P, 4 * D])
        g.bias3 = sb("bias3", [3, 4 * D], BF16)
        g.ones3 = sb("ones3", [3, P], BF16)
        g.m_empty = sb("m_empty", [P, D])
        g.node_bias = sb("node_bias", [P, 2])
        g.gamma_col = sb("gamma_col", [P, 1])
        g.beta_col = sb("beta_col", [P, 1])
        g.ident = sb("ident", [P, P])
        g.b = sb("b", [P, D])
        g.gamma = sb("gamma", [P, D])
        g.beta = sb("beta", [P, D])
        g.w_dst = sb("w_dst", [P, 2, HEADS])
        g.w_src = sb("w_src", [P, 2, HEADS])
        g.w_edge = sb("w_edge", [P, J, HEADS])
        g.half_power = sb("half_power", [P, J])
        g.carry = sb("carry", [P, D])
        g.whole64 = sb("whole64", [P, 3, D])
        g.whole_t = sb("whole_t", [D, 3, P])
        g.l_src, g.tmp, g.alpha = (g.work[:, k * HEADS * TILES:(k + 1) * HEADS * TILES].rearrange("p (h j) -> p h j", h=HEADS)
                                   for k in range(3))
        g.count, g.own_row = g.big[:, 0:TILES], g.big[:, TILES:2 * TILES]
        g.gathered = [ctx.enter_context(nc.semaphore(f"gathered{p}")) for p in range(2)]
        g.scattered = [ctx.enter_context(nc.semaphore(f"scattered{p}")) for p in range(2)]
        g.gathered_count = [0, 0]

        def scratch(name, count, width=D):
            return nc.dram_tensor(name, (count, width), F32, kind="ExternalOutput" if trace else "Internal").ap()

        x_slot = scratch("x_slot", SLOTS)
        table0 = scratch("table0", SLOTS, D + 1)
        h_slot = [scratch(f"h_slot{t}", SLOTS) for t in range(2)]
        h_node = [scratch(f"h_node{t}", SLOTS) for t in range(2)]
        tables = [scratch(f"normed{t}", 2 * SLOTS) for t in range(STEPS)]
        x1 = scratch("x1", 2 * SLOTS)

        setup_phase(nc, g, dram)
        gather_phase(nc, g, "dst", dram["x"][:, :], D, g.dst_idx, g.w_dst, g.l_dst, save=x_slot,
                     beside=(Position, lambda nc, g, ph: EdgeLogits(nc, g, ph, dram["edge"])))
        plain_cumulation_phase(nc, g)
        table_phase(nc, g, dram["x"], table0)
        for t in range(STEPS):
            last = t == STEPS - 1
            nodes = ((h_node[(t - 1) % 2] if t else dram["x"], None if last else h_node[t % 2]), tables[t])
            if t == 0:
                gather_phase(nc, g, "src0", table0[:, :], D + 1, g.src, g.w_src, g.l_src, keep=g.big, pos=g.src_slot,
                             nodes=nodes)
            else:
                gather_phase(nc, g, f"src{t}", tables[t - 1][:, :], D, g.src_slot, g.w_src, g.l_src, keep=g.big,
                             nodes=nodes)
            softmax_phase(nc, g, f"softmax{t}")
            message_phase(nc, g, f"message{t}", dram,
                          (dram["x"], tables[t], SLOTS, x1, out) if last else None)
            if t == 0:
                weights_phase(nc, g)
            segment_sum_phase(nc, g, f"sum{t}")
            gru_phase(nc, g, f"gru{t}", (h_slot[(t - 1) % 2] if t else x_slot, None if last else h_slot[t % 2]),
                      None if last else tables[t], None if last else g.l_dst, (x_slot, x1) if last else None)
        relation_phase(nc, g, dram, x1[:, :])
        degree_phase(nc, g)
        segment_sum_phase(nc, g, "sum_rel")
        final_phase(nc, g, x1, out[:, :])


def kernel(**inputs):
    import numpy as np
    import concourse.bacc as bacc
    from concourse import mybir as mb
    from concourse.bass_utils import run_bass_kernel_spmd as run

    a = {k: np.ascontiguousarray(v) for k, v in inputs.items()}
    pad = SLOTS - N

    def padded(v, fill=0):
        return np.concatenate([v, np.full((pad,) + v.shape[1:], fill, v.dtype)])

    def split(v):
        return np.ascontiguousarray(v.reshape(P, TILES))

    def on_all(v):
        return np.ascontiguousarray(np.broadcast_to(v.reshape(1, -1), (P, v.size)))

    f = np.float32
    dst = padded(a["dst"], N)
    edge = np.array([-1], dst.dtype)
    wn, we, wsum = a["L0_gnn_Wn"], a["L0_gnn_We"], a["L0_gnn_Ws"]
    wn_two = np.zeros((P, 2, HC), f)
    we_two = np.zeros((P, 2, HC), f)
    for s in range(2):
        wn_two[s * D:(s + 1) * D, s] = wn
        for h in range(HEADS):
            we_two[s * D + h * K:s * D + (h + 1) * K, s, h * D:(h + 1) * D] = we[:, h * D:(h + 1) * D]
    wih, whh = a["L0_gnn_Wih"].T, a["L0_gnn_Whh"].T
    wg = np.zeros((P, 4 * D), f)
    wg[0:D, 0:3 * D] = wih
    wg[D:, 0:2 * D] = whh[:, 0:2 * D]
    wg[D:, 3 * D:] = whh[:, 2 * D:]
    bg = np.zeros((2, 4 * D), f)
    bg[0, 0:3 * D] = a["L0_gnn_bih"]
    bg[1, 0:2 * D] = a["L0_gnn_bhh"][0:2 * D]
    bg[1, 3 * D:] = a["L0_gnn_bhh"][2 * D:]
    wr = np.ascontiguousarray(a["L1_gnn_weight_r"].reshape(RELS // 2, P, D).transpose(1, 0, 2))
    wa = a["L0_gnn_Wa"].reshape(HEADS, 3, D).transpose(1, 0, 2).reshape(-1)
    half, eighth = np.zeros((P, 2), f), np.zeros((P, J), f)
    half[np.arange(P), np.arange(P) // D] = 1
    eighth[np.arange(P), np.arange(P) // K] = 1
    gamma_col = np.concatenate([a["L0_gnn_gamma"]] * 2).reshape(P, 1)
    beta_col = np.concatenate([a["L0_gnn_beta"]] * 2).reshape(P, 1)
    arrays = dict(
        gamma_col=gamma_col, beta_col=beta_col,
        x=padded(a["x"]), edge=padded(a["edge_attr_16"]), src=split(padded(a["src"])),
        dst_cur=split(dst), dst_prev=split(np.concatenate([edge, dst[:-1]])), dst_next=split(np.concatenate([dst[1:], edge])),
        rel=split(padded(a["edge_type_8"])), wn_twice=np.concatenate([wn, wn]), we_eight=np.tile(we, (P // K, 1)),
        wa=on_all(wa).reshape(P, 3, HC), half=half, eighth=eighth, wn=wn_two, we=we_two,
        ws=np.ascontiguousarray(wsum.reshape(2, P, D).transpose(1, 0, 2)), wg=wg, bg=bg, wr=wr,
        ident=np.eye(P, dtype=f), b=on_all(a["L0_gnn_b"]), gamma=on_all(a["L0_gnn_gamma"]), beta=on_all(a["L0_gnn_beta"]))
    nc = bacc.Bacc("TRN2", target_bir_lowering=False, num_devices=1)
    dram = {n: nc.dram_tensor(f"in_{n}", v.shape, mb.dt.from_np(v.dtype), kind="ExternalInput").ap()
            for n, v in arrays.items()}
    out = nc.dram_tensor("result", (SLOTS, D), F32, kind="ExternalOutput").ap()
    build(nc, dram, out)
    r = run(nc, [{f"in_{n}": v for n, v in arrays.items()}], core_ids=[0])
    return r.results[0]["result"][0:N]
```
